# Optimizing a Trainium2 kernel written in Bass

```python
import numpy as np
import jax
import jax.numpy as jnp

def _softmax(x, axis=-1):
    return jax.nn.softmax(x, axis=axis)

def _gelu(x):
    return jax.nn.gelu(x, approximate=True)

def _silu(x):
    return jax.nn.silu(x)

def _sigmoid(x):
    return jax.nn.sigmoid(x)

def _layernorm(x, axis=-1, eps=1e-05):
    m = jnp.mean(x, axis=axis, keepdims=True)
    v = jnp.var(x, axis=axis, keepdims=True)
    return (x - m) / jnp.sqrt(v + eps)

def _scatter_add(tgt, idx, src, axis=0):
    return tgt.at[idx].add(src)

def _segment_sum(src, seg, n):
    return jax.ops.segment_sum(src, seg, n)
kernel_name = 'mk_xattn_ffn_d1_seqx_r4_eacb36'

def setup_inputs(seed: int=0):
    np.random.seed(seed)
    _w = jnp.asarray

    def _rec_inputs():
        import jax
        import jax.numpy as jnp
        _rk = jax.random.key(seed)
        x = 0.0003765 + 1 * jax.random.normal(jax.random.fold_in(_rk, 1), (4, 512, 256), jnp.float32)
        _lenS = 512 - jax.random.randint(jax.random.fold_in(_rk, 7), (4,), 0, max(1, 512 // 4) + 1, jnp.int32)
        _lenS2 = 64 - jax.random.randint(jax.random.fold_in(_rk, 8), (4,), 0, max(1, 64 // 4) + 1, jnp.int32)
        _ctx_1024P = jax.random.normal(jax.random.fold_in(_rk, 11), (4, 16, 256), jnp.float32)
        _ctx_1024c = jax.random.dirichlet(jax.random.fold_in(_rk, 511), 0.3 * jnp.ones((16,), jnp.float32), (4, 64))
        _ctx_1024t = jnp.einsum('bsk,bkd->bsd', _ctx_1024c, _ctx_1024P)
        _ctx_1024t = _ctx_1024t * jax.lax.rsqrt(jnp.mean(jnp.square(_ctx_1024t)) + 1e-12) * 0.953939
        ctx_1024 = -0.000292821 + 1.00034 * (_ctx_1024t + 0.3 * jax.random.normal(jax.random.fold_in(_rk, 611), (4, 64, 256), jnp.float32))
        return (x, ctx_1024)
    x, ctx_1024 = _rec_inputs()

    def _L0_xattn_setup():
        import jax, jax.numpy as jnp
        import numpy as np
        EMBED = 256
        HEADS = 16
        HEAD_DIM = EMBED // HEADS
        key = jax.random.key(seed)
        ks = jax.random.split(key, 8)
        B, S = (2, 512)
        value = jax.random.normal(ks[0], (B, S, EMBED), dtype=jnp.float32)
        key_t = jax.random.normal(ks[1], (B, S, EMBED), dtype=jnp.float32)
        query = jax.random.normal(ks[2], (B, S, EMBED), dtype=jnp.float32)
        scale = 1.0 / np.sqrt(EMBED)
        Wv = jax.random.normal(ks[3], (EMBED, EMBED), dtype=jnp.float32) * scale
        Wk = jax.random.normal(ks[4], (EMBED, EMBED), dtype=jnp.float32) * scale
        Wq = jax.random.normal(ks[5], (EMBED, EMBED), dtype=jnp.float32) * scale
        Wo = jax.random.normal(ks[6], (EMBED, EMBED), dtype=jnp.float32) * scale
        bo = jax.random.normal(ks[7], (EMBED,), dtype=jnp.float32) * 0.01
        return {'value': value, 'key': key_t, 'query': query, 'Wv': Wv, 'Wk': Wk, 'Wq': Wq, 'Wo': Wo, 'bo': bo}
    _L0_xattn_all = _L0_xattn_setup()
    _L0_xattn_in = {k: v for k, v in _L0_xattn_all.items() if k in ('Wv', 'Wk', 'Wq', 'Wo', 'bo')}
    del _L0_xattn_all

    def _L0_ffn_setup():
        import jax, jax.numpy as jnp
        import numpy as np
        TOP_K = 2

        def gelu(x):
            return jax.nn.gelu(x, approximate=False)
        key = jax.random.key(seed)
        ks = jax.random.split(key, 6)
        B, L, D, H, E, S = (4, 512, 256, 512, 8, 2)
        sd = 0.02
        return {'x': jax.random.normal(ks[0], (B, L, D), dtype=jnp.float32), 'router_w': jax.random.normal(ks[1], (D, E), dtype=jnp.float32) * sd, 'router_b': jnp.zeros((E,), dtype=jnp.float32), 'w1': jax.random.normal(ks[2], (E, D, H), dtype=jnp.float32) * sd, 'b1': jnp.zeros((E, H), dtype=jnp.float32), 'w2': jax.random.normal(ks[3], (E, H, D), dtype=jnp.float32) * sd, 'b2': jnp.zeros((E, D), dtype=jnp.float32), 'sw1': jax.random.normal(ks[4], (S, D, H), dtype=jnp.float32) * sd, 'sb1': jnp.zeros((S, H), dtype=jnp.float32), 'sw2': jax.random.normal(ks[5], (S, H, D), dtype=jnp.float32) * sd, 'sb2': jnp.zeros((S, D), dtype=jnp.float32)}
    _L0_ffn_all = _L0_ffn_setup()
    _L0_ffn_in = {k: v for k, v in _L0_ffn_all.items() if k in ('router_w', 'router_b', 'w1', 'b1', 'w2', 'b2', 'sw1', 'sb1', 'sw2', 'sb2')}
    del _L0_ffn_all
    return {'x': x, 'ctx_1024': ctx_1024, 'L0_xattn_Wv': _L0_xattn_in['Wv'], 'L0_xattn_Wk': _L0_xattn_in['Wk'], 'L0_xattn_Wq': _L0_xattn_in['Wq'], 'L0_xattn_Wo': _L0_xattn_in['Wo'], 'L0_xattn_bo': _L0_xattn_in['bo'], 'L0_ffn_router_w': _L0_ffn_in['router_w'], 'L0_ffn_router_b': _L0_ffn_in['router_b'], 'L0_ffn_w1': _L0_ffn_in['w1'], 'L0_ffn_b1': _L0_ffn_in['b1'], 'L0_ffn_w2': _L0_ffn_in['w2'], 'L0_ffn_b2': _L0_ffn_in['b2'], 'L0_ffn_sw1': _L0_ffn_in['sw1'], 'L0_ffn_sb1': _L0_ffn_in['sb1'], 'L0_ffn_sw2': _L0_ffn_in['sw2'], 'L0_ffn_sb2': _L0_ffn_in['sb2']}

def reference(x, ctx_1024, L0_xattn_Wv, L0_xattn_Wk, L0_xattn_Wq, L0_xattn_Wo, L0_xattn_bo, L0_ffn_router_w, L0_ffn_router_b, L0_ffn_w1, L0_ffn_b1, L0_ffn_w2, L0_ffn_b2, L0_ffn_sw1, L0_ffn_sb1, L0_ffn_sw2, L0_ffn_sb2):
    import jax
    import jax.numpy as jnp

    def _L0_xattn_ref(value, key, query, Wv, Wk, Wq, Wo, bo):
        import jax, jax.numpy as jnp
        import numpy as np
        EMBED = 256
        HEADS = 16
        HEAD_DIM = EMBED // HEADS
        B = query.shape[0]

        def split(x, W):
            y = jnp.einsum('bse,fe->bsf', x, W)
            return y.reshape(B, -1, HEADS, HEAD_DIM).transpose(0, 2, 1, 3)
        v = split(value, Wv)
        k = split(key, Wk)
        q = split(query, Wq)
        scores = jnp.einsum('bhqd,bhkd->bhqk', q, k) / jnp.sqrt(jnp.float32(HEAD_DIM))
        attn = jax.nn.softmax(scores, axis=-1)
        out = jnp.einsum('bhqk,bhkd->bhqd', attn, v)
        out = out.transpose(0, 2, 1, 3).reshape(B, -1, EMBED)
        return jnp.einsum('bse,fe->bsf', out, Wo) + bo

    def _L0_ffn_ref(x, router_w, router_b, w1, b1, w2, b2, sw1, sb1, sw2, sb2):
        import jax, jax.numpy as jnp
        import numpy as np
        TOP_K = 2

        def gelu(x):
            return jax.nn.gelu(x, approximate=False)
        B, L, D = x.shape
        E = router_b.shape[0]
        S = sw1.shape[0]
        xf = x.reshape(-1, D)
        sh = gelu(jnp.einsum('nd,sdh->snh', xf, sw1) + sb1[:, None, :])
        shared_out = (jnp.einsum('snh,shd->nd', sh, sw2) + sb2.sum(0)) / S
        gates = xf @ router_w + router_b
        topv, topi = jax.lax.top_k(gates, TOP_K)
        probs = jax.nn.softmax(topv, axis=-1)
        comb = jnp.einsum('nke,nk->ne', jax.nn.one_hot(topi, E, dtype=xf.dtype), probs)
        h = gelu(jnp.einsum('nd,edh->enh', xf, w1) + b1[:, None, :])
        y = jnp.einsum('enh,ehd->end', h, w2) + b2[:, None, :]
        moe_out = jnp.einsum('ne,end->nd', comb, y)
        return (shared_out + moe_out).reshape(B, L, D)
    x = x + _L0_xattn_ref(ctx_1024, ctx_1024, _layernorm(x, axis=-1), L0_xattn_Wv, L0_xattn_Wk, L0_xattn_Wq, L0_xattn_Wo, L0_xattn_bo)
    x = x + _L0_ffn_ref(_layernorm(x, axis=-1), L0_ffn_router_w, L0_ffn_router_b, L0_ffn_w1, L0_ffn_b1, L0_ffn_w2, L0_ffn_b2, L0_ffn_sw1, L0_ffn_sb1, L0_ffn_sw2, L0_ffn_sb2)
    return x

_drawn_inputs = setup_inputs


def setup_inputs(seed=0):
    import zlib

    import numpy as np

    out = dict(_drawn_inputs(seed))
    spreads = {'L0_ffn_router_b': (0.0, 0.1),
     'L0_ffn_b1': (0.0, 0.513),
     'L0_ffn_b2': (0.0, 0.1),
     'L0_ffn_sb1': (0.0, 0.489),
     'L0_ffn_sb2': (0.0, 0.1)}
    factors = {'L0_xattn_bo': 5.497}
    for name, (base, spread) in spreads.items():
        noise = np.random.default_rng([zlib.crc32(name.encode()), seed]).standard_normal(out[name].shape)
        drawn = base * np.exp(spread * noise) if base else spread * noise
        out[name] = jnp.asarray(drawn.astype(out[name].dtype))
    for name, factor in factors.items():
        out[name] = (out[name] * factor).astype(out[name].dtype)
    return out
```

```python
import numpy as np
import concourse.bass as bass
from concourse import mybir
from contextlib import ExitStack

F32 = mybir.dt.float32
F32R = mybir.dt.float32r
BF16 = mybir.dt.bfloat16
I32 = mybir.dt.int32
U32 = mybir.dt.uint32
ALU = mybir.AluOpType
ACT = mybir.ActivationFunctionType
AX = mybir.AxisListType

P = 128
B, S, D = 4, 512, 256
TOK = B * S
NT = TOK // P
TPB = S // P
L = 64
NH, HD = 16, 16
C = D // P
HPC = P // HD
NJ = NH // 2
NE, NSH, HF = 8, 2, 512
HC = HF // P
EPS = 1e-5
LAST = 8
ROW = D + 4
CAP = TOK + P
FILL_ROW = NE * CAP
XG_ROWS = FILL_ROW + P
TILES = (2 * TOK + NE * (P - 1)) // P
SKIP = 2 * TOK + 4096


def attention(nc, ios, keep, scratch):
    (x, ctx, Wv, Wk, Wq, Wo, bo, rw, rb, sb2) = ios
    p12, counts, metas = keep
    x1_d, xt_d, xg_d = scratch
    with ExitStack() as es:
        def sb(name, shape, dt=F32):
            return es.enter_context(nc.sbuf_tensor(name, shape, dt))

        def sem(name):
            return es.enter_context(nc.semaphore(name))

        xres = sb("xres", [P, NT, D])
        wraw = sb("wraw", [P, 4, C, D])
        craw = sb("craw", [P, C, D])
        WT = sb("WT", [P, 4, C, D])
        ctxT = sb("ctxT", [P, C, B * L])
        ctxT2 = sb("ctxT2", [P, C, B, 2, L])
        KT = sb("KT", [P, C, B, L])
        Vsb = sb("Vsb", [P, B, D])
        Kbd = sb("Kbd", [P, 2, C, HPC, L])
        Vbd = sb("Vbd", [P, 2, NJ, P])
        maskK = sb("maskK", [P, HPC])
        maskV = sb("maskV", [P, 4, HPC])
        ident = sb("ident", [P, P])
        tri = sb("tri", [P, P], BF16)
        ones = sb("ones", [P, P], BF16)
        bo_bc = sb("bo_bc", [P, D])
        rb_bc = sb("rb_bc", [P, NE])
        sb2_bc = sb("sb2_bc", [P, NSH, D])
        sbh = sb("sbh", [P, D])
        rws = sb("rws", [P, C, NE])
        iota8 = sb("iota8", [P, NE])
        ebase = sb("ebase", [P, NE])
        ids = sb("ids", [P, 2, NT], I32)
        half = sb("half", [P, 1])
        st1 = sb("st1", [P, NT, 6])
        mv1 = sb("mv1", [P, NT, 2])
        ve1 = sb("ve1", [P, NT])
        rs1 = sb("rs1", [P, NT])
        st2 = sb("st2", [P, NT, 6])
        mv2 = sb("mv2", [P, NT, 2])
        ve2 = sb("ve2", [P, NT])
        rs2 = sb("rs2", [P, NT])
        xn = sb("xn", [P, 2, D])
        xnT = sb("xnT", [P, 2, C, P])
        QT = sb("QT", [P, 2, C, P])
        mx = sb("mx", [P, 2, NH])
        sm = sb("sm", [P, 2, NH])
        inv = sb("inv", [P, 2, NH])
        Pr = sb("Pr", [P, 3, NH, L])
        PT = sb("PT", [P, 2, NJ, P])
        OT = sb("OT", [P, 2, C, P])
        x1 = sb("x1", [P, 2, D])
        x1s = sb("x1s", [P, 2, D])
        rows = sb("rows", [P, 2, 2, TPB, ROW])
        x2T = sb("x2T", [P, 2, C, P])
        gates = sb("gates", [P, TPB, NE])
        top = sb("top", [P, TPB, 8])
        topi = sb("topi", [P, TPB, 8], U32)
        topf = sb("topf", [P, 2, TPB])
        oh = sb("oh", [P, 2, TPB, NE])
        ohs = sb("ohs", [P, NT, NE], BF16)
        ohc = sb("ohc", [P, TPB + 1, NE], BF16)
        gd = sb("gd", [P, TPB])
        ge = sb("ge", [P, TPB])
        ge1 = sb("ge1", [P, TPB])
        rk = sb("rk", [P, TPB, NE])
        pk = sb("pk", [P, 2, TPB, NE])
        slotf = sb("slotf", [P, 2, TPB])
        slots = sb("slots", [P, 2, 2, TPB], I32)
        filler = sb("filler", [P, ROW])
        psS = es.enter_context(nc.psum_tensor("psS", [P, 2, C, 512], F32))
        psP = es.enter_context(nc.psum_tensor("psP", [P, NJ, P], F32))
        psA = es.enter_context(nc.psum_tensor("psA", [P, 512], F32))
        psD = es.enter_context(nc.psum_tensor("psD", [P, 512], F32))
        psW = psS[:, :, :, :].rearrange("p a c n -> p (a c) n")

        ld_w, ld_c, ld_small = sem("ld_w"), sem("ld_c"), sem("ld_small")
        ld_x = [sem(f"ld_x{b}") for b in range(B)]
        consts, fillers = sem("consts"), sem("fillers")
        wt_psum, wt_sb = sem("wt_psum"), sem("wt_sb")
        ctxt_psum, ctxt_sb = sem("ctxt_psum"), sem("ctxt_sb")
        kv_psum, kv_sb = sem("kv_psum"), sem("kv_sb")
        kbd_ready, vbd_ready = sem("kbd_ready"), sem("vbd_ready")
        st1_done, mv1_done, ve1_done, rs1_done, xn_done = sem("st1_done"), sem("mv1_done"), sem("ve1_done"), sem("rs1_done"), sem("xn_done")
        xnt_psum, xnt_sb, qt_psum, qt_sb = sem("xnt_psum"), sem("xnt_sb"), sem("qt_psum"), sem("qt_sb")
        scores_done, max_done, shift_done, exp_done = sem("scores_done"), sem("max_done"), sem("shift_done"), sem("exp_done")
        sum_done, inv_done, probs_done = sem("sum_done"), sem("inv_done"), sem("probs_done")
        pt_psum, pt_sb, ot_psum, ot_sb = sem("pt_psum"), sem("pt_sb"), sem("ot_psum"), sem("ot_sb")
        att_psum, x1_done, x1s_done, x1_stored = sem("att_psum"), sem("x1_done"), sem("x1s_done"), [sem(f"x1_stored{i}") for i in range(2)]
        xbo_done, sbh_done, small_done = sem("xbo_done"), sem("sbh_done"), sem("small_done")
        st2_done, mv2_done, ve2_done, rs2_done, rows_done = sem("st2_done"), sem("mv2_done"), sem("ve2_done"), sem("rs2_done"), sem("rows_done")
        x2t_psum, x2t_sb, x2t_stored = sem("x2t_psum"), sem("x2t_sb"), [sem(f"x2t_stored{i}") for i in range(2)]
        gates_psum, gates_done = sem("gates_psum"), sem("gates_done")
        ids_done = sem("ids_done")
        route, gap_ready, exp2_done, ohs_ready, ranks_psum = sem("route"), sem("gap_ready"), sem("exp2_done"), sem("ohs_ready"), sem("ranks_psum")
        ranks_read, slots_ready, scattered, total_psum = sem("ranks_read"), sem("slots_ready"), [sem(f"scattered{i}") for i in range(2)], sem("total_psum")
        block = es.enter_context(nc.Block())

        @block.sync
        def _(sp):
            for m, w in enumerate((Wq, Wk, Wv, Wo)):
                sp.dma_start(wraw[:, m], w.rearrange("(c p) e -> p c e", p=P)).then_inc(ld_w, 16)
            for b in range(B):
                sp.dma_start(xres[:, b * TPB:(b + 1) * TPB], x[b].rearrange("(t p) d -> p t d", p=P)).then_inc(ld_x[b], 16)
            for g in range(NT):
                sp.wait_ge(x1s_done, g + 1)
                sp.dma_start(x1_d[g], x1s[:, g % 2]).then_inc(x1_stored[g % 2], 16)
                sp.wait_ge(x2t_sb, g + 1)
                sp.dma_start(xt_d[:, :, g * P:(g + 1) * P], x2T[:, g % 2]).then_inc(x2t_stored[g % 2], 16)
            for parity in range(2):
                sp.wait_ge(x1_stored[parity], 16 * NT // 2)
                sp.wait_ge(x2t_stored[parity], 16 * NT // 2)

        @block.gpsimd
        def _(pool):
            pool.memset(ident[:], 0.0).then_inc(consts, 1)
            pool.memset(maskK[:], 1.0).then_inc(consts, 1)
            pool.memset(maskV[:], 1.0).then_inc(consts, 1)
            pool.memset(tri[:], 1.0).then_inc(consts, 1)
            pool.memset(ones[:], 1.0).then_inc(consts, 1)
            pool.memset(half[:], -0.5).then_inc(consts, 1)
            pool.memset(filler[:], 0.0).then_inc(consts, 1)
            pool.memset(rows[:, :, :, :, D:ROW], 0.0).then_inc(consts, 1)
            pool.wait_ge(consts, 8)
            pool.affine_select(out=ident[:], in_=ident[:], compare_op=ALU.not_equal, fill=1.0, base=0,
                               pattern=[[-1, P]], channel_multiplier=1).then_inc(consts, 1)
            pool.affine_select(out=tri[:], in_=tri[:], compare_op=ALU.is_ge, fill=0.0, base=-1,
                               pattern=[[1, P]], channel_multiplier=-1).then_inc(consts, 1)
            pool.affine_select(out=maskK[:], in_=maskK[:], compare_op=ALU.is_ge, fill=0.0, base=0,
                               pattern=[[-HD, HPC]], channel_multiplier=1).then_inc(consts, 1)
            pool.affine_select(out=maskV[:], in_=maskV[:], compare_op=ALU.is_ge, fill=0.0, base=0,
                               pattern=[[2 * L, 4], [-L, HPC]], channel_multiplier=1).then_inc(consts, 1)
            pool.iota(iota8[:], pattern=[[1, NE]], base=0, channel_multiplier=0,
                      allow_small_or_imprecise_dtypes=True).then_inc(consts, 1)
            pool.iota(ebase[:], pattern=[[CAP, NE]], base=0, channel_multiplier=0,
                      allow_small_or_imprecise_dtypes=True).then_inc(consts, 1)
            pool.iota(ids[:, 0, :], pattern=[[P, NT]], base=0, channel_multiplier=1).then_inc(consts, 1)
            pool.iota(ids[:, 1, :], pattern=[[P, NT]], base=TOK, channel_multiplier=1).then_inc(consts, 1)
            pool.iota(filler[:, D:D + 1].bitcast(I32), pattern=[[0, 1]], base=SKIP, channel_multiplier=1).then_inc(consts, 1)
            pool.wait_ge(consts, 17)
            pool.affine_select(out=maskK[:], in_=maskK[:], compare_op=ALU.is_ge, fill=0.0, base=HD - 1,
                               pattern=[[HD, HPC]], channel_multiplier=-1).then_inc(consts, 1)
            pool.affine_select(out=maskV[:], in_=maskV[:], compare_op=ALU.is_ge, fill=0.0, base=L - 1,
                               pattern=[[-2 * L, 4], [L, HPC]], channel_multiplier=-1).then_inc(consts, 1)
            pool.dma_start(xg_d[FILL_ROW:FILL_ROW + P, :], filler[:]).then_inc(fillers, 16)
            pool.wait_ge(ld_small, 16 * 4)
            pool.tensor_tensor(out=sbh[:], in0=sb2_bc[:, 0], in1=sb2_bc[:, 1], op=ALU.add).then_inc(small_done, 1)
            pool.wait_ge(small_done, 1)
            pool.tensor_scalar(out=sbh[:], in0=sbh[:], scalar1=1.0 / NSH, scalar2=None, op0=ALU.mult).then_inc(small_done, 1)
            pool.wait_ge(small_done, 2)

            def k_diagonal(b):
                if b == 0:
                    pool.wait_ge(kv_sb, C)
                    pool.wait_ge(consts, 19)
                if b >= 2:
                    pool.wait_ge(scores_done, TPB * (b - 1))
                for c in range(C):
                    pool.tensor_tensor(out=Kbd[:, b % 2, c], in0=KT[:, c, b].unsqueeze(1).to_broadcast([P, HPC, L]),
                                       in1=maskK[:].unsqueeze(2).to_broadcast([P, HPC, L]), op=ALU.mult).then_inc(kbd_ready, 1)

            k_diagonal(0)

            def rstd1(g):
                pool.wait_ge(ve1_done, g + 1)
                pool.tensor_tensor(out=rs1[:, g:g + 1], in0=ve1[:, g:g + 1], in1=half[:], op=ALU.pow).then_inc(rs1_done, 1)

            for g in range(TPB):
                rstd1(g)
            for s in range(NT + LAST):
                if 5 <= s < NT + 5:
                    g = s - 5
                    pool.wait_ge(ve2_done, g + 1)
                    pool.tensor_tensor(out=rs2[:, g:g + 1], in0=ve2[:, g:g + 1], in1=half[:], op=ALU.pow).then_inc(rs2_done, 1)
                if 1 <= s and s + TPB - 1 < NT:
                    rstd1(s + TPB - 1)
                if 1 <= s <= NT:
                    g = s - 1
                    pool.wait_ge(inv_done, g + 1)
                    pool.tensor_tensor(out=Pr[:, g % 3], in0=Pr[:, g % 3], in1=inv[:, g % 2].unsqueeze(2).to_broadcast([P, NH, L]),
                                       op=ALU.mult).then_inc(probs_done, 1)
                if s % TPB == 1 and s // TPB + 1 < B:
                    k_diagonal(s // TPB + 1)
                if 5 <= s < NT + 5:
                    g = s - 5
                    if g >= 2:
                        pool.wait_ge(x1_stored[g % 2], 16 * (g // 2))
                    pool.tensor_tensor(out=x1s[:, g % 2], in0=x1[:, g % 2], in1=sbh[:], op=ALU.add).then_inc(x1s_done, 1)
                if s >= 7 + 3 and (s - 7) % TPB == 3:
                    b = (s - 7) // TPB
                    if b >= 2:
                        pool.wait_ge(scattered[b % 2], 16 * 2 * TPB * (b // 2))
                    pool.tensor_copy(rows[:, b % 2, :, :, D].bitcast(I32), ids[:, :, b * TPB:(b + 1) * TPB]).then_inc(ids_done, 1)
                    pool.wait_ge(ids_done, b + 1)
                    pool.wait_ge(slots_ready, b + 1)
                    for t in range(TPB):
                        for k in range(2):
                            pool.indirect_dma_start(xg_d, bass.IndirectOffsetOnAxis(ap=slots[:, b % 2, k, t:t + 1], axis=0),
                                                    rows[:, b % 2, k, t, :], None).then_inc(scattered[b % 2], 16)
            for parity in range(2):
                pool.wait_ge(scattered[parity], 16 * NT)
            pool.wait_ge(fillers, 16)

        @block.scalar
        def _(act):
            nc.scalar.dma_start(craw[:], ctx.rearrange("(r b) k e -> (b k) r e", b=2)).then_inc(ld_c, 16)
            nc.scalar.dma_start(bo_bc[:], bo.partition_broadcast(P)).then_inc(ld_small, 16)
            nc.scalar.dma_start(rb_bc[:], rb.partition_broadcast(P)).then_inc(ld_small, 16)
            nc.scalar.dma_start(sb2_bc[:], sb2.partition_broadcast(P)).then_inc(ld_small, 16)
            nc.scalar.dma_start(rws[:], rw.rearrange("(c p) e -> p c e", p=P)).then_inc(ld_small, 16)
            for m in range(4):
                act.wait_ge(wt_psum, m + 1)
                nc.scalar.activation(WT[:, m], psW[:, m].rearrange("p (c f) -> p c f", c=C), ACT.Copy).then_inc(wt_sb, 1)
            act.wait_ge(ctxt_psum, 1)
            nc.scalar.activation(ctxT[:], psA[:, :].rearrange("p (c n) -> p c n", c=C), ACT.Copy).then_inc(ctxt_sb, 1)
            for c in range(C):
                nc.scalar.activation(ctxT2[:, c], psA[:, c * 256:(c + 1) * 256].rearrange("p (b k) -> p b k", b=B).unsqueeze(2).to_broadcast([P, B, 2, L]),
                                     ACT.Copy).then_inc(ctxt_sb, 1)
            act.wait_ge(kv_psum, 1)
            nc.scalar.activation(KT[:, 0], psP[:, 0:2].rearrange("p a (b k) -> p (a b) k", k=L), ACT.Copy, scale=float(HD) ** -0.5).then_inc(kv_sb, 1)
            nc.scalar.activation(KT[:, 1], psP[:, 4:6].rearrange("p a (b k) -> p (a b) k", k=L), ACT.Copy, scale=float(HD) ** -0.5).then_inc(kv_sb, 1)
            act.wait_ge(kv_psum, 2)
            nc.scalar.activation(Vsb[:], psW[:, :, 0:D], ACT.Copy).then_inc(kv_sb, 1)

            def xnt_evac(g):
                act.wait_ge(xnt_psum, g + 1)
                if g >= 2:
                    act.wait_ge(qt_psum, g - 1)
                nc.scalar.activation(xnT[:, g % 2], psA[:, 0:D].rearrange("p (c n) -> p c n", c=C), ACT.Copy).then_inc(xnt_sb, 1)

            def qt_evac(g):
                act.wait_ge(qt_psum, g + 1)
                if g >= 2:
                    act.wait_ge(scores_done, g - 1)
                nc.scalar.activation(QT[:, g % 2], psA[:, D:2 * D].rearrange("p (c n) -> p c n", c=C), ACT.Copy).then_inc(qt_sb, 1)

            xnt_evac(0)
            qt_evac(0)
            for s in range(NT + LAST):
                if s >= 7 + 3 and (s - 7) % TPB == 3:
                    act.wait_ge(gap_ready, (s - 7) // TPB + 1)
                    nc.scalar.activation(ge[:], gd[:], ACT.Exp).then_inc(exp2_done, 1)
                if s + 1 < NT:
                    xnt_evac(s + 1)
                    qt_evac(s + 1)
                if s < NT:
                    act.wait_ge(shift_done, s + 1)
                    nc.scalar.activation(Pr[:, s % 3], Pr[:, s % 3], ACT.Exp).then_inc(exp_done, 1)
                if 3 <= s < NT + 3:
                    g = s - 3
                    act.wait_ge(ot_psum, g + 1)
                    if g >= 2:
                        act.wait_ge(att_psum, g - 1)
                    nc.scalar.activation(OT[:, g % 2], psA[:, D:2 * D].rearrange("p (c n) -> p c n", c=C), ACT.Copy).then_inc(ot_sb, 1)
                if 2 <= s < NT + 2:
                    g = s - 2
                    act.wait_ge(pt_psum, g + 1)
                    if g >= 2:
                        act.wait_ge(ot_psum, g - 1)
                    nc.scalar.activation(PT[:, g % 2], psP[:], ACT.Copy).then_inc(pt_sb, 1)
                if 5 <= s < NT + 5:
                    g = s - 5
                    act.wait_ge(x2t_psum, g + 1)
                    if g >= 2:
                        act.wait_ge(gates_psum, g - 1)
                        act.wait_ge(x2t_stored[g % 2], 16 * (g // 2))
                    nc.scalar.activation(x2T[:, g % 2], psA[:, 0:D].rearrange("p (c n) -> p c n", c=C), ACT.Copy).then_inc(x2t_sb, 1)

        @block.vector
        def _(dve):
            dve.wait_ge(ld_small, 16 * 4)

            def stats(g):
                b = g // TPB
                if g % TPB == 0:
                    dve.wait_ge(ld_x[b], 16)
                nc.vector.bn_stats(st1[:, g], xres[:, g]).then_inc(st1_done, 1)

            def norm1(g):
                dve.wait_ge(rs1_done, g + 1)
                if g >= 2:
                    dve.wait_ge(xnt_psum, g - 1)
                nc.vector.tensor_scalar(out=xn[:, g % 2], in0=xres[:, g], scalar1=mv1[:, g, 0:1], scalar2=rs1[:, g:g + 1],
                                        op0=ALU.subtract, op1=ALU.mult).then_inc(xn_done, 1)

            def aggregate(g):
                dve.wait_ge(st1_done, g + 1)
                nc.vector.bn_aggr(mv1[:, g], st1[:, g]).then_inc(mv1_done, 1)
                dve.wait_ge(mv1_done, g + 1)
                nc.vector.tensor_scalar(out=ve1[:, g:g + 1], in0=mv1[:, g, 1:2], scalar1=EPS, scalar2=None, op0=ALU.add).then_inc(ve1_done, 1)

            for g in range(TPB + 1):
                stats(g)
            for g in range(TPB):
                aggregate(g)
            norm1(0)
            norm1(1)

            def v_diagonal(b):
                if b == 0:
                    dve.wait_ge(kv_sb, C + 1)
                    dve.wait_ge(consts, 19)
                if b >= 2:
                    dve.wait_ge(ot_psum, TPB * (b - 1))
                for c in range(C):
                    nc.vector.tensor_tensor(out=Vbd[:, b % 2, 4 * c:4 * c + 4].rearrange("p j (h d) -> p j h d", d=HD),
                                            in0=Vsb[:, b, c * P:(c + 1) * P].rearrange("p (h d) -> p h d", d=HD).unsqueeze(1).to_broadcast([P, 4, HPC, HD]),
                                            in1=maskV[:].unsqueeze(3).to_broadcast([P, 4, HPC, HD]), op=ALU.mult).then_inc(vbd_ready, 1)

            v_diagonal(0)
            routed = [0]

            def chain(ins):
                routed[0] += 1
                ins.then_inc(route, 1)
                dve.wait_ge(route, routed[0])

            chain(nc.vector.memset(ohc[:, 0], 0.0))

            def choose(b):
                dve.wait_ge(gates_done, TPB * (b + 1))
                for t in range(TPB):
                    ins = nc.vector.max(out=top[:, t], in_=gates[:, t])
                chain(ins)
                for t in range(TPB):
                    ins = nc.vector.max_index(out=topi[:, t], in_max=top[:, t], in_values=gates[:, t])
                chain(ins)
                nc.vector.tensor_tensor(out=gd[:], in0=top[:, :, 1], in1=top[:, :, 0], op=ALU.subtract).then_inc(gap_ready, 1)
                chain(nc.vector.tensor_copy(topf[:].rearrange("p k t -> p t k"), topi[:, :, 0:2]))
                for k in range(2):
                    ins = nc.vector.tensor_tensor(out=oh[:, k], in0=iota8[:].unsqueeze(1).to_broadcast([P, TPB, NE]),
                                                  in1=topf[:, k].unsqueeze(2).to_broadcast([P, TPB, NE]), op=ALU.is_equal)
                chain(ins)
                chain(nc.vector.tensor_tensor(out=ohs[:, b * TPB:(b + 1) * TPB], in0=oh[:, 0], in1=oh[:, 1], op=ALU.add))
                for t in range(TPB):
                    ins = nc.vector.tensor_tensor(out=ohc[:, t + 1], in0=ohc[:, t], in1=ohs[:, b * TPB + t], op=ALU.add)
                    if t < TPB - 1:
                        chain(ins)
                ins.then_inc(ohs_ready, 1)

            def place(b):
                dve.wait_ge(ranks_psum, b + 1)
                nc.vector.tensor_tensor(out=rk[:], in0=psD[:, 384:384 + TPB * NE].rearrange("p (t e) -> p t e", e=NE),
                                        in1=ebase[:].unsqueeze(1).to_broadcast([P, TPB, NE]), op=ALU.add).then_inc(ranks_read, 1)
                dve.wait_ge(ranks_read, b + 1)
                for k in range(2):
                    ins = nc.vector.tensor_tensor(out=pk[:, k], in0=oh[:, k], in1=rk[:], op=ALU.mult)
                chain(ins)
                chain(nc.vector.reduce_sum(slotf[:], pk[:], axis=AX.X))
                if b >= 2:
                    dve.wait_ge(scattered[b % 2], 16 * 2 * TPB * (b // 2))
                nc.vector.tensor_copy(slots[:, b % 2], slotf[:]).then_inc(slots_ready, 1)
                dve.wait_ge(exp2_done, b + 1)
                chain(nc.vector.tensor_scalar(out=ge1[:], in0=ge[:], scalar1=1.0, scalar2=None, op0=ALU.add))
                chain(nc.vector.reciprocal(p12[:, 0, b * TPB:(b + 1) * TPB], ge1[:]))
                chain(nc.vector.tensor_tensor(out=p12[:, 1, b * TPB:(b + 1) * TPB], in0=p12[:, 0, b * TPB:(b + 1) * TPB], in1=ge[:], op=ALU.mult))
                if b + 1 < B:
                    chain(nc.vector.tensor_copy(ohc[:, 0], ohc[:, TPB]))

            for s in range(NT + LAST):
                if s < NT:
                    dve.wait_ge(scores_done, s + 1)
                    v = psS[:, s % 2].rearrange("p c (h k) -> p (c h) k", k=L)
                    nc.vector.reduce_max(mx[:, s % 2], v, axis=AX.X).then_inc(max_done, 1)
                if 4 <= s < NT + 4:
                    g = s - 4
                    dve.wait_ge(att_psum, g + 1)
                    dve.wait_ge(xbo_done, g + 1)
                    if g >= 2:
                        dve.wait_ge(x1s_done, g - 1)
                    nc.vector.tensor_tensor(out=x1[:, g % 2], in0=psD[:, 0:D], in1=xres[:, g], op=ALU.add).then_inc(x1_done, 1)
                if s < NT:
                    if s >= 3:
                        dve.wait_ge(pt_psum, s - 2)
                    dve.wait_ge(max_done, s + 1)
                    nc.vector.tensor_tensor(out=Pr[:, s % 3], in0=v, in1=mx[:, s % 2].unsqueeze(2).to_broadcast([P, NH, L]),
                                            op=ALU.subtract).then_inc(shift_done, 1)
                if s + 2 < NT:
                    norm1(s + 2)
                if 5 <= s < NT + 5:
                    g = s - 5
                    b, t = g // TPB, g % TPB
                    dve.wait_ge(rs2_done, g + 1)
                    if b >= 2 and t == 0:
                        dve.wait_ge(scattered[b % 2], 16 * 2 * TPB * (b // 2))
                    for k in range(2):
                        nc.vector.tensor_scalar(out=rows[:, b % 2, k, t, 0:D], in0=x1[:, g % 2], scalar1=mv2[:, g, 0:1],
                                                scalar2=rs2[:, g:g + 1], op0=ALU.subtract, op1=ALU.mult).then_inc(rows_done, 1)
                if s < NT:
                    nc.vector.tensor_tensor(out=xres[:, s], in0=xres[:, s], in1=bo_bc[:], op=ALU.add).then_inc(xbo_done, 1)
                if 4 <= s < NT + 4:
                    g = s - 4
                    dve.wait_ge(x1_done, g + 1)
                    nc.vector.bn_stats(st2[:, g], x1[:, g % 2]).then_inc(st2_done, 1)
                if s + TPB < NT:
                    aggregate(s + TPB)
                if s % TPB == 3 and s // TPB + 1 < B:
                    v_diagonal(s // TPB + 1)
                if s < NT:
                    dve.wait_ge(exp_done, s + 1)
                    nc.vector.reduce_sum(sm[:, s % 2], Pr[:, s % 3], axis=AX.X).then_inc(sum_done, 1)
                if 4 <= s < NT + 4:
                    dve.wait_ge(st2_done, g + 1)
                    nc.vector.bn_aggr(mv2[:, g], st2[:, g]).then_inc(mv2_done, 1)
                if s + TPB + 1 < NT:
                    stats(s + TPB + 1)
                if s < NT:
                    dve.wait_ge(sum_done, s + 1)
                    if s >= 2:
                        dve.wait_ge(probs_done, s - 1)
                    nc.vector.reciprocal(inv[:, s % 2], sm[:, s % 2]).then_inc(inv_done, 1)
                if 4 <= s < NT + 4:
                    dve.wait_ge(mv2_done, g + 1)
                    nc.vector.tensor_scalar(out=ve2[:, g:g + 1], in0=mv2[:, g, 1:2], scalar1=EPS, scalar2=None, op0=ALU.add).then_inc(ve2_done, 1)
                if s >= 7 + 3 and (s - 7) % TPB == 3:
                    place((s - 7) // TPB)
                if 6 <= s < NT + 6:
                    n = s - 6
                    dve.wait_ge(gates_psum, n + 1)
                    nc.vector.tensor_tensor(out=gates[:, n % TPB], in0=psD[:, D:D + NE], in1=rb_bc[:], op=ALU.add).then_inc(gates_done, 1)
                    if n % TPB == TPB - 1:
                        choose(n // TPB)
            dve.wait_ge(total_psum, 1)
            nc.vector.tensor_copy(counts[:], psD[:, 0:NE]).then_inc(metas, 1)

        @block.tensor
        def _(pe):
            pe.wait_ge(consts, 17)
            pe.wait_ge(ld_w, 16 * 4)
            for m in range(4):
                for c in range(C):
                    for f in range(C):
                        last = nc.tensor.transpose(psW[:, m, c * D + f * P:c * D + (f + 1) * P], wraw[:, m, f, c * P:(c + 1) * P], ident[:])
                last.then_inc(wt_psum, 1)
            pe.wait_ge(ld_c, 16)
            for c in range(C):
                for r in range(C):
                    last = nc.tensor.transpose(psA[:, c * 256 + r * P:c * 256 + (r + 1) * P], craw[:, r, c * P:(c + 1) * P], ident[:])
            last.then_inc(ctxt_psum, 1)
            pe.wait_ge(ctxt_sb, 1 + C)
            pe.wait_ge(wt_sb, 4)
            for f in range(C):
                for c in range(C):
                    last = nc.tensor.matmul(psP[:, 4 * f:4 * f + 2].rearrange("p a n -> p (a n)"), WT[:, 1, c, f * P:(f + 1) * P], ctxT[:, c],
                                            start=(c == 0), stop=(c == C - 1))
            last.then_inc(kv_psum, 1)
            for b in range(B):
                for c in range(C):
                    last = nc.tensor.matmul(psW[:, b, 0:D], ctxT2[:, c, b].rearrange("p a k -> p (a k)"), WT[:, 2, c],
                                            start=(c == 0), stop=(c == C - 1))
            last.then_inc(kv_psum, 1)

            def xn_transpose(g):
                pe.wait_ge(xn_done, g + 1)
                for c in range(C):
                    last = nc.tensor.transpose(psA[:, c * P:(c + 1) * P], xn[:, g % 2, c * P:(c + 1) * P], ident[:])
                last.then_inc(xnt_psum, 1)

            def queries(g):
                pe.wait_ge(xnt_sb, g + 1)
                for f in range(C):
                    for c in range(C):
                        last = nc.tensor.matmul(psA[:, D + f * P:D + (f + 1) * P], WT[:, 0, c, f * P:(f + 1) * P], xnT[:, g % 2, c],
                                                start=(c == 0), stop=(c == C - 1))
                last.then_inc(qt_psum, 1)

            xn_transpose(0)
            queries(0)
            pe.wait_ge(kv_sb, C + 1)
            for s in range(NT + LAST):
                if 4 <= s < NT + 4:
                    g = s - 4
                    pe.wait_ge(ot_sb, g + 1)
                    if s >= 7:
                        pe.wait_ge(gates_done, s - 6)
                    if s >= 8 + 3 and (s - 8) % TPB == 3:
                        pe.wait_ge(ranks_read, (s - 8) // TPB + 1)
                    for c in range(C):
                        last = nc.tensor.matmul(psD[:, 0:D], OT[:, g % 2, c], WT[:, 3, c], start=(c == 0), stop=(c == C - 1))
                    last.then_inc(att_psum, 1)
                if s + 1 < NT:
                    if s >= 6:
                        pe.wait_ge(x2t_sb, s - 5)
                    elif s >= 4:
                        pe.wait_ge(ot_sb, s - 3)
                    pe.wait_ge(qt_sb, s + 1)
                    xn_transpose(s + 1)
                if s < NT:
                    b = s // TPB
                    if s % TPB == 0:
                        pe.wait_ge(kbd_ready, C * (b + 1))
                    pe.wait_ge(qt_sb, s + 1)
                    if s >= 2:
                        pe.wait_ge(shift_done, s - 1)
                    for c in range(C):
                        last = nc.tensor.matmul(psS[:, s % 2, c], QT[:, s % 2, c], Kbd[:, b % 2, c].rearrange("p h k -> p (h k)"),
                                                start=True, stop=True)
                    last.then_inc(scores_done, 1)
                if s + 1 < NT:
                    queries(s + 1)
                if 6 <= s < NT + 6:
                    g = s - 6
                    pe.wait_ge(x2t_sb, g + 1)
                    pe.wait_ge(x1_done, min(s - 3, NT))
                    if s >= 7:
                        pe.wait_ge(gates_done, s - 6)
                    if s >= 8 + 3 and (s - 8) % TPB == 3:
                        pe.wait_ge(ranks_read, (s - 8) // TPB + 1)
                    for c in range(C):
                        last = nc.tensor.matmul(psD[:, D:D + NE], x2T[:, g % 2, c], rws[:, c], start=(c == 0), stop=(c == C - 1))
                    last.then_inc(gates_psum, 1)
                if s >= 7 + 3 and (s - 7) % TPB == 3:
                    b = (s - 7) // TPB
                    pe.wait_ge(ohs_ready, b + 1)
                    pe.wait_ge(gates_done, TPB * (b + 1))
                    for t in range(TPB):
                        o = psD[:, 384 + t * NE:384 + (t + 1) * NE]
                        nc.tensor.matmul(o, tri[:], ohs[:, b * TPB + t], start=True, stop=False)
                        last = nc.tensor.matmul(o, ones[:], ohc[:, t], start=False, stop=True)
                    last.then_inc(ranks_psum, 1)
                if 3 <= s < NT + 3:
                    g = s - 3
                    b = g // TPB
                    if g % TPB == 0:
                        pe.wait_ge(vbd_ready, C * (b + 1))
                    pe.wait_ge(pt_sb, g + 1)
                    pe.wait_ge(qt_sb, min(s + 2, NT))
                    if s >= 6:
                        pe.wait_ge(x2t_sb, s - 5)
                    for c in range(C):
                        for j in range(4):
                            last = nc.tensor.matmul(psA[:, D + c * P:D + (c + 1) * P], Vbd[:, b % 2, 4 * c + j], PT[:, g % 2, 4 * c + j],
                                                    start=(j == 0), stop=(j == 3))
                    last.then_inc(ot_psum, 1)
                if 2 <= s < NT + 2:
                    g = s - 2
                    pe.wait_ge(probs_done, g + 1)
                    if g >= 1:
                        pe.wait_ge(pt_sb, g)
                    for j in range(NJ):
                        last = nc.tensor.transpose(psP[:, j], Pr[:, g % 3, 2 * j:2 * j + 2].rearrange("p h k -> p (h k)"), ident[:])
                    last.then_inc(pt_psum, 1)
                if 5 <= s < NT + 5:
                    g = s - 5
                    b, t = g // TPB, g % TPB
                    pe.wait_ge(rows_done, 2 * (g + 1))
                    pe.wait_ge(ot_sb, min(s - 2, NT))
                    for c in range(C):
                        last = nc.tensor.transpose(psA[:, c * P:(c + 1) * P], rows[:, b % 2, 0, t, c * P:(c + 1) * P], ident[:])
                    last.then_inc(x2t_psum, 1)
            pe.wait_ge(slots_ready, B)
            nc.tensor.matmul(psD[:, 0:NE], ones[:], ohc[:, TPB], start=True, stop=True).then_inc(total_psum, 1)


WPE = C * HF + HC * D
HALF = 256
NQ = TOK // HALF


def shared_experts(nc, ios, keep, scratch):
    (w1, w2, sw1, sb1, sw2) = ios
    w_hi, w_lo, counts, row_tab, exp_tab, tabs_ready = keep
    x1_d, xt_d, xg_d, acc_d = scratch
    with ExitStack() as es:
        def sb(name, shape, dt=F32):
            return es.enter_context(nc.sbuf_tensor(name, shape, dt))

        def sem(name):
            return es.enter_context(nc.semaphore(name))

        s_hi = sb("s_hi", [P, NSH, WPE], F32R)
        s_lo = sb("s_lo", [P, NSH, WPE], F32R)
        raw = sb("raw", [P, 2, WPE // 2])
        xt = sb("xt", [P, 2, C, HALF])
        xt_hi = sb("xt_hi", [P, 2, C, HALF], F32R)
        xt_lo = sb("xt_lo", [P, 2, C, HALF], F32R)
        g = sb("g", [P, 2, HALF])
        h_hi = sb("h_hi", [P, NSH, HC, HALF], F32R)
        h_lo = sb("h_lo", [P, NSH, HC, HALF], F32R)
        x1 = sb("x1b", [P, 2, D])
        acc = sb("accs", [P, 2, D])
        sb1T = sb("sb1T", [P, NSH, HC])
        filler = sb("filler2", [P, ROW])
        tile_f = sb("tile_f", [1, TILES])
        ntf = sb("ntf", [1, NE])
        nti = sb("nti", [1, 2, NE], I32)
        cum = sb("cum", [1, NE])
        onef = sb("onef", [1, NE])
        past = sb("past", [1, 2, NE, TILES])
        exp_f = sb("exp_f", [1, TILES])
        row_f = sb("row_f", [1, 3, TILES])
        fill_f = sb("fill_f", [1, 2, NE])
        fill_i = sb("fill_i", [1, NE], I32)
        psH = es.enter_context(nc.psum_tensor("psH", [P, 4, 512], F32))
        psY = es.enter_context(nc.psum_tensor("psY", [P, 4, 512], F32))

        raw_in = [sem(f"raw_in{i}") for i in range(2)]
        hi_done, lo_done = sem("hi_done"), sem("lo_done")
        xt_in = [sem(f"xt_in{i}") for i in range(2)]
        xhi_done, xlo_done = sem("xhi_done"), sem("xlo_done")
        b1_in, h_psum, g_done, hhi_done, hlo_done, y_psum = sem("b1_in"), sem("h_psum"), sem("g_done"), sem("hhi_done"), sem("hlo_done"), sem("y_psum")
        x1_in = [sem(f"x1_in{i}") for i in range(2)]
        acc_done = sem("acc_done")
        acc_out = [sem(f"acc_out{i}") for i in range(2)]
        cst, tab, fill_ready, fill_out = sem("cst"), sem("tab"), sem("fill_ready"), sem("fill_out")
        block = es.enter_context(nc.Block())

        def piece_source(n):
            e, second = n // 2, n % 2
            if e < NSH:
                w = (sw2 if second else sw1)[e]
            else:
                w = (w2 if second else w1)[e - NSH]
            return w.rearrange("(p c) n -> p c n", p=P) if second else w.rearrange("(c p) n -> p c n", p=P)

        def piece_target(which, n):
            e, second = n // 2, n % 2
            t = (s_hi, s_lo)[which] if e < NSH else (w_hi, w_lo)[which]
            e = e if e < NSH else e - NSH
            return t[:, e, second * (WPE // 2):(second + 1) * (WPE // 2)]

        PIECES = 2 * (NSH + NE)

        @block.sync
        def _(sp):
            def load_piece(n):
                if n >= 2:
                    sp.wait_ge(lo_done, n - 1)
                w = piece_source(n)
                sp.dma_start(raw[:, n % 2].rearrange("p (c n) -> p c n", c=w.shape[1]), w).then_inc(raw_in[n % 2], 16)

            def load_x(q):
                if q >= 2:
                    sp.wait_ge(xlo_done, q - 1)
                sp.dma_start(xt[:, q % 2], xt_d[:, :, q * HALF:(q + 1) * HALF]).then_inc(xt_in[q % 2], 16)

            load_piece(0)
            load_piece(1)
            load_x(0)
            load_x(1)
            load_piece(2)
            load_piece(3)
            sp.wait_ge(fill_ready, 1)
            sp.wait_ge(cst, 4)
            for e in range(NE):
                r = sp.value_load(fill_i[0:1, e:e + 1], min_val=0, max_val=FILL_ROW - P)
                sp.dma_start(xg_d[bass.ds(r, P), :], filler[:]).then_inc(fill_out, 16)
            for q in range(NQ):
                load_piece(4 + 2 * q)
                load_piece(5 + 2 * q)
                if q + 2 < NQ:
                    load_x(q + 2)
            sp.wait_ge(fill_out, 16 * NE)

        @block.gpsimd
        def _(pool):
            pool.memset(filler[:], 0.0).then_inc(cst, 1)
            pool.memset(onef[:], 1.0).then_inc(cst, 1)
            pool.iota(tile_f[:], pattern=[[1, TILES]], base=0, channel_multiplier=0,
                      allow_small_or_imprecise_dtypes=True).then_inc(cst, 1)
            pool.wait_ge(cst, 3)
            pool.iota(filler[:, D:D + 1].bitcast(I32), pattern=[[0, 1]], base=SKIP, channel_multiplier=1).then_inc(cst, 1)
            for n in range(PIECES):
                pool.wait_ge(hi_done, n + 1)
                pool.tensor_tensor(out=piece_target(1, n), in0=raw[:, n % 2], in1=piece_target(0, n).bitcast(F32),
                                   op=ALU.subtract).then_inc(lo_done, 1)

        @block.scalar
        def _(act):
            nc.scalar.dma_start(sb1T[:], sb1.rearrange("s (p c) -> p s c", p=P)).then_inc(b1_in, 16)
            done = [0]

            def split(n):
                act.wait_ge(raw_in[n % 2], 16 * (n // 2 + 1))
                nc.scalar.activation(piece_target(0, n), raw[:, n % 2], ACT.Copy).then_inc(hi_done, 1)

            def x1_load(q):
                for u in range(2):
                    t = 2 * q + u
                    if q >= 1:
                        act.wait_ge(acc_done, t - 1)
                    nc.scalar.dma_start(x1[:, u], x1_d[t]).then_inc(x1_in[u], 16)

            for n in range(4):
                split(n)
            act.wait_ge(b1_in, 16)
            for q in range(NQ):
                x1_load(q)
                act.wait_ge(xt_in[q % 2], 16 * (q // 2 + 1))
                if q >= 2:
                    act.wait_ge(h_psum, (q - 1) * NSH * HC)
                nc.scalar.activation(xt_hi[:, q % 2], xt[:, q % 2], ACT.Copy).then_inc(xhi_done, 1)
                for s in range(NSH):
                    for c in range(HC):
                        n = (q * NSH + s) * HC + c
                        act.wait_ge(h_psum, n + 1)
                        if n >= 2:
                            act.wait_ge(hlo_done, n - 1)
                        if q >= 1 and c == 0:
                            act.wait_ge(y_psum, NSH * (q - 1) + s + 1)
                        nc.scalar.activation(g[:, n % 2], psH[:, n % 4, 0:HALF], ACT.Gelu, bias=sb1T[:, s, c:c + 1]).then_inc(g_done, 1)
                        nc.scalar.activation(h_hi[:, s, c], psH[:, n % 4, 0:HALF], ACT.Gelu, bias=sb1T[:, s, c:c + 1]).then_inc(hhi_done, 1)
                for n in range(4 + 2 * q, 6 + 2 * q):
                    split(n)
                for u in range(2):
                    t = 2 * q + u
                    act.wait_ge(acc_done, t + 1)
                    nc.scalar.dma_start(acc_d[t], acc[:, u]).then_inc(acc_out[u], 16)
            for u in range(2):
                act.wait_ge(acc_out[u], 16 * NQ)

        @block.vector
        def _(dve):
            steps = [0]

            def chain(ins):
                steps[0] += 1
                ins.then_inc(tab, 1)
                dve.wait_ge(tab, steps[0])

            V = nc.vector
            dve.wait_ge(cst, 4)
            chain(V.tensor_scalar(out=nti[:, 0], in0=counts[0:1, :], scalar1=float(P - 1), scalar2=None, op0=ALU.add))
            chain(V.tensor_scalar(out=nti[:, 1], in0=nti[:, 0], scalar1=P.bit_length() - 1, scalar2=None, op0=ALU.arith_shift_right))
            chain(V.tensor_copy(ntf[:], nti[:, 1]))
            chain(V.tensor_tensor_scan(out=cum[:], data0=onef[:], data1=ntf[:], initial=0.0, op0=ALU.mult, op1=ALU.add))
            V.tensor_scalar(out=fill_f[:, 0], in0=tile_f[:, 0:NE], scalar1=float(CAP), scalar2=None, op0=ALU.mult)
            chain(V.tensor_tensor(out=past[:, 0], in0=tile_f[:].unsqueeze(1).to_broadcast([1, NE, TILES]),
                                  in1=cum[:].unsqueeze(2).to_broadcast([1, NE, TILES]), op=ALU.is_ge))
            V.tensor_tensor(out=fill_f[:, 1], in0=fill_f[:, 0], in1=counts[0:1, :], op=ALU.add)
            V.tensor_tensor(out=past[:, 1], in0=past[:, 0], in1=ntf[:].unsqueeze(2).to_broadcast([1, NE, TILES]), op=ALU.mult)
            chain(V.reduce_sum(exp_f[:], past[:, 0, 0:NE - 1].rearrange("p e t -> p t e"), axis=AX.X))
            V.tensor_copy(fill_i[:], fill_f[:, 1]).then_inc(fill_ready, 1)
            chain(V.reduce_sum(row_f[:, 0], past[:, 1, 0:NE - 1].rearrange("p e t -> p t e"), axis=AX.X))
            chain(V.tensor_tensor(out=row_f[:, 1], in0=tile_f[:], in1=row_f[:, 0], op=ALU.subtract))
            chain(V.tensor_scalar(out=row_f[:, 2], in0=exp_f[:], scalar1=float(CAP), scalar2=None, op0=ALU.mult))
            chain(V.scalar_tensor_tensor(out=row_f[:, 0], in0=row_f[:, 1], scalar=float(P), in1=row_f[:, 2], op0=ALU.mult, op1=ALU.add))
            chain(V.tensor_scalar(out=row_f[:, 1], in0=row_f[:, 0], scalar1=-1.0, scalar2=float(FILL_ROW), op0=ALU.mult, op1=ALU.add))
            chain(V.tensor_tensor(out=row_f[:, 2], in0=row_f[:, 1], in1=past[:, 0, NE - 1], op=ALU.mult))
            chain(V.tensor_tensor(out=row_f[:, 1], in0=row_f[:, 0], in1=row_f[:, 2], op=ALU.add))
            V.tensor_copy(row_tab[:], row_f[:, 1]).then_inc(tabs_ready, 1)
            V.tensor_copy(exp_tab[:], exp_f[:]).then_inc(tabs_ready, 1)
            for q in range(NQ):
                dve.wait_ge(xhi_done, q + 1)
                if q >= 2:
                    dve.wait_ge(h_psum, (q - 1) * NSH * HC)
                V.tensor_tensor(out=xt_lo[:, q % 2], in0=xt[:, q % 2], in1=xt_hi[:, q % 2].bitcast(F32), op=ALU.subtract).then_inc(xlo_done, 1)
                for s in range(NSH):
                    for c in range(HC):
                        n = (q * NSH + s) * HC + c
                        dve.wait_ge(g_done, n + 1)
                        dve.wait_ge(hhi_done, n + 1)
                        V.tensor_tensor(out=h_lo[:, s, c], in0=g[:, n % 2], in1=h_hi[:, s, c].bitcast(F32), op=ALU.subtract).then_inc(hlo_done, 1)
                for u in range(2):
                    t = 2 * q + u
                    dve.wait_ge(x1_in[u], 16 * (q + 1))
                    dve.wait_ge(y_psum, NSH * (q + 1))
                    if q >= 1:
                        dve.wait_ge(acc_out[u], 16 * q)
                    V.scalar_tensor_tensor(out=acc[:, u], in0=psY[:, (q % 2) * 2 + u, 0:D], scalar=1.0 / NSH, in1=x1[:, u],
                                           op0=ALU.mult, op1=ALU.add).then_inc(acc_done, 1)

        @block.tensor
        def _(pe):
            for q in range(NQ):
                for s in range(NSH):
                    if q == 0:
                        pe.wait_ge(lo_done, 2 * s + 2)
                    if s == 0:
                        pe.wait_ge(xlo_done, q + 1)
                    for c in range(HC):
                        n = (q * NSH + s) * HC + c
                        if n >= 4:
                            pe.wait_ge(hhi_done, n - 3)
                        k = 0
                        for ch in range(C):
                            w = slice(ch * HF + c, (ch + 1) * HF, HC)
                            for a, b in ((s_lo, xt_hi), (s_hi, xt_lo), (s_hi, xt_hi)):
                                last = nc.tensor.matmul(psH[:, n % 4, 0:HALF], a[:, s, w], b[:, q % 2, ch], start=(k == 0), stop=(k == 3 * C - 1))
                                k += 1
                        last.then_inc(h_psum, 1)
                for s in range(NSH):
                    pe.wait_ge(hlo_done, (q * NSH + s + 1) * HC)
                    if q >= 2 and s == 0:
                        pe.wait_ge(acc_done, 2 * (q - 1))
                    for u in range(2):
                        for c in range(HC):
                            w = slice(C * HF + c * D, C * HF + (c + 1) * D)
                            for k, (a, b) in enumerate(((h_hi, s_lo), (h_lo, s_hi), (h_hi, s_hi))):
                                last = nc.tensor.matmul(psY[:, (q % 2) * 2 + u, 0:D], a[:, s, c, u * P:(u + 1) * P], b[:, s, w],
                                                        start=(s == 0 and c == 0 and k == 0), stop=(s == NSH - 1 and c == HC - 1 and k == 2))
                    last.then_inc(y_psum, 1)


def routed_experts(nc, ios, keep, scratch, out):
    (b1, b2) = ios
    w_hi, w_lo, p12, row_tab, exp_tab, tabs_ready = keep
    xg_d, acc_d, y_d = scratch
    with ExitStack() as es:
        def sb(name, shape, dt=F32):
            return es.enter_context(nc.sbuf_tensor(name, shape, dt))

        def sem(name):
            return es.enter_context(nc.semaphore(name))

        b1T = sb("b1T", [P, NE, HC])
        b2_bc = sb("b2_bc", [P, NE, D])
        ident = sb("ident3", [P, P])
        NXB, NYB = 8, 4
        xg = sb("xg", [P, NXB, ROW])
        x_hi = sb("x_hi", [P, 2, C, P], F32R)
        x_lo = sb("x_lo", [P, 2, C, P], F32R)
        hpre = sb("hpre", [P, 2, HF])
        hb = sb("hb", [P, 2, HC, P])
        g = sb("g3", [P, 2, HC, P])
        h_hi = sb("hh_hi", [P, 2, HC, P], F32R)
        h_lo = sb("hh_lo", [P, 2, HC, P], F32R)
        y = sb("y", [P, NYB, D])
        yin = sb("yin", [P, 4, 2, D])
        ain = sb("ain", [P, 4, D])
        fin = sb("fin", [P, 4, D])
        ps = es.enter_context(nc.psum_tensor("ps3", [P, 8, 512], F32))

        xg_in = [sem(f"xg_in{i}") for i in range(NXB)]
        y_out = [sem(f"y_out{i}") for i in range(NXB)]
        cst, small = sem("cst3"), sem("small3")
        xt_psum, xhi_done, xlo_done = sem("xt_psum"), sem("xhi3"), sem("xlo3")
        hid_psum, hpre_done, ht_psum, hb_done = sem("hid_psum"), sem("hpre_done"), sem("ht_psum"), sem("hb_done")
        g_done, hhi_done, hlo_done, res_psum, y_done = sem("g3_done"), sem("hhi3"), sem("hlo3"), sem("res_psum"), sem("y_done")
        yin_in = [sem(f"yin_in{i}") for i in range(4)]
        half_done, fin_done = sem("half_done"), sem("fin_done")
        out_sem = [sem(f"out{i}") for i in range(4)]
        block = es.enter_context(nc.Block())

        @block.sync
        def _(sp):
            sp.wait_ge(tabs_ready, 2)
            for t in range(TILES):
                r = sp.value_load(row_tab[0:1, t:t + 1], min_val=0, max_val=FILL_ROW)
                if t >= NXB:
                    sp.wait_ge(y_out[t % NXB], 16 * (t // NXB))
                sp.dma_start(xg[:, t % NXB], xg_d[bass.ds(r, P), :]).then_inc(xg_in[t % NXB], 16)
            for i in range(NXB):
                sp.wait_ge(y_out[i], 16 * len(range(i, TILES, NXB)))
            for t in range(NT):
                if t >= 4:
                    sp.wait_ge(fin_done, t - 3)
                sp.dma_start(yin[:, t % 4], y_d[:, t * P:(t + 1) * P, :].rearrange("k p d -> p k d")).then_inc(yin_in[t % 4], 16)
                sp.dma_start(ain[:, t % 4], acc_d[t]).then_inc(yin_in[t % 4], 16)

        @block.gpsimd
        def _(pool):
            pool.memset(ident[:], 0.0).then_inc(cst, 1)
            pool.wait_ge(cst, 1)
            pool.affine_select(out=ident[:], in_=ident[:], compare_op=ALU.not_equal, fill=1.0, base=0,
                               pattern=[[-1, P]], channel_multiplier=1).then_inc(cst, 1)
            for t in range(TILES):
                pool.wait_ge(y_done, t + 1)
                pool.indirect_dma_start(y_d.rearrange("k n d -> (k n) d"),
                                        bass.IndirectOffsetOnAxis(ap=xg[:, t % NXB, D:D + 1].bitcast(U32), axis=0),
                                        y[:, t % NYB], None, bounds_check=2 * TOK - 1, oob_is_err=False).then_inc(y_out[t % NXB], 16)

        @block.scalar
        def _(act):
            nc.scalar.dma_start(b1T[:], b1.rearrange("e (p c) -> p e c", p=P)).then_inc(small, 16)
            nc.scalar.dma_start(b2_bc[:], b2.partition_broadcast(P)).then_inc(small, 16)
            for t in range(-1, TILES + 1):
                if t + 1 < TILES:
                    n = t + 1
                    act.wait_ge(xt_psum, n + 1)
                    if n >= 2:
                        act.wait_ge(hid_psum, n - 1)
                    nc.scalar.activation(x_hi[:, n % 2], ps[:, n % 2, 0:D].rearrange("p (c n) -> p c n", c=C), ACT.Copy).then_inc(xhi_done, 1)
                if 0 <= t < TILES:
                    act.wait_ge(hid_psum, t + 1)
                    if t >= 2:
                        act.wait_ge(ht_psum, t - 1)
                    nc.scalar.activation(hpre[:, t % 2], ps[:, 2 + t % 2], ACT.Copy).then_inc(hpre_done, 1)
                if 1 <= t:
                    n = t - 1
                    act.wait_ge(hb_done, n + 1)
                    if n >= 2:
                        act.wait_ge(hlo_done, n - 1)
                    nc.scalar.activation(g[:, n % 2], hb[:, n % 2], ACT.Gelu).then_inc(g_done, 1)
                    if n >= 2:
                        act.wait_ge(res_psum, n - 1)
                    nc.scalar.activation(h_hi[:, n % 2], hb[:, n % 2], ACT.Gelu).then_inc(hhi_done, 1)
            for t in range(NT):
                act.wait_ge(fin_done, t + 1)
                nc.scalar.dma_start(out[t], fin[:, t % 4]).then_inc(out_sem[t % 4], 16)
            for i in range(4):
                act.wait_ge(out_sem[i], 16 * NT // 4)

        @block.vector
        def _(dve):
            V = nc.vector
            dve.wait_ge(small, 32)
            dve.wait_ge(tabs_ready, 2)
            for t in range(-1, TILES + 2):
                if t + 1 < TILES:
                    n = t + 1
                    dve.wait_ge(xhi_done, n + 1)
                    V.tensor_tensor(out=x_lo[:, n % 2], in0=ps[:, n % 2, 0:D].rearrange("p (c n) -> p c n", c=C),
                                    in1=x_hi[:, n % 2].bitcast(F32), op=ALU.subtract).then_inc(xlo_done, 1)
                if 1 <= t <= TILES:
                    n = t - 1
                    e = dve.value_load(exp_tab[0:1, n:n + 1], min_val=0, max_val=NE - 1)
                    dve.wait_ge(ht_psum, n + 1)
                    if n >= 2:
                        dve.wait_ge(hhi_done, n - 1)
                    V.tensor_tensor(out=hb[:, n % 2], in0=ps[:, 4 + n % 2].rearrange("p (c n) -> p c n", c=HC),
                                    in1=b1T[:, bass.ds(e, 1), :].squeeze(1).unsqueeze(2).to_broadcast([P, HC, P]), op=ALU.add).then_inc(hb_done, 1)
                    dve.wait_ge(g_done, n + 1)
                    dve.wait_ge(hhi_done, n + 1)
                    V.tensor_tensor(out=h_lo[:, n % 2], in0=g[:, n % 2], in1=h_hi[:, n % 2].bitcast(F32), op=ALU.subtract).then_inc(hlo_done, 1)
                if 2 <= t:
                    n = t - 2
                    e = dve.value_load(exp_tab[0:1, n:n + 1], min_val=0, max_val=NE - 1)
                    dve.wait_ge(res_psum, n + 1)
                    if n >= NYB:
                        dve.wait_ge(y_out[(n - NYB) % NXB], 16 * ((n - NYB) // NXB + 1))
                    V.tensor_tensor(out=y[:, n % NYB], in0=ps[:, 6 + n % 2, 0:D], in1=b2_bc[:, bass.ds(e, 1), :].squeeze(1),
                                    op=ALU.add).then_inc(y_done, 1)
            for t in range(NT):
                dve.wait_ge(yin_in[t % 4], 32 * (t // 4 + 1))
                V.scalar_tensor_tensor(out=ain[:, t % 4], in0=yin[:, t % 4, 0], scalar=p12[:, 0, t:t + 1], in1=ain[:, t % 4],
                                       op0=ALU.mult, op1=ALU.add).then_inc(half_done, 1)
                dve.wait_ge(half_done, t + 1)
                if t >= 4:
                    dve.wait_ge(out_sem[t % 4], 16 * (t // 4))
                V.scalar_tensor_tensor(out=fin[:, t % 4], in0=yin[:, t % 4, 1], scalar=p12[:, 1, t:t + 1], in1=ain[:, t % 4],
                                       op0=ALU.mult, op1=ALU.add).then_inc(fin_done, 1)

        @block.tensor
        def _(pe):
            pe.wait_ge(cst, 2)
            pe.wait_ge(tabs_ready, 2)

            def x_transpose(n):
                pe.wait_ge(xg_in[n % NXB], 16 * (n // NXB + 1))
                if n >= 2:
                    pe.wait_ge(xlo_done, n - 1)
                for c in range(C):
                    last = nc.tensor.transpose(ps[:, n % 2, c * P:(c + 1) * P], xg[:, n % NXB, c * P:(c + 1) * P], ident[:])
                last.then_inc(xt_psum, 1)

            x_transpose(0)
            for t in range(TILES + 2):
                if t + 1 < TILES:
                    x_transpose(t + 1)
                if t < TILES:
                    e = pe.value_load(exp_tab[0:1, t:t + 1], min_val=0, max_val=NE - 1)
                    pe.wait_ge(xlo_done, t + 1)
                    if t >= 2:
                        pe.wait_ge(hpre_done, t - 1)
                    k = 0
                    for c in range(C):
                        for a, b in ((x_hi, w_lo), (x_lo, w_hi), (x_hi, w_hi)):
                            last = nc.tensor.matmul(ps[:, 2 + t % 2], a[:, t % 2, c], b[:, bass.ds(e, 1), c * HF:(c + 1) * HF].squeeze(1),
                                                    start=(k == 0), stop=(k == 3 * C - 1))
                            k += 1
                    last.then_inc(hid_psum, 1)
                if 1 <= t <= TILES:
                    n = t - 1
                    pe.wait_ge(hpre_done, n + 1)
                    if n >= 2:
                        pe.wait_ge(hb_done, n - 1)
                    for c in range(HC):
                        last = nc.tensor.transpose(ps[:, 4 + n % 2, c * P:(c + 1) * P], hpre[:, n % 2, c:HF:HC], ident[:])
                    last.then_inc(ht_psum, 1)
                if 2 <= t:
                    n = t - 2
                    e = pe.value_load(exp_tab[0:1, n:n + 1], min_val=0, max_val=NE - 1)
                    pe.wait_ge(hlo_done, n + 1)
                    if n >= 2:
                        pe.wait_ge(y_done, n - 1)
                    k = 0
                    for c in range(HC):
                        for a, b in ((h_hi, w_lo), (h_lo, w_hi), (h_hi, w_hi)):
                            last = nc.tensor.matmul(ps[:, 6 + n % 2, 0:D], a[:, n % 2, c],
                                                    b[:, bass.ds(e, 1), C * HF + c * D:C * HF + (c + 1) * D].squeeze(1),
                                                    start=(k == 0), stop=(k == 3 * HC - 1))
                            k += 1
                    last.then_inc(res_psum, 1)


def build(nc, a, out):
    x1_d = nc.dram_tensor("x1_d", [NT, P, D], F32, kind="Internal").ap()
    xt_d = nc.dram_tensor("xt_d", [P, C, TOK], F32, kind="Internal").ap()
    xg_d = nc.dram_tensor("xg_d", [XG_ROWS, ROW], F32, kind="Internal").ap()
    acc_d = nc.dram_tensor("acc_d", [NT, P, D], F32, kind="Internal").ap()
    y_d = nc.dram_tensor("y_d", [2, TOK, D], F32, kind="Internal").ap()
    with ExitStack() as es:
        def sb(name, shape, dt=F32):
            return es.enter_context(nc.sbuf_tensor(name, shape, dt))

        p12 = sb("p12", [P, 2, NT])
        counts = sb("counts", [P, NE])
        row_tab = sb("row_tab", [1, TILES], I32)
        exp_tab = sb("exp_tab", [1, TILES], I32)
        counts_ready = es.enter_context(nc.semaphore("counts_ready"))
        tabs_ready = es.enter_context(nc.semaphore("tabs_ready"))
        X, F = "L0_xattn_", "L0_ffn_"
        attention(nc, (a["x"], a["ctx_1024"], a[X + "Wv"], a[X + "Wk"], a[X + "Wq"], a[X + "Wo"], a[X + "bo"],
                       a[F + "router_w"], a[F + "router_b"], a[F + "sb2"]), (p12, counts, counts_ready), (x1_d, xt_d, xg_d))
        w_hi = sb("w_hi", [P, NE, WPE], F32R)
        w_lo = sb("w_lo", [P, NE, WPE], F32R)
        shared_experts(nc, (a[F + "w1"], a[F + "w2"], a[F + "sw1"], a[F + "sb1"], a[F + "sw2"]),
                       (w_hi, w_lo, counts, row_tab, exp_tab, tabs_ready), (x1_d, xt_d, xg_d, acc_d))
        routed_experts(nc, (a[F + "b1"], a[F + "b2"]), (w_hi, w_lo, p12, row_tab, exp_tab, tabs_ready), (xg_d, acc_d, y_d),
                       out.rearrange("b (t p) d -> (b t) p d", p=P))


INS = ["x", "ctx_1024", "L0_xattn_Wv", "L0_xattn_Wk", "L0_xattn_Wq", "L0_xattn_Wo", "L0_xattn_bo", "L0_ffn_router_w",
       "L0_ffn_router_b", "L0_ffn_w1", "L0_ffn_b1", "L0_ffn_w2", "L0_ffn_b2", "L0_ffn_sw1", "L0_ffn_sb1", "L0_ffn_sw2", "L0_ffn_sb2"]


def kernel(**inputs):
    import concourse.bacc as bacc
    from concourse.bass_utils import run_bass_kernel_spmd

    nc = bacc.Bacc("TRN2", target_bir_lowering=False, num_devices=1)
    arrays, aps = {}, {}
    for name in INS:
        a = np.ascontiguousarray(inputs[name])
        arrays[f"in_{name}"] = a
        aps[name] = nc.dram_tensor(f"in_{name}", a.shape, mybir.dt.from_np(a.dtype), kind="ExternalInput").ap()
    out = nc.dram_tensor("out", (B, S, D), F32, kind="ExternalOutput").ap()
    build(nc, aps, out)
    r = run_bass_kernel_spmd(nc, [arrays], core_ids=[0])
    return r.results[0]["out"]
```

```python
import numpy as np
import concourse.bass as bass
from concourse import mybir
from contextlib import ExitStack

F32 = mybir.dt.float32
F32R = mybir.dt.float32r
BF16 = mybir.dt.bfloat16
I32 = mybir.dt.int32
U32 = mybir.dt.uint32
ALU = mybir.AluOpType
ACT = mybir.ActivationFunctionType
AX = mybir.AxisListType

P = 128
B, S, D = 4, 512, 256
TOK = B * S
NT = TOK // P
TPB = S // P
L = 64
NH, HD = 16, 16
C = D // P
HPC = P // HD
NJ = NH // 2
NE, NSH, HF = 8, 2, 512
HC = HF // P
EPS = 1e-5
LAST = 8
HALF = 256
NQ = TOK // HALF
QA = 4
WPE = C * HF + HC * D
ROW = D + 4
CAP = TOK + P
FILL_ROW = NE * CAP
XG_ROWS = FILL_ROW + P
TILES = (2 * TOK + NE * (P - 1)) // P
SKIP = 2 * TOK + 4096


class SharedExperts:

    def __init__(self, nc, es, ios):
        self.nc = nc
        self.w1, self.w2, self.sw1, self.sb1, self.sw2 = ios

        def sb(name, shape, dt=F32):
            return es.enter_context(nc.sbuf_tensor(name, shape, dt, side="right"))

        def sem(name):
            return es.enter_context(nc.semaphore(name))

        self.s_hi = sb("s_hi", [P, NSH, WPE], F32R)
        self.s_lo = sb("s_lo", [P, NSH, WPE], F32R)
        self.raw = sb("raw", [P, 2, WPE // 2])
        self.xt_hi = sb("xt_hi", [P, 2, C, HALF], F32R)
        self.xt_lo = sb("xt_lo", [P, 2, C, HALF], F32R)
        self.g = sb("g", [P, 2, HALF])
        self.h_hi = sb("h_hi", [P, NSH, HC, HALF], F32R)
        self.h_lo = sb("h_lo", [P, NSH, HC, HALF], F32R)
        self.sb1T = sb("sb1T", [P, NSH, HC])
        self.raw_in = [sem(f"raw_in{i}") for i in range(2)]
        self.hi_done, self.lo_done = sem("hi_done"), sem("lo_done")
        self.xhi_done, self.xlo_done = sem("xhi_done"), sem("xlo_done")
        self.b1_in, self.h_psum, self.g_done, self.hhi_done = sem("b1_in"), sem("h_psum"), sem("g_done"), sem("hhi_done")
        self.hlo_done, self.y_psum, self.acc_done = sem("hlo_done"), sem("y_psum"), sem("acc_done")

    def piece_source(self, n):
        e, second = n // 2, n % 2
        if e < NSH:
            w = (self.sw2 if second else self.sw1)[e]
        else:
            w = (self.w2 if second else self.w1)[e - NSH]
        return w.rearrange("(p c) n -> p c n", p=P) if second else w.rearrange("(c p) n -> p c n", p=P)

    def load_piece(self, sp, n):
        if n >= 2:
            sp.wait_ge(self.lo_done, n - 1)
        w = self.piece_source(n)
        sp.dma_start(self.raw[:, n % 2].rearrange("p (c n) -> p c n", c=w.shape[1]), w).then_inc(self.raw_in[n % 2], 16)

    def split_high(self, act, n, target):
        act.wait_ge(self.raw_in[n % 2], 16 * (n // 2 + 1))
        self.nc.scalar.activation(target, self.raw[:, n % 2], ACT.Copy).then_inc(self.hi_done, 1)

    def split_low(self, pool, n, high, target):
        pool.wait_ge(self.hi_done, n + 1)
        pool.tensor_tensor(out=target, in0=self.raw[:, n % 2], in1=high.bitcast(F32), op=ALU.subtract).then_inc(self.lo_done, 1)

    def scalar_x(self, act, q, src):
        if q >= 2:
            act.wait_ge(self.h_psum, (q - 1) * NSH * HC)
        self.nc.scalar.activation(self.xt_hi[:, q % 2], src, ACT.Copy).then_inc(self.xhi_done, 1)

    def vector_x(self, dve, q, src):
        dve.wait_ge(self.xhi_done, q + 1)
        if q >= 2:
            dve.wait_ge(self.h_psum, (q - 1) * NSH * HC)
        self.nc.vector.tensor_tensor(out=self.xt_lo[:, q % 2], in0=src, in1=self.xt_hi[:, q % 2].bitcast(F32),
                                     op=ALU.subtract).then_inc(self.xlo_done, 1)

    def tensor_hidden(self, pe, q, banks):
        for s in range(NSH):
            if q == 0:
                pe.wait_ge(self.lo_done, 2 * s + 2)
            if s == 0:
                pe.wait_ge(self.xlo_done, q + 1)
            for c in range(HC):
                n = (q * NSH + s) * HC + c
                if n >= len(banks):
                    pe.wait_ge(self.hhi_done, n - len(banks) + 1)
                k = 0
                for ch in range(C):
                    w = slice(ch * HF + c, (ch + 1) * HF, HC)
                    for a, b in ((self.s_lo, self.xt_hi), (self.s_hi, self.xt_lo), (self.s_hi, self.xt_hi)):
                        last = self.nc.tensor.matmul(banks[n % len(banks)], a[:, s, w], b[:, q % 2, ch], start=(k == 0), stop=(k == 3 * C - 1))
                        k += 1
                last.then_inc(self.h_psum, 1)

    def scalar_hidden(self, act, q, s, banks):
        for c in range(HC):
            n = (q * NSH + s) * HC + c
            act.wait_ge(self.h_psum, n + 1)
            if n >= 2:
                act.wait_ge(self.hlo_done, n - 1)
            if q >= 1 and c == 0:
                act.wait_ge(self.y_psum, NSH * (q - 1) + s + 1)
            self.nc.scalar.activation(self.g[:, n % 2], banks[n % len(banks)], ACT.Gelu, bias=self.sb1T[:, s, c:c + 1]).then_inc(self.g_done, 1)
            self.nc.scalar.activation(self.h_hi[:, s, c], banks[n % len(banks)], ACT.Gelu, bias=self.sb1T[:, s, c:c + 1]).then_inc(self.hhi_done, 1)

    def vector_hidden(self, dve, q, s):
        for c in range(HC):
            n = (q * NSH + s) * HC + c
            dve.wait_ge(self.g_done, n + 1)
            dve.wait_ge(self.hhi_done, n + 1)
            self.nc.vector.tensor_tensor(out=self.h_lo[:, s, c], in0=self.g[:, n % 2], in1=self.h_hi[:, s, c].bitcast(F32),
                                         op=ALU.subtract).then_inc(self.hlo_done, 1)

    def tensor_output(self, pe, q, banks):
        for s in range(NSH):
            pe.wait_ge(self.hlo_done, (q * NSH + s + 1) * HC)
            if q >= len(banks) and s == 0:
                pe.wait_ge(self.acc_done, 2 * (q - len(banks) + 1))
            for u in range(2):
                for c in range(HC):
                    w = slice(C * HF + c * D, C * HF + (c + 1) * D)
                    for k, (a, b) in enumerate(((self.h_hi, self.s_lo), (self.h_lo, self.s_hi), (self.h_hi, self.s_hi))):
                        last = self.nc.tensor.matmul(banks[q % len(banks)][u], a[:, s, c, u * P:(u + 1) * P], b[:, s, w],
                                                     start=(s == 0 and c == 0 and k == 0), stop=(s == NSH - 1 and c == HC - 1 and k == 2))
            last.then_inc(self.y_psum, 1)

    def vector_output(self, dve, q, banks, x1, out):
        dve.wait_ge(self.y_psum, NSH * (q + 1))
        for u in range(2):
            self.nc.vector.scalar_tensor_tensor(out=out[u], in0=banks[q % len(banks)][u], scalar=1.0 / NSH, in1=x1[u],
                                                op0=ALU.mult, op1=ALU.add).then_inc(self.acc_done, 1)


def x_step(q):
    return NT - 4 + q if q < 2 else NT + 2 * (q - 2) + 1


def attention(nc, ios, keep, scratch, shared):
    (x, ctx, Wv, Wk, Wq, Wo, bo, rw, rb, sb2) = ios
    gap, counts, metas = keep
    x1_d, xt_d, xg_d, acc_d = scratch
    with ExitStack() as es:
        def sb(name, shape, dt=F32):
            return es.enter_context(nc.sbuf_tensor(name, shape, dt))

        def sem(name):
            return es.enter_context(nc.semaphore(name))

        xres = sb("xres", [P, NT, D])
        wraw = sb("wraw", [P, 4, C, D])
        craw = sb("craw", [P, C, D])
        WT = sb("WT", [P, 4, C, D])
        ctxT = sb("ctxT", [P, C, B * L])
        ctxT2 = sb("ctxT2", [P, C, B, 2, L])
        KT = sb("KT", [P, C, B, L])
        Vsb = sb("Vsb", [P, B, D])
        Kbd = sb("Kbd", [P, 2, C, HPC, L])
        Vbd = sb("Vbd", [P, 2, NJ, P])
        maskK = sb("maskK", [P, HPC])
        maskV = sb("maskV", [P, 4, HPC])
        ident = sb("ident", [P, P])
        tri = sb("tri", [P, P], BF16)
        ones = sb("ones", [P, P], BF16)
        bo_bc = sb("bo_bc", [P, D])
        rb_bc = sb("rb_bc", [P, NE])
        sb2_bc = sb("sb2_bc", [P, NSH, D])
        sbh = sb("sbh", [P, D])
        rws = sb("rws", [P, C, NE])
        iota8 = sb("iota8", [P, NE])
        ebase = sb("ebase", [P, NE])
        ids = sb("ids", [P, 2, NT], I32)
        half = sb("half", [P, 1])
        st1 = sb("st1", [P, NT, 6])
        mv1 = sb("mv1", [P, NT, 2])
        ve1 = sb("ve1", [P, NT])
        rs1 = sb("rs1", [P, NT])
        st2 = sb("st2", [P, NT, 6])
        mv2 = sb("mv2", [P, NT, 2])
        ve2 = sb("ve2", [P, NT])
        rs2 = sb("rs2", [P, NT])
        xn = sb("xn", [P, 2, D])
        xnT = sb("xnT", [P, 2, C, P])
        QT = sb("QT", [P, 2, C, P])
        mx = sb("mx", [P, 2, NH])
        sm = sb("sm", [P, 2, NH])
        inv = sb("inv", [P, 2, NH])
        Pr = sb("Pr", [P, 3, NH, L])
        PT = sb("PT", [P, 2, NJ, P])
        OT = sb("OT", [P, 2, C, P])
        x1 = sb("x1", [P, 2, D])
        rows = sb("rows", [P, 2, 2, TPB, ROW])
        x2T = sb("x2T", [P, C, TOK])
        gates = sb("gates", [P, 2, TPB, NE])
        top = sb("top", [P, TPB, 8])
        topi = sb("topi", [P, TPB, 8], U32)
        topf = sb("topf", [P, 2, TPB])
        oh = sb("oh", [P, 2, TPB, NE])
        ohs = sb("ohs", [P, NT, NE], BF16)
        ohc = sb("ohc", [P, TPB + 1, NE], BF16)
        rk = sb("rk", [P, TPB, NE])
        pk = sb("pk", [P, 2, TPB, NE])
        slotf = sb("slotf", [P, 2, TPB])
        slots = sb("slots", [P, 2, 2, TPB], I32)
        filler = sb("filler", [P, ROW])
        psS = es.enter_context(nc.psum_tensor("psS", [P, 2, C, 512], F32))
        psP = es.enter_context(nc.psum_tensor("psP", [P, NJ, P], F32))
        psA = es.enter_context(nc.psum_tensor("psA", [P, 512], F32))
        psD = es.enter_context(nc.psum_tensor("psD", [P, 512], F32))
        psW = psS[:, :, :, :].rearrange("p a c n -> p (a c) n")
        h_banks = [psS[:, 0, i, 0:HALF] for i in range(2)]
        y_banks = [[psS[:, 1, u, 0:D] for u in range(2)]]

        ld_w, ld_c, ld_small = sem("ld_w"), sem("ld_c"), sem("ld_small")
        ld_x = [sem(f"ld_x{b}") for b in range(B)]
        consts, fillers = sem("consts"), sem("fillers")
        wt_psum, wt_sb = sem("wt_psum"), sem("wt_sb")
        ctxt_psum, ctxt_sb = sem("ctxt_psum"), sem("ctxt_sb")
        kv_psum, kv_sb = sem("kv_psum"), sem("kv_sb")
        kbd_ready, vbd_ready = sem("kbd_ready"), sem("vbd_ready")
        st1_done, mv1_done, ve1_done, rs1_done, xn_done = sem("st1_done"), sem("mv1_done"), sem("ve1_done"), sem("rs1_done"), sem("xn_done")
        xnt_psum, xnt_sb, qt_psum, qt_sb = sem("xnt_psum"), sem("xnt_sb"), sem("qt_psum"), sem("qt_sb")
        scores_done, max_done, shift_done, exp_done = sem("scores_done"), sem("max_done"), sem("shift_done"), sem("exp_done")
        sum_done, inv_done, probs_done = sem("sum_done"), sem("inv_done"), sem("probs_done")
        pt_psum, pt_sb, ot_psum, ot_sb = sem("pt_psum"), sem("pt_sb"), sem("ot_psum"), sem("ot_sb")
        att_psum, x1_done, x1s_done, x1_stored = sem("att_psum"), sem("x1_done"), sem("x1s_done"), sem("x1_stored")
        xbo_done, sbh_done, small_done = sem("xbo_done"), sem("sbh_done"), sem("small_done")
        st2_done, mv2_done, ve2_done, rs2_done, rows_done = sem("st2_done"), sem("mv2_done"), sem("ve2_done"), sem("rs2_done"), sem("rows_done")
        x2t_psum, x2t_sb, x2t_stored = sem("x2t_psum"), sem("x2t_sb"), sem("x2t_stored")
        gates_psum, gates_sb, gates_done = sem("gates_psum"), sem("gates_sb"), sem("gates_done")
        acc_stored = sem("acc_stored")
        ids_done = sem("ids_done")
        route, ohs_ready, ranks_psum = sem("route"), sem("ohs_ready"), sem("ranks_psum")
        ranks_read, slots_ready, scattered, total_psum = sem("ranks_read"), sem("slots_ready"), [sem(f"scattered{i}") for i in range(2)], sem("total_psum")
        block = es.enter_context(nc.Block())

        @block.sync
        def _(sp):
            for m, w in enumerate((Wq, Wk, Wv, Wo)):
                sp.dma_start(wraw[:, m], w.rearrange("(c p) e -> p c e", p=P)).then_inc(ld_w, 16)
            for b in range(B):
                sp.dma_start(xres[:, b * TPB:(b + 1) * TPB], x[b].rearrange("(t p) d -> p t d", p=P)).then_inc(ld_x[b], 16)
            sp.dma_start(shared.sb1T[:], shared.sb1.rearrange("s (p c) -> p s c", p=P)).then_inc(shared.b1_in, 16)
            for n in range(2 * NSH + 2):
                shared.load_piece(sp, n)
            for g in range(2 * QA, NT):
                sp.wait_ge(x1s_done, g + 1)
                sp.dma_start(x1_d[g], xres[:, g]).then_inc(x1_stored, 16)
                sp.wait_ge(x2t_sb, g + 1)
                sp.dma_start(xt_d[:, :, g * P:(g + 1) * P], x2T[:, :, g * P:(g + 1) * P]).then_inc(x2t_stored, 16)
            for g in range(2 * QA):
                sp.wait_ge(shared.acc_done, g + 1)
                sp.dma_start(acc_d[g], xres[:, g]).then_inc(acc_stored, 16)
            sp.wait_ge(x1_stored, 16 * (NT - 2 * QA))
            sp.wait_ge(x2t_stored, 16 * (NT - 2 * QA))
            sp.wait_ge(acc_stored, 16 * 2 * QA)

        @block.gpsimd
        def _(pool):
            pool.memset(ident[:], 0.0).then_inc(consts, 1)
            pool.memset(maskK[:], 1.0).then_inc(consts, 1)
            pool.memset(maskV[:], 1.0).then_inc(consts, 1)
            pool.memset(tri[:], 1.0).then_inc(consts, 1)
            pool.memset(ones[:], 1.0).then_inc(consts, 1)
            pool.memset(half[:], -0.5).then_inc(consts, 1)
            pool.memset(filler[:], 0.0).then_inc(consts, 1)
            pool.memset(rows[:, :, :, :, D:ROW], 0.0).then_inc(consts, 1)
            pool.wait_ge(consts, 8)
            pool.affine_select(out=ident[:], in_=ident[:], compare_op=ALU.not_equal, fill=1.0, base=0,
                               pattern=[[-1, P]], channel_multiplier=1).then_inc(consts, 1)
            pool.affine_select(out=tri[:], in_=tri[:], compare_op=ALU.is_ge, fill=0.0, base=-1,
                               pattern=[[1, P]], channel_multiplier=-1).then_inc(consts, 1)
            pool.affine_select(out=maskK[:], in_=maskK[:], compare_op=ALU.is_ge, fill=0.0, base=0,
                               pattern=[[-HD, HPC]], channel_multiplier=1).then_inc(consts, 1)
            pool.affine_select(out=maskV[:], in_=maskV[:], compare_op=ALU.is_ge, fill=0.0, base=0,
                               pattern=[[2 * L, 4], [-L, HPC]], channel_multiplier=1).then_inc(consts, 1)
            pool.iota(iota8[:], pattern=[[1, NE]], base=0, channel_multiplier=0,
                      allow_small_or_imprecise_dtypes=True).then_inc(consts, 1)
            pool.iota(ebase[:], pattern=[[CAP, NE]], base=0, channel_multiplier=0,
                      allow_small_or_imprecise_dtypes=True).then_inc(consts, 1)
            pool.iota(ids[:, 0, :], pattern=[[P, NT]], base=0, channel_multiplier=1).then_inc(consts, 1)
            pool.iota(ids[:, 1, :], pattern=[[P, NT]], base=TOK, channel_multiplier=1).then_inc(consts, 1)
            pool.iota(filler[:, D:D + 1].bitcast(I32), pattern=[[0, 1]], base=SKIP, channel_multiplier=1).then_inc(consts, 1)
            pool.wait_ge(consts, 17)
            pool.affine_select(out=maskK[:], in_=maskK[:], compare_op=ALU.is_ge, fill=0.0, base=HD - 1,
                               pattern=[[HD, HPC]], channel_multiplier=-1).then_inc(consts, 1)
            pool.affine_select(out=maskV[:], in_=maskV[:], compare_op=ALU.is_ge, fill=0.0, base=L - 1,
                               pattern=[[-2 * L, 4], [L, HPC]], channel_multiplier=-1).then_inc(consts, 1)
            pool.dma_start(xg_d[FILL_ROW:FILL_ROW + P, :], filler[:]).then_inc(fillers, 16)
            pool.wait_ge(ld_small, 16 * 4)
            pool.tensor_tensor(out=sbh[:], in0=sb2_bc[:, 0], in1=sb2_bc[:, 1], op=ALU.add).then_inc(small_done, 1)
            pool.wait_ge(small_done, 1)
            pool.tensor_scalar(out=sbh[:], in0=sbh[:], scalar1=1.0 / NSH, scalar2=None, op0=ALU.mult).then_inc(small_done, 1)
            pool.wait_ge(small_done, 2)

            def k_diagonal(b):
                if b == 0:
                    pool.wait_ge(kv_sb, C)
                    pool.wait_ge(consts, 19)
                if b >= 2:
                    pool.wait_ge(scores_done, TPB * (b - 1))
                for c in range(C):
                    pool.tensor_tensor(out=Kbd[:, b % 2, c], in0=KT[:, c, b].unsqueeze(1).to_broadcast([P, HPC, L]),
                                       in1=maskK[:].unsqueeze(2).to_broadcast([P, HPC, L]), op=ALU.mult).then_inc(kbd_ready, 1)

            k_diagonal(0)

            def rstd1(g):
                pool.wait_ge(ve1_done, g + 1)
                pool.tensor_tensor(out=rs1[:, g:g + 1], in0=ve1[:, g:g + 1], in1=half[:], op=ALU.pow).then_inc(rs1_done, 1)

            for g in range(TPB):
                rstd1(g)
            for s in range(NT + LAST):
                if 5 <= s < NT + 5:
                    g = s - 5
                    pool.wait_ge(ve2_done, g + 1)
                    pool.tensor_tensor(out=rs2[:, g:g + 1], in0=ve2[:, g:g + 1], in1=half[:], op=ALU.pow).then_inc(rs2_done, 1)
                if 1 <= s and s + TPB - 1 < NT:
                    rstd1(s + TPB - 1)
                if 1 <= s <= NT:
                    g = s - 1
                    pool.wait_ge(inv_done, g + 1)
                    pool.tensor_tensor(out=Pr[:, g % 3], in0=Pr[:, g % 3], in1=inv[:, g % 2].unsqueeze(2).to_broadcast([P, NH, L]),
                                       op=ALU.mult).then_inc(probs_done, 1)
                if s % TPB == 1 and s // TPB + 1 < B:
                    k_diagonal(s // TPB + 1)
                if 5 <= s < NT + 5:
                    g = s - 5
                    pool.tensor_tensor(out=xres[:, g], in0=x1[:, g % 2], in1=sbh[:], op=ALU.add).then_inc(x1s_done, 1)
                if TPB <= s < TPB + 2 * NSH:
                    n = s - TPB
                    e, w = n // 2, slice(n % 2 * (WPE // 2), (n % 2 + 1) * (WPE // 2))
                    shared.split_low(pool, n, shared.s_hi[:, e, w], shared.s_lo[:, e, w])
                if s >= 7 + 3 and (s - 7) % TPB == 3:
                    b = (s - 7) // TPB
                    if b >= 2:
                        pool.wait_ge(scattered[b % 2], 16 * 2 * TPB * (b // 2))
                    pool.tensor_copy(rows[:, b % 2, :, :, D].bitcast(I32), ids[:, :, b * TPB:(b + 1) * TPB]).then_inc(ids_done, 1)
                    pool.wait_ge(ids_done, b + 1)
                    pool.wait_ge(slots_ready, b + 1)
                    for t in range(TPB):
                        for k in range(2):
                            pool.indirect_dma_start(xg_d, bass.IndirectOffsetOnAxis(ap=slots[:, b % 2, k, t:t + 1], axis=0),
                                                    rows[:, b % 2, k, t, :], None).then_inc(scattered[b % 2], 16)
            for parity in range(2):
                pool.wait_ge(scattered[parity], 16 * NT)
            pool.wait_ge(fillers, 16)

        @block.scalar
        def _(act):
            nc.scalar.dma_start(craw[:], ctx.rearrange("(r b) k e -> (b k) r e", b=2)).then_inc(ld_c, 16)
            nc.scalar.dma_start(bo_bc[:], bo.partition_broadcast(P)).then_inc(ld_small, 16)
            nc.scalar.dma_start(rb_bc[:], rb.partition_broadcast(P)).then_inc(ld_small, 16)
            nc.scalar.dma_start(sb2_bc[:], sb2.partition_broadcast(P)).then_inc(ld_small, 16)
            nc.scalar.dma_start(rws[:], rw.rearrange("(c p) e -> p c e", p=P)).then_inc(ld_small, 16)
            for m in range(4):
                act.wait_ge(wt_psum, m + 1)
                nc.scalar.activation(WT[:, m], psW[:, m].rearrange("p (c f) -> p c f", c=C), ACT.Copy).then_inc(wt_sb, 1)
            act.wait_ge(ctxt_psum, 1)
            nc.scalar.activation(ctxT[:], psA[:, :].rearrange("p (c n) -> p c n", c=C), ACT.Copy).then_inc(ctxt_sb, 1)
            for c in range(C):
                nc.scalar.activation(ctxT2[:, c], psA[:, c * 256:(c + 1) * 256].rearrange("p (b k) -> p b k", b=B).unsqueeze(2).to_broadcast([P, B, 2, L]),
                                     ACT.Copy).then_inc(ctxt_sb, 1)
            act.wait_ge(kv_psum, 1)
            nc.scalar.activation(KT[:, 0], psP[:, 0:2].rearrange("p a (b k) -> p (a b) k", k=L), ACT.Copy, scale=float(HD) ** -0.5).then_inc(kv_sb, 1)
            nc.scalar.activation(KT[:, 1], psP[:, 4:6].rearrange("p a (b k) -> p (a b) k", k=L), ACT.Copy, scale=float(HD) ** -0.5).then_inc(kv_sb, 1)
            act.wait_ge(kv_psum, 2)
            nc.scalar.activation(Vsb[:], psW[:, :, 0:D], ACT.Copy).then_inc(kv_sb, 1)

            def xnt_evac(g):
                act.wait_ge(xnt_psum, g + 1)
                if g >= 2:
                    act.wait_ge(qt_psum, g - 1)
                nc.scalar.activation(xnT[:, g % 2], psA[:, 0:D].rearrange("p (c n) -> p c n", c=C), ACT.Copy).then_inc(xnt_sb, 1)

            def qt_evac(g):
                act.wait_ge(qt_psum, g + 1)
                if g >= 2:
                    act.wait_ge(scores_done, g - 1)
                nc.scalar.activation(QT[:, g % 2], psA[:, D:2 * D].rearrange("p (c n) -> p c n", c=C), ACT.Copy).then_inc(qt_sb, 1)

            xnt_evac(0)
            qt_evac(0)
            for s in range(NT + LAST):
                if s + 1 < NT:
                    xnt_evac(s + 1)
                if 6 <= s < NT + 6:
                    g = s - 6
                    act.wait_ge(gates_psum, g + 1)
                    if g >= TPB:
                        act.wait_ge(gates_done, g // TPB)
                    nc.scalar.activation(gates[:, 0, g % TPB], psA[:, D:D + NE], ACT.Copy).then_inc(gates_sb, 1)
                if s + 1 < NT:
                    qt_evac(s + 1)
                if 2 <= s < NT + 2:
                    g = s - 2
                    act.wait_ge(pt_psum, g + 1)
                    if g >= 2:
                        act.wait_ge(ot_psum, g - 1)
                    nc.scalar.activation(PT[:, g % 2], psP[:], ACT.Copy).then_inc(pt_sb, 1)
                if s < NT:
                    act.wait_ge(shift_done, s + 1)
                    nc.scalar.activation(Pr[:, s % 3], Pr[:, s % 3], ACT.Exp).then_inc(exp_done, 1)
                if 3 <= s < NT + 3:
                    g = s - 3
                    act.wait_ge(ot_psum, g + 1)
                    if g >= 2:
                        act.wait_ge(att_psum, g - 1)
                    nc.scalar.activation(OT[:, g % 2], psA[:, D:2 * D].rearrange("p (c n) -> p c n", c=C), ACT.Copy).then_inc(ot_sb, 1)
                if 5 <= s < NT + 5:
                    g = s - 5
                    act.wait_ge(x2t_psum, g + 1)
                    nc.scalar.activation(x2T[:, :, g * P:(g + 1) * P], psA[:, 0:D].rearrange("p (c n) -> p c n", c=C), ACT.Copy).then_inc(x2t_sb, 1)
                if TPB <= s < TPB + 2 * NSH:
                    n = s - TPB
                    shared.split_high(act, n, shared.s_hi[:, n // 2, n % 2 * (WPE // 2):(n % 2 + 1) * (WPE // 2)])
                for q in range(QA):
                    if s == x_step(q):
                        act.wait_ge(x2t_sb, 2 * q + 2)
                        shared.scalar_x(act, q, x2T[:, :, q * HALF:(q + 1) * HALF])
                if s >= NT and (s - NT) % 2 == 0 and (s - NT) // 2 < QA:
                    if s == NT:
                        act.wait_ge(shared.b1_in, 16)
                    for e in range(NSH):
                        shared.scalar_hidden(act, (s - NT) // 2, e, h_banks)

        @block.vector
        def _(dve):
            dve.wait_ge(ld_small, 16 * 4)

            def stats(g):
                b = g // TPB
                if g % TPB == 0:
                    dve.wait_ge(ld_x[b], 16)
                nc.vector.bn_stats(st1[:, g], xres[:, g]).then_inc(st1_done, 1)

            def norm1(g):
                dve.wait_ge(rs1_done, g + 1)
                if g >= 2:
                    dve.wait_ge(xnt_psum, g - 1)
                nc.vector.tensor_scalar(out=xn[:, g % 2], in0=xres[:, g], scalar1=mv1[:, g, 0:1], scalar2=rs1[:, g:g + 1],
                                        op0=ALU.subtract, op1=ALU.mult).then_inc(xn_done, 1)

            def aggregate(g):
                dve.wait_ge(st1_done, g + 1)
                nc.vector.bn_aggr(mv1[:, g], st1[:, g]).then_inc(mv1_done, 1)
                dve.wait_ge(mv1_done, g + 1)
                nc.vector.tensor_scalar(out=ve1[:, g:g + 1], in0=mv1[:, g, 1:2], scalar1=EPS, scalar2=None, op0=ALU.add).then_inc(ve1_done, 1)

            for g in range(TPB + 1):
                stats(g)
            for g in range(TPB):
                aggregate(g)
            norm1(0)
            norm1(1)

            def v_diagonal(b):
                if b == 0:
                    dve.wait_ge(kv_sb, C + 1)
                    dve.wait_ge(consts, 19)
                if b >= 2:
                    dve.wait_ge(ot_psum, TPB * (b - 1))
                for c in range(C):
                    nc.vector.tensor_tensor(out=Vbd[:, b % 2, 4 * c:4 * c + 4].rearrange("p j (h d) -> p j h d", d=HD),
                                            in0=Vsb[:, b, c * P:(c + 1) * P].rearrange("p (h d) -> p h d", d=HD).unsqueeze(1).to_broadcast([P, 4, HPC, HD]),
                                            in1=maskV[:].unsqueeze(3).to_broadcast([P, 4, HPC, HD]), op=ALU.mult).then_inc(vbd_ready, 1)

            v_diagonal(0)
            routed = [0]

            def chain(ins):
                routed[0] += 1
                ins.then_inc(route, 1)
                dve.wait_ge(route, routed[0])

            chain(nc.vector.memset(ohc[:, 0], 0.0))

            def choose(b):
                dve.wait_ge(gates_sb, TPB * (b + 1))
                nc.vector.tensor_tensor(out=gates[:, 1], in0=gates[:, 0], in1=rb_bc[:].unsqueeze(1).to_broadcast([P, TPB, NE]),
                                        op=ALU.add).then_inc(gates_done, 1)
                dve.wait_ge(gates_done, b + 1)
                for t in range(TPB):
                    ins = nc.vector.max(out=top[:, t], in_=gates[:, 1, t])
                chain(ins)
                for t in range(TPB):
                    ins = nc.vector.max_index(out=topi[:, t], in_max=top[:, t], in_values=gates[:, 1, t])
                chain(ins)
                nc.vector.tensor_tensor(out=gap[:, b * TPB:(b + 1) * TPB], in0=top[:, :, 1], in1=top[:, :, 0], op=ALU.subtract).then_inc(metas, 1)
                chain(nc.vector.tensor_copy(topf[:].rearrange("p k t -> p t k"), topi[:, :, 0:2]))
                for k in range(2):
                    ins = nc.vector.tensor_tensor(out=oh[:, k], in0=iota8[:].unsqueeze(1).to_broadcast([P, TPB, NE]),
                                                  in1=topf[:, k].unsqueeze(2).to_broadcast([P, TPB, NE]), op=ALU.is_equal)
                chain(ins)
                chain(nc.vector.tensor_tensor(out=ohs[:, b * TPB:(b + 1) * TPB], in0=oh[:, 0], in1=oh[:, 1], op=ALU.add))
                for t in range(TPB):
                    ins = nc.vector.tensor_tensor(out=ohc[:, t + 1], in0=ohc[:, t], in1=ohs[:, b * TPB + t], op=ALU.add)
                    if t < TPB - 1:
                        chain(ins)
                ins.then_inc(ohs_ready, 1)

            def place(b):
                dve.wait_ge(ranks_psum, b + 1)
                nc.vector.tensor_tensor(out=rk[:], in0=psD[:, 384:384 + TPB * NE].rearrange("p (t e) -> p t e", e=NE),
                                        in1=ebase[:].unsqueeze(1).to_broadcast([P, TPB, NE]), op=ALU.add).then_inc(ranks_read, 1)
                dve.wait_ge(ranks_read, b + 1)
                for k in range(2):
                    ins = nc.vector.tensor_tensor(out=pk[:, k], in0=oh[:, k], in1=rk[:], op=ALU.mult)
                chain(ins)
                chain(nc.vector.reduce_sum(slotf[:], pk[:], axis=AX.X))
                if b >= 2:
                    dve.wait_ge(scattered[b % 2], 16 * 2 * TPB * (b // 2))
                nc.vector.tensor_copy(slots[:, b % 2], slotf[:]).then_inc(slots_ready, 1)
                if b + 1 < B:
                    chain(nc.vector.tensor_copy(ohc[:, 0], ohc[:, TPB]))

            for s in range(NT + LAST):
                if s < NT:
                    dve.wait_ge(scores_done, s + 1)
                    v = psS[:, s % 2].rearrange("p c (h k) -> p (c h) k", k=L)
                    nc.vector.reduce_max(mx[:, s % 2], v, axis=AX.X).then_inc(max_done, 1)
                if 4 <= s < NT + 4:
                    g = s - 4
                    dve.wait_ge(att_psum, g + 1)
                    dve.wait_ge(xbo_done, g + 1)
                    if g >= 2:
                        dve.wait_ge(x1s_done, g - 1)
                    nc.vector.tensor_tensor(out=x1[:, g % 2], in0=psD[:, 0:D], in1=xres[:, g], op=ALU.add).then_inc(x1_done, 1)
                if s < NT:
                    if s >= 3:
                        dve.wait_ge(pt_psum, s - 2)
                    dve.wait_ge(max_done, s + 1)
                    nc.vector.tensor_tensor(out=Pr[:, s % 3], in0=v, in1=mx[:, s % 2].unsqueeze(2).to_broadcast([P, NH, L]),
                                            op=ALU.subtract).then_inc(shift_done, 1)
                if s + 2 < NT:
                    norm1(s + 2)
                if 5 <= s < NT + 5:
                    g = s - 5
                    b, t = g // TPB, g % TPB
                    dve.wait_ge(rs2_done, g + 1)
                    if b >= 2 and t == 0:
                        dve.wait_ge(scattered[b % 2], 16 * 2 * TPB * (b // 2))
                    for k in range(2):
                        nc.vector.tensor_scalar(out=rows[:, b % 2, k, t, 0:D], in0=x1[:, g % 2], scalar1=mv2[:, g, 0:1],
                                                scalar2=rs2[:, g:g + 1], op0=ALU.subtract, op1=ALU.mult).then_inc(rows_done, 1)
                if s < NT:
                    nc.vector.tensor_tensor(out=xres[:, s], in0=xres[:, s], in1=bo_bc[:], op=ALU.add).then_inc(xbo_done, 1)
                if 4 <= s < NT + 4:
                    g = s - 4
                    dve.wait_ge(x1_done, g + 1)
                    nc.vector.bn_stats(st2[:, g], x1[:, g % 2]).then_inc(st2_done, 1)
                if s + TPB < NT:
                    aggregate(s + TPB)
                if s % TPB == 3 and s // TPB + 1 < B:
                    v_diagonal(s // TPB + 1)
                if s < NT:
                    dve.wait_ge(exp_done, s + 1)
                    nc.vector.reduce_sum(sm[:, s % 2], Pr[:, s % 3], axis=AX.X).then_inc(sum_done, 1)
                if 4 <= s < NT + 4:
                    dve.wait_ge(st2_done, g + 1)
                    nc.vector.bn_aggr(mv2[:, g], st2[:, g]).then_inc(mv2_done, 1)
                if s + TPB + 1 < NT:
                    stats(s + TPB + 1)
                if s < NT:
                    dve.wait_ge(sum_done, s + 1)
                    if s >= 2:
                        dve.wait_ge(probs_done, s - 1)
                    nc.vector.reciprocal(inv[:, s % 2], sm[:, s % 2]).then_inc(inv_done, 1)
                if 4 <= s < NT + 4:
                    dve.wait_ge(mv2_done, g + 1)
                    nc.vector.tensor_scalar(out=ve2[:, g:g + 1], in0=mv2[:, g, 1:2], scalar1=EPS, scalar2=None, op0=ALU.add).then_inc(ve2_done, 1)
                if s >= 7 + 3 and (s - 7) % TPB == 3:
                    place((s - 7) // TPB)
                if 6 <= s < NT + 6 and (s - 6) % TPB == TPB - 1:
                    choose((s - 6) // TPB)
                for q in range(QA):
                    if s == x_step(q):
                        dve.wait_ge(x2t_sb, 2 * q + 2)
                        shared.vector_x(dve, q, x2T[:, :, q * HALF:(q + 1) * HALF])
                if s >= NT and (s - NT) // 2 < QA:
                    q = (s - NT) // 2
                    if (s - NT) % 2 == 0:
                        for e in range(NSH):
                            shared.vector_hidden(dve, q, e)
                    else:
                        dve.wait_ge(x1s_done, 2 * q + 2)
                        own = [xres[:, 2 * q + u] for u in range(2)]
                        shared.vector_output(dve, q, y_banks, own, own)
            dve.wait_ge(total_psum, 1)
            nc.vector.tensor_copy(counts[:], psD[:, 0:NE]).then_inc(metas, 1)

        @block.tensor
        def _(pe):
            pe.wait_ge(consts, 17)
            pe.wait_ge(ld_w, 16 * 4)
            for m in range(4):
                for c in range(C):
                    for f in range(C):
                        last = nc.tensor.transpose(psW[:, m, c * D + f * P:c * D + (f + 1) * P], wraw[:, m, f, c * P:(c + 1) * P], ident[:])
                last.then_inc(wt_psum, 1)
            pe.wait_ge(ld_c, 16)
            for c in range(C):
                for r in range(C):
                    last = nc.tensor.transpose(psA[:, c * 256 + r * P:c * 256 + (r + 1) * P], craw[:, r, c * P:(c + 1) * P], ident[:])
            last.then_inc(ctxt_psum, 1)
            pe.wait_ge(ctxt_sb, 1 + C)
            pe.wait_ge(wt_sb, 4)
            for f in range(C):
                for c in range(C):
                    last = nc.tensor.matmul(psP[:, 4 * f:4 * f + 2].rearrange("p a n -> p (a n)"), WT[:, 1, c, f * P:(f + 1) * P], ctxT[:, c],
                                            start=(c == 0), stop=(c == C - 1))
            last.then_inc(kv_psum, 1)
            for b in range(B):
                for c in range(C):
                    last = nc.tensor.matmul(psW[:, b, 0:D], ctxT2[:, c, b].rearrange("p a k -> p (a k)"), WT[:, 2, c],
                                            start=(c == 0), stop=(c == C - 1))
            last.then_inc(kv_psum, 1)

            def xn_transpose(g):
                pe.wait_ge(xn_done, g + 1)
                for c in range(C):
                    last = nc.tensor.transpose(psA[:, c * P:(c + 1) * P], xn[:, g % 2, c * P:(c + 1) * P], ident[:])
                last.then_inc(xnt_psum, 1)

            def queries(g):
                pe.wait_ge(xnt_sb, g + 1)
                for f in range(C):
                    for c in range(C):
                        last = nc.tensor.matmul(psA[:, D + f * P:D + (f + 1) * P], WT[:, 0, c, f * P:(f + 1) * P], xnT[:, g % 2, c],
                                                start=(c == 0), stop=(c == C - 1))
                last.then_inc(qt_psum, 1)

            xn_transpose(0)
            queries(0)
            pe.wait_ge(kv_sb, C + 1)
            for s in range(NT + LAST):
                if 4 <= s < NT + 4:
                    g = s - 4
                    pe.wait_ge(ot_sb, g + 1)
                    if g >= 1:
                        pe.wait_ge(x1_done, g)
                    if s >= 8 + 3 and (s - 8) % TPB == 3:
                        pe.wait_ge(ranks_read, (s - 8) // TPB + 1)
                    for c in range(C):
                        last = nc.tensor.matmul(psD[:, 0:D], OT[:, g % 2, c], WT[:, 3, c], start=(c == 0), stop=(c == C - 1))
                    last.then_inc(att_psum, 1)
                if s + 1 < NT or 6 <= s < NT + 6:
                    if s >= 6:
                        pe.wait_ge(x2t_sb, s - 5)
                    elif s >= 4:
                        pe.wait_ge(ot_sb, s - 3)
                if 6 <= s < NT + 6:
                    g = s - 6
                    for c in range(C):
                        last = nc.tensor.matmul(psA[:, D:D + NE], x2T[:, c, g * P:(g + 1) * P], rws[:, c], start=(c == 0), stop=(c == C - 1))
                    last.then_inc(gates_psum, 1)
                if s + 1 < NT:
                    pe.wait_ge(qt_sb, s + 1)
                    xn_transpose(s + 1)
                if s < NT:
                    b = s // TPB
                    if s % TPB == 0:
                        pe.wait_ge(kbd_ready, C * (b + 1))
                    pe.wait_ge(qt_sb, s + 1)
                    if s >= 2:
                        pe.wait_ge(shift_done, s - 1)
                    for c in range(C):
                        last = nc.tensor.matmul(psS[:, s % 2, c], QT[:, s % 2, c], Kbd[:, b % 2, c].rearrange("p h k -> p (h k)"),
                                                start=True, stop=True)
                    last.then_inc(scores_done, 1)
                if s + 1 < NT:
                    if s >= 6:
                        pe.wait_ge(gates_sb, s - 5)
                    queries(s + 1)
                if s >= 7 + 3 and (s - 7) % TPB == 3:
                    b = (s - 7) // TPB
                    pe.wait_ge(ohs_ready, b + 1)
                    pe.wait_ge(x1_done, min(s - 3, NT))
                    for t in range(TPB):
                        o = psD[:, 384 + t * NE:384 + (t + 1) * NE]
                        nc.tensor.matmul(o, tri[:], ohs[:, b * TPB + t], start=True, stop=False)
                        last = nc.tensor.matmul(o, ones[:], ohc[:, t], start=False, stop=True)
                    last.then_inc(ranks_psum, 1)
                if 2 <= s < NT + 2:
                    g = s - 2
                    pe.wait_ge(probs_done, g + 1)
                    if g >= 1:
                        pe.wait_ge(pt_sb, g)
                    for j in range(NJ):
                        last = nc.tensor.transpose(psP[:, j], Pr[:, g % 3, 2 * j:2 * j + 2].rearrange("p h k -> p (h k)"), ident[:])
                    last.then_inc(pt_psum, 1)
                if 3 <= s < NT + 3:
                    g = s - 3
                    b = g // TPB
                    if g % TPB == 0:
                        pe.wait_ge(vbd_ready, C * (b + 1))
                    pe.wait_ge(pt_sb, g + 1)
                    pe.wait_ge(qt_sb, min(s + 2, NT))
                    if s >= 6:
                        pe.wait_ge(gates_sb, s - 5)
                    for c in range(C):
                        for j in range(4):
                            last = nc.tensor.matmul(psA[:, D + c * P:D + (c + 1) * P], Vbd[:, b % 2, 4 * c + j], PT[:, g % 2, 4 * c + j],
                                                    start=(j == 0), stop=(j == 3))
                    last.then_inc(ot_psum, 1)
                if 5 <= s < NT + 5:
                    g = s - 5
                    b, t = g // TPB, g % TPB
                    pe.wait_ge(rows_done, 2 * (g + 1))
                    pe.wait_ge(ot_sb, min(s - 2, NT))
                    if s >= 6:
                        pe.wait_ge(gates_sb, s - 5)
                    for c in range(C):
                        last = nc.tensor.transpose(psA[:, c * P:(c + 1) * P], rows[:, b % 2, 0, t, c * P:(c + 1) * P], ident[:])
                    last.then_inc(x2t_psum, 1)
                if s >= NT and (s - NT) // 2 < QA:
                    if s == NT:
                        pe.wait_ge(shift_done, NT)
                    if (s - NT) % 2 == 0:
                        shared.tensor_hidden(pe, (s - NT) // 2, h_banks)
                    else:
                        shared.tensor_output(pe, (s - NT) // 2, y_banks)
            pe.wait_ge(slots_ready, B)
            nc.tensor.matmul(psD[:, 0:NE], ones[:], ohc[:, TPB], start=True, stop=True).then_inc(total_psum, 1)


def shared_experts(nc, keep, scratch, shared):
    w_hi, w_lo, counts, row_tab, exp_tab, tabs_ready = keep
    x1_d, xt_d, xg_d, acc_d = scratch
    with ExitStack() as es:
        def sb(name, shape, dt=F32):
            return es.enter_context(nc.sbuf_tensor(name, shape, dt))

        def sem(name):
            return es.enter_context(nc.semaphore(name))

        xt = sb("xt", [P, 2, C, HALF])
        acc = sb("acc", [P, 2, 2, D])
        filler = sb("filler2", [P, ROW])
        tile_f = sb("tile_f", [1, TILES])
        ntf = sb("ntf", [1, NE])
        nti = sb("nti", [1, 2, NE], I32)
        cum = sb("cum", [1, NE])
        onef = sb("onef", [1, NE])
        past = sb("past", [1, 2, NE, TILES])
        exp_f = sb("exp_f", [1, TILES])
        row_f = sb("row_f", [1, 3, TILES])
        fill_f = sb("fill_f", [1, 2, NE])
        fill_i = sb("fill_i", [1, NE], I32)
        psH = es.enter_context(nc.psum_tensor("psH", [P, 4, 512], F32))
        psY = es.enter_context(nc.psum_tensor("psY", [P, 4, 512], F32))
        h_banks = [psH[:, i, 0:HALF] for i in range(4)]
        y_banks = [[psY[:, 2 * i + u, 0:D] for u in range(2)] for i in range(2)]

        xt_in = [sem(f"xt_in{i}") for i in range(2)]
        acc_in = [sem(f"acc_in{i}") for i in range(2)]
        acc_out = [sem(f"acc_out{i}") for i in range(2)]
        cst, tab, fill_ready, fill_out = sem("cst"), sem("tab"), sem("fill_ready"), sem("fill_out")
        block = es.enter_context(nc.Block())

        FIRST, PIECES = 2 * NSH, 2 * (NSH + NE)
        STEPS = NQ - QA

        def target(w, n):
            return w[:, n // 2 - NSH, n % 2 * (WPE // 2):(n % 2 + 1) * (WPE // 2)]

        @block.sync
        def _(sp):
            for n in range(FIRST + 2, FIRST + 6):
                shared.load_piece(sp, n)
            sp.wait_ge(fill_ready, 1)
            sp.wait_ge(cst, 4)
            for e in range(NE):
                r = sp.value_load(fill_i[0:1, e:e + 1], min_val=0, max_val=FILL_ROW - P)
                sp.dma_start(xg_d[bass.ds(r, P), :], filler[:]).then_inc(fill_out, 16)
            for n in range(FIRST + 6, PIECES):
                shared.load_piece(sp, n)
            sp.wait_ge(fill_out, 16 * NE)

        @block.gpsimd
        def _(pool):
            pool.memset(filler[:], 0.0).then_inc(cst, 1)
            pool.memset(onef[:], 1.0).then_inc(cst, 1)
            pool.iota(tile_f[:], pattern=[[1, TILES]], base=0, channel_multiplier=0,
                      allow_small_or_imprecise_dtypes=True).then_inc(cst, 1)
            pool.wait_ge(cst, 3)
            pool.iota(filler[:, D:D + 1].bitcast(I32), pattern=[[0, 1]], base=SKIP, channel_multiplier=1).then_inc(cst, 1)
            for n in range(FIRST, PIECES):
                shared.split_low(pool, n, target(w_hi, n), target(w_lo, n))

        @block.scalar
        def _(act):
            def load_x(j):
                if j >= 2:
                    act.wait_ge(shared.xlo_done, QA + j - 1)
                act_q = QA + j
                nc.scalar.dma_start(xt[:, j % 2], xt_d[:, :, act_q * HALF:(act_q + 1) * HALF]).then_inc(xt_in[j % 2], 16)

            def load_acc(j):
                if j >= 2:
                    act.wait_ge(acc_out[j % 2], 16 * (j // 2))
                t = 2 * (QA + j)
                nc.scalar.dma_start(acc[:, j % 2], x1_d[t:t + 2].rearrange("t p d -> p t d")).then_inc(acc_in[j % 2], 16)

            def store_acc(j):
                act.wait_ge(shared.acc_done, 2 * (QA + j + 1))
                t = 2 * (QA + j)
                nc.scalar.dma_start(acc_d[t:t + 2].rearrange("t p d -> p t d"), acc[:, j % 2]).then_inc(acc_out[j % 2], 16)

            def split_x(j):
                act.wait_ge(xt_in[j % 2], 16 * (j // 2 + 1))
                shared.scalar_x(act, QA + j, xt[:, j % 2])

            load_x(0)
            load_x(1)
            load_acc(0)
            load_acc(1)
            split_x(0)
            n = FIRST
            for j in range(STEPS):
                for s in range(NSH):
                    shared.scalar_hidden(act, QA + j, s, h_banks)
                    if s == 0 and j + 1 < STEPS:
                        split_x(j + 1)
                    if s == 0 and j >= 1:
                        store_acc(j - 1)
                    if s == 0 and j + 2 < STEPS:
                        load_x(j + 2)
                    if s == 1 and 1 <= j and j + 1 < STEPS:
                        load_acc(j + 1)
                    while n < FIRST + (PIECES - FIRST) * (j * NSH + s + 1) // (STEPS * NSH):
                        shared.split_high(act, n, target(w_hi, n))
                        n += 1
            store_acc(STEPS - 1)
            for parity in range(2):
                act.wait_ge(acc_out[parity], 16 * len(range(parity, STEPS, 2)))

        @block.vector
        def _(dve):
            steps = [0]

            def chain(ins):
                steps[0] += 1
                ins.then_inc(tab, 1)
                dve.wait_ge(tab, steps[0])

            V = nc.vector
            dve.wait_ge(cst, 4)
            chain(V.tensor_scalar(out=nti[:, 0], in0=counts[0:1, :], scalar1=float(P - 1), scalar2=None, op0=ALU.add))
            chain(V.tensor_scalar(out=nti[:, 1], in0=nti[:, 0], scalar1=P.bit_length() - 1, scalar2=None, op0=ALU.arith_shift_right))
            chain(V.tensor_copy(ntf[:], nti[:, 1]))
            chain(V.tensor_tensor_scan(out=cum[:], data0=onef[:], data1=ntf[:], initial=0.0, op0=ALU.mult, op1=ALU.add))
            V.tensor_scalar(out=fill_f[:, 0], in0=tile_f[:, 0:NE], scalar1=float(CAP), scalar2=None, op0=ALU.mult)
            chain(V.tensor_tensor(out=past[:, 0], in0=tile_f[:].unsqueeze(1).to_broadcast([1, NE, TILES]),
                                  in1=cum[:].unsqueeze(2).to_broadcast([1, NE, TILES]), op=ALU.is_ge))
            V.tensor_tensor(out=fill_f[:, 1], in0=fill_f[:, 0], in1=counts[0:1, :], op=ALU.add)
            V.tensor_tensor(out=past[:, 1], in0=past[:, 0], in1=ntf[:].unsqueeze(2).to_broadcast([1, NE, TILES]), op=ALU.mult)
            chain(V.reduce_sum(exp_f[:], past[:, 0, 0:NE - 1].rearrange("p e t -> p t e"), axis=AX.X))
            V.tensor_copy(fill_i[:], fill_f[:, 1]).then_inc(fill_ready, 1)
            chain(V.reduce_sum(row_f[:, 0], past[:, 1, 0:NE - 1].rearrange("p e t -> p t e"), axis=AX.X))
            chain(V.tensor_tensor(out=row_f[:, 1], in0=tile_f[:], in1=row_f[:, 0], op=ALU.subtract))
            chain(V.tensor_scalar(out=row_f[:, 2], in0=exp_f[:], scalar1=float(CAP), scalar2=None, op0=ALU.mult))
            chain(V.scalar_tensor_tensor(out=row_f[:, 0], in0=row_f[:, 1], scalar=float(P), in1=row_f[:, 2], op0=ALU.mult, op1=ALU.add))
            chain(V.tensor_scalar(out=row_f[:, 1], in0=row_f[:, 0], scalar1=-1.0, scalar2=float(FILL_ROW), op0=ALU.mult, op1=ALU.add))
            chain(V.tensor_tensor(out=row_f[:, 2], in0=row_f[:, 1], in1=past[:, 0, NE - 1], op=ALU.mult))
            chain(V.tensor_tensor(out=row_f[:, 1], in0=row_f[:, 0], in1=row_f[:, 2], op=ALU.add))
            V.tensor_copy(row_tab[:], row_f[:, 1]).then_inc(tabs_ready, 1)
            V.tensor_copy(exp_tab[:], exp_f[:]).then_inc(tabs_ready, 1)
            for j in range(STEPS):
                q = QA + j
                if j == 0:
                    shared.vector_x(dve, q, xt[:, 0])
                for s in range(NSH):
                    shared.vector_hidden(dve, q, s)
                    if s == 0 and j + 1 < STEPS:
                        shared.vector_x(dve, q + 1, xt[:, (j + 1) % 2])
                dve.wait_ge(acc_in[j % 2], 16 * (j // 2 + 1))
                own = [acc[:, j % 2, u] for u in range(2)]
                shared.vector_output(dve, q, y_banks, own, own)

        @block.tensor
        def _(pe):
            for q in range(QA, NQ):
                shared.tensor_hidden(pe, q, h_banks)
                shared.tensor_output(pe, q, y_banks)


def routed_experts(nc, ios, keep, scratch, out):
    (b1, b2) = ios
    w_hi, w_lo, gap, row_tab, exp_tab, tabs_ready = keep
    xg_d, acc_d, y_d = scratch
    with ExitStack() as es:
        def sb(name, shape, dt=F32):
            return es.enter_context(nc.sbuf_tensor(name, shape, dt))

        def sem(name):
            return es.enter_context(nc.semaphore(name))

        b1T = sb("b1T", [P, NE, HC])
        b2_bc = sb("b2_bc", [P, NE, D])
        ident = sb("ident3", [P, P])
        NXB, NYB = 8, 4
        xg = sb("xg", [P, NXB, ROW])
        x_hi = sb("x_hi", [P, 2, C, P], F32R)
        x_lo = sb("x_lo", [P, 2, C, P], F32R)
        hpre = sb("hpre", [P, 2, HF])
        hb = sb("hb", [P, 2, HC, P])
        g = sb("g3", [P, 2, HC, P])
        h_hi = sb("hh_hi", [P, 2, HC, P], F32R)
        h_lo = sb("hh_lo", [P, 2, HC, P], F32R)
        y = sb("y", [P, NYB, D])
        yin = sb("yin", [P, 4, 2, D])
        ain = sb("ain", [P, 4, D])
        ge = sb("ge", [P, 2, NT])
        p12 = sb("p12", [P, 2, NT])
        fin = sb("fin", [P, 4, D])
        ps = es.enter_context(nc.psum_tensor("ps3", [P, 8, 512], F32))

        xg_in = [sem(f"xg_in{i}") for i in range(NXB)]
        y_out = [sem(f"y_out{i}") for i in range(NXB)]
        cst, small = sem("cst3"), sem("small3")
        exp2_done, weights = sem("exp2_done"), sem("weights")
        xt_psum, xhi_done, xlo_done = sem("xt_psum"), sem("xhi3"), sem("xlo3")
        hid_psum, hpre_done, ht_psum, hb_done = sem("hid_psum"), sem("hpre_done"), sem("ht_psum"), sem("hb_done")
        g_done, hhi_done, hlo_done, res_psum, y_done = sem("g3_done"), sem("hhi3"), sem("hlo3"), sem("res_psum"), sem("y_done")
        yin_in = [sem(f"yin_in{i}") for i in range(4)]
        half_done, fin_done = sem("half_done"), sem("fin_done")
        out_sem = [sem(f"out{i}") for i in range(4)]
        block = es.enter_context(nc.Block())

        @block.sync
        def _(sp):
            sp.wait_ge(tabs_ready, 2)
            for t in range(TILES):
                r = sp.value_load(row_tab[0:1, t:t + 1], min_val=0, max_val=FILL_ROW)
                if t >= NXB:
                    sp.wait_ge(y_out[t % NXB], 16 * (t // NXB))
                sp.dma_start(xg[:, t % NXB], xg_d[bass.ds(r, P), :]).then_inc(xg_in[t % NXB], 16)
            for i in range(NXB):
                sp.wait_ge(y_out[i], 16 * len(range(i, TILES, NXB)))
            for t in range(NT):
                if t >= 4:
                    sp.wait_ge(fin_done, t - 3)
                sp.dma_start(yin[:, t % 4], y_d[:, t * P:(t + 1) * P, :].rearrange("k p d -> p k d")).then_inc(yin_in[t % 4], 16)
                sp.dma_start(ain[:, t % 4], acc_d[t]).then_inc(yin_in[t % 4], 16)

        @block.gpsimd
        def _(pool):
            pool.memset(ident[:], 0.0).then_inc(cst, 1)
            pool.wait_ge(cst, 1)
            pool.affine_select(out=ident[:], in_=ident[:], compare_op=ALU.not_equal, fill=1.0, base=0,
                               pattern=[[-1, P]], channel_multiplier=1).then_inc(cst, 1)
            for t in range(TILES):
                pool.wait_ge(y_done, t + 1)
                pool.indirect_dma_start(y_d.rearrange("k n d -> (k n) d"),
                                        bass.IndirectOffsetOnAxis(ap=xg[:, t % NXB, D:D + 1].bitcast(U32), axis=0),
                                        y[:, t % NYB], None, bounds_check=2 * TOK - 1, oob_is_err=False).then_inc(y_out[t % NXB], 16)

        @block.scalar
        def _(act):
            nc.scalar.dma_start(b1T[:], b1.rearrange("e (p c) -> p e c", p=P)).then_inc(small, 16)
            nc.scalar.dma_start(b2_bc[:], b2.partition_broadcast(P)).then_inc(small, 16)
            for t in range(-1, TILES + 1):
                if t + 1 < TILES:
                    n = t + 1
                    act.wait_ge(xt_psum, n + 1)
                    if n >= 2:
                        act.wait_ge(hid_psum, n - 1)
                    nc.scalar.activation(x_hi[:, n % 2], ps[:, n % 2, 0:D].rearrange("p (c n) -> p c n", c=C), ACT.Copy).then_inc(xhi_done, 1)
                if 0 <= t < TILES:
                    act.wait_ge(hid_psum, t + 1)
                    if t >= 2:
                        act.wait_ge(ht_psum, t - 1)
                    nc.scalar.activation(hpre[:, t % 2], ps[:, 2 + t % 2], ACT.Copy).then_inc(hpre_done, 1)
                if 1 <= t:
                    n = t - 1
                    act.wait_ge(hb_done, n + 1)
                    if n >= 2:
                        act.wait_ge(hlo_done, n - 1)
                    nc.scalar.activation(g[:, n % 2], hb[:, n % 2], ACT.Gelu).then_inc(g_done, 1)
                    if n >= 2:
                        act.wait_ge(res_psum, n - 1)
                    nc.scalar.activation(h_hi[:, n % 2], hb[:, n % 2], ACT.Gelu).then_inc(hhi_done, 1)
            nc.scalar.activation(ge[:, 0], gap[:], ACT.Exp).then_inc(exp2_done, 1)
            for t in range(NT):
                act.wait_ge(fin_done, t + 1)
                nc.scalar.dma_start(out[t], fin[:, t % 4]).then_inc(out_sem[t % 4], 16)
            for i in range(4):
                act.wait_ge(out_sem[i], 16 * NT // 4)

        @block.vector
        def _(dve):
            V = nc.vector
            dve.wait_ge(small, 32)
            dve.wait_ge(tabs_ready, 2)
            for t in range(-1, TILES + 2):
                if t + 1 < TILES:
                    n = t + 1
                    dve.wait_ge(xhi_done, n + 1)
                    V.tensor_tensor(out=x_lo[:, n % 2], in0=ps[:, n % 2, 0:D].rearrange("p (c n) -> p c n", c=C),
                                    in1=x_hi[:, n % 2].bitcast(F32), op=ALU.subtract).then_inc(xlo_done, 1)
                if 1 <= t <= TILES:
                    n = t - 1
                    e = dve.value_load(exp_tab[0:1, n:n + 1], min_val=0, max_val=NE - 1)
                    dve.wait_ge(ht_psum, n + 1)
                    if n >= 2:
                        dve.wait_ge(hhi_done, n - 1)
                    V.tensor_tensor(out=hb[:, n % 2], in0=ps[:, 4 + n % 2].rearrange("p (c n) -> p c n", c=HC),
                                    in1=b1T[:, bass.ds(e, 1), :].squeeze(1).unsqueeze(2).to_broadcast([P, HC, P]), op=ALU.add).then_inc(hb_done, 1)
                    dve.wait_ge(g_done, n + 1)
                    dve.wait_ge(hhi_done, n + 1)
                    V.tensor_tensor(out=h_lo[:, n % 2], in0=g[:, n % 2], in1=h_hi[:, n % 2].bitcast(F32), op=ALU.subtract).then_inc(hlo_done, 1)
                if 2 <= t:
                    n = t - 2
                    e = dve.value_load(exp_tab[0:1, n:n + 1], min_val=0, max_val=NE - 1)
                    dve.wait_ge(res_psum, n + 1)
                    if n >= NYB:
                        dve.wait_ge(y_out[(n - NYB) % NXB], 16 * ((n - NYB) // NXB + 1))
                    V.tensor_tensor(out=y[:, n % NYB], in0=ps[:, 6 + n % 2, 0:D], in1=b2_bc[:, bass.ds(e, 1), :].squeeze(1),
                                    op=ALU.add).then_inc(y_done, 1)
            dve.wait_ge(exp2_done, 1)
            V.tensor_scalar(out=ge[:, 1], in0=ge[:, 0], scalar1=1.0, scalar2=None, op0=ALU.add).then_inc(weights, 1)
            dve.wait_ge(weights, 1)
            V.reciprocal(p12[:, 0], ge[:, 1]).then_inc(weights, 1)
            dve.wait_ge(weights, 2)
            V.tensor_tensor(out=p12[:, 1], in0=p12[:, 0], in1=ge[:, 0], op=ALU.mult).then_inc(weights, 1)
            dve.wait_ge(weights, 3)
            for t in range(NT):
                dve.wait_ge(yin_in[t % 4], 32 * (t // 4 + 1))
                V.scalar_tensor_tensor(out=ain[:, t % 4], in0=yin[:, t % 4, 0], scalar=p12[:, 0, t:t + 1], in1=ain[:, t % 4],
                                       op0=ALU.mult, op1=ALU.add).then_inc(half_done, 1)
                dve.wait_ge(half_done, t + 1)
                if t >= 4:
                    dve.wait_ge(out_sem[t % 4], 16 * (t // 4))
                V.scalar_tensor_tensor(out=fin[:, t % 4], in0=yin[:, t % 4, 1], scalar=p12[:, 1, t:t + 1], in1=ain[:, t % 4],
                                       op0=ALU.mult, op1=ALU.add).then_inc(fin_done, 1)

        @block.tensor
        def _(pe):
            pe.wait_ge(cst, 2)
            pe.wait_ge(tabs_ready, 2)

            def x_transpose(n):
                pe.wait_ge(xg_in[n % NXB], 16 * (n // NXB + 1))
                if n >= 2:
                    pe.wait_ge(xlo_done, n - 1)
                for c in range(C):
                    last = nc.tensor.transpose(ps[:, n % 2, c * P:(c + 1) * P], xg[:, n % NXB, c * P:(c + 1) * P], ident[:])
                last.then_inc(xt_psum, 1)

            x_transpose(0)
            for t in range(TILES + 2):
                if t + 1 < TILES:
                    x_transpose(t + 1)
                if t < TILES:
                    e = pe.value_load(exp_tab[0:1, t:t + 1], min_val=0, max_val=NE - 1)
                    pe.wait_ge(xlo_done, t + 1)
                    if t >= 2:
                        pe.wait_ge(hpre_done, t - 1)
                    k = 0
                    for c in range(C):
                        for a, b in ((x_hi, w_lo), (x_lo, w_hi), (x_hi, w_hi)):
                            last = nc.tensor.matmul(ps[:, 2 + t % 2], a[:, t % 2, c], b[:, bass.ds(e, 1), c * HF:(c + 1) * HF].squeeze(1),
                                                    start=(k == 0), stop=(k == 3 * C - 1))
                            k += 1
                    last.then_inc(hid_psum, 1)
                if 1 <= t <= TILES:
                    n = t - 1
                    pe.wait_ge(hpre_done, n + 1)
                    if n >= 2:
                        pe.wait_ge(hb_done, n - 1)
                    for c in range(HC):
                        last = nc.tensor.transpose(ps[:, 4 + n % 2, c * P:(c + 1) * P], hpre[:, n % 2, c:HF:HC], ident[:])
                    last.then_inc(ht_psum, 1)
                if 2 <= t:
                    n = t - 2
                    e = pe.value_load(exp_tab[0:1, n:n + 1], min_val=0, max_val=NE - 1)
                    pe.wait_ge(hlo_done, n + 1)
                    if n >= 2:
                        pe.wait_ge(y_done, n - 1)
                    k = 0
                    for c in range(HC):
                        for a, b in ((h_hi, w_lo), (h_lo, w_hi), (h_hi, w_hi)):
                            last = nc.tensor.matmul(ps[:, 6 + n % 2, 0:D], a[:, n % 2, c],
                                                    b[:, bass.ds(e, 1), C * HF + c * D:C * HF + (c + 1) * D].squeeze(1),
                                                    start=(k == 0), stop=(k == 3 * HC - 1))
                            k += 1
                    last.then_inc(res_psum, 1)


def build(nc, a, out):
    x1_d = nc.dram_tensor("x1_d", [NT, P, D], F32, kind="Internal").ap()
    xt_d = nc.dram_tensor("xt_d", [P, C, TOK], F32, kind="Internal").ap()
    xg_d = nc.dram_tensor("xg_d", [XG_ROWS, ROW], F32, kind="Internal").ap()
    acc_d = nc.dram_tensor("acc_d", [NT, P, D], F32, kind="Internal").ap()
    y_d = nc.dram_tensor("y_d", [2, TOK, D], F32, kind="Internal").ap()
    with ExitStack() as es:
        def sb(name, shape, dt=F32):
            return es.enter_context(nc.sbuf_tensor(name, shape, dt))

        gap = sb("gap", [P, NT])
        counts = sb("counts", [P, NE])
        row_tab = sb("row_tab", [1, TILES], I32)
        exp_tab = sb("exp_tab", [1, TILES], I32)
        counts_ready = es.enter_context(nc.semaphore("counts_ready"))
        tabs_ready = es.enter_context(nc.semaphore("tabs_ready"))
        X, F = "L0_xattn_", "L0_ffn_"
        with ExitStack() as es_shared:
            shared = SharedExperts(nc, es_shared, (a[F + "w1"], a[F + "w2"], a[F + "sw1"], a[F + "sb1"], a[F + "sw2"]))
            attention(nc, (a["x"], a["ctx_1024"], a[X + "Wv"], a[X + "Wk"], a[X + "Wq"], a[X + "Wo"], a[X + "bo"],
                           a[F + "router_w"], a[F + "router_b"], a[F + "sb2"]), (gap, counts, counts_ready), (x1_d, xt_d, xg_d, acc_d), shared)
            w_hi = sb("w_hi", [P, NE, WPE], F32R)
            w_lo = sb("w_lo", [P, NE, WPE], F32R)
            shared_experts(nc, (w_hi, w_lo, counts, row_tab, exp_tab, tabs_ready), (x1_d, xt_d, xg_d, acc_d), shared)
        routed_experts(nc, (a[F + "b1"], a[F + "b2"]), (w_hi, w_lo, gap, row_tab, exp_tab, tabs_ready), (xg_d, acc_d, y_d),
                       out.rearrange("b (t p) d -> (b t) p d", p=P))


INS = ["x", "ctx_1024", "L0_xattn_Wv", "L0_xattn_Wk", "L0_xattn_Wq", "L0_xattn_Wo", "L0_xattn_bo", "L0_ffn_router_w",
       "L0_ffn_router_b", "L0_ffn_w1", "L0_ffn_b1", "L0_ffn_w2", "L0_ffn_b2", "L0_ffn_sw1", "L0_ffn_sb1", "L0_ffn_sw2", "L0_ffn_sb2"]


def kernel(**inputs):
    import concourse.bacc as bacc
    from concourse.bass_utils import run_bass_kernel_spmd

    nc = bacc.Bacc("TRN2", target_bir_lowering=False, num_devices=1)
    arrays, aps = {}, {}
    for name in INS:
        a = np.ascontiguousarray(inputs[name])
        arrays[f"in_{name}"] = a
        aps[name] = nc.dram_tensor(f"in_{name}", a.shape, mybir.dt.from_np(a.dtype), kind="ExternalInput").ap()
    out = nc.dram_tensor("out", (B, S, D), F32, kind="ExternalOutput").ap()
    build(nc, aps, out)
    r = run_bass_kernel_spmd(nc, [arrays], core_ids=[0])
    return r.results[0]["out"]
```

```python
import numpy as np
import concourse.bass as bass
from concourse import mybir
from contextlib import ExitStack

F32 = mybir.dt.float32
F32R = mybir.dt.float32r
BF16 = mybir.dt.bfloat16
I32 = mybir.dt.int32
U32 = mybir.dt.uint32
ALU = mybir.AluOpType
ACT = mybir.ActivationFunctionType
AX = mybir.AxisListType

P = 128
B, S, D = 4, 512, 256
TOK = B * S
NT = TOK // P
TPB = S // P
L = 64
NH, HD = 16, 16
C = D // P
HPC = P // HD
NJ = NH // 2
NE, NSH, HF = 8, 2, 512
HC = HF // P
EPS = 1e-5
LAST = 2 * 4 + 1
NR = 3
AHEAD = TPB + 3
HALF = 256
NQ = TOK // HALF
QUERY, KEY, VALUE, OUT = range(4)
RAW = 4
NXB = 8
EARLY = 3
QA = LAST // 2
WPE = C * HF + HC * D
PIECE = 512
PPE = WPE // PIECE
ROW = D + 4
CAP = TOK + P
FILL_ROW = NE * CAP
XG_ROWS = FILL_ROW + P
TILES = (2 * TOK + NE * (P - 1)) // P
SKIP = 2 * TOK + 4096


class SharedExperts:

    def __init__(self, nc, es, stage, ios):
        self.nc = nc
        self.w1, self.w2, self.sw1, self.sb1, self.sw2 = ios

        def sb(name, shape, dt=F32):
            return es.enter_context(nc.sbuf_tensor(name, shape, dt, side="right"))

        def sem(name):
            return es.enter_context(nc.semaphore(name))

        self.s_hi = sb("s_hi", [P, NSH, WPE], F32R)
        self.s_lo = sb("s_lo", [P, NSH, WPE], F32R)
        self.raw = stage[:, 0:RAW * PIECE].rearrange("p (r n) -> p r n", r=RAW)
        self.xt_hi = sb("xt_hi", [P, 2, C, HALF], F32R)
        self.xt_lo = sb("xt_lo", [P, 2, C, HALF], F32R)
        self.g = sb("g", [P, 2, HALF])
        self.h_hi = sb("h_hi", [P, NSH, HC, HALF], F32R)
        self.h_lo = sb("h_lo", [P, NSH, HC, HALF], F32R)
        self.sb1T = sb("sb1T", [P, NSH, HC])
        self.raw_in = [sem(f"raw_in{i}") for i in range(RAW)]
        self.hi_done = [sem(f"hi_done{i}") for i in range(RAW)]
        self.lo_done = [sem(f"lo_done{i}") for i in range(RAW)]
        self.xhi_done, self.xlo_done = sem("xhi_done"), sem("xlo_done")
        self.b1_in, self.h_psum, self.g_done, self.hhi_done = sem("b1_in"), sem("h_psum"), sem("g_done"), sem("hhi_done")
        self.hlo_done, self.y_psum, self.acc_done = sem("hlo_done"), sem("y_psum"), sem("acc_done")

    def piece_source(self, n):
        e, k = n // PPE, n % PPE
        if e < NSH:
            w1, w2 = self.sw1[e], self.sw2[e]
        else:
            w1, w2 = self.w1[e - NSH], self.w2[e - NSH]
        if k < C:
            return w1[k * P:(k + 1) * P, :]
        c = (k - C) * PIECE // D
        return w2.rearrange("(p c) n -> p c n", p=P)[:, c:c + PIECE // D, :]

    def load_piece(self, sp, n):
        if n >= RAW:
            sp.wait_ge(self.lo_done[n % RAW], n // RAW)
        w = self.piece_source(n)
        to = self.raw[:, n % RAW]
        if n % PPE >= C:
            to = to.rearrange("p (c n) -> p c n", n=D)
        sp.dma_start(to, w).then_inc(self.raw_in[n % RAW], 16)

    @staticmethod
    def part(w, n, first):
        return w[:, n // PPE - first, n % PPE * PIECE:(n % PPE + 1) * PIECE]

    def split_high(self, act, n, target):
        act.wait_ge(self.raw_in[n % RAW], 16 * (n // RAW + 1))
        self.nc.scalar.activation(target, self.raw[:, n % RAW], ACT.Copy).then_inc(self.hi_done[n % RAW], 1)

    def split_low(self, engine, n, high, target):
        engine.wait_ge(self.hi_done[n % RAW], n // RAW + 1)
        engine.tensor_tensor(out=target, in0=self.raw[:, n % RAW], in1=high.bitcast(F32), op=ALU.subtract).then_inc(self.lo_done[n % RAW], 1)

    def scalar_x(self, act, q, src):
        if q >= 2:
            act.wait_ge(self.h_psum, (q - 1) * NSH * HC)
        self.nc.scalar.activation(self.xt_hi[:, q % 2], src, ACT.Copy).then_inc(self.xhi_done, 1)

    def vector_x(self, dve, q, src):
        dve.wait_ge(self.xhi_done, q + 1)
        if q >= 2:
            dve.wait_ge(self.h_psum, (q - 1) * NSH * HC)
        self.nc.vector.tensor_tensor(out=self.xt_lo[:, q % 2], in0=src, in1=self.xt_hi[:, q % 2].bitcast(F32),
                                     op=ALU.subtract).then_inc(self.xlo_done, 1)

    def tensor_hidden(self, pe, q, banks, fresh=False):
        for s in range(NSH):
            if q == 0:
                for n in range(s * PPE, (s + 1) * PPE):
                    pe.wait_ge(self.lo_done[n % RAW], n // RAW + 1)
            if fresh and s == 0:
                pe.wait_ge(self.hhi_done, q * NSH * HC)
            if s == 0:
                pe.wait_ge(self.xlo_done, q + 1)
            for c in range(HC):
                n = (q * NSH + s) * HC + c
                if n >= len(banks):
                    pe.wait_ge(self.hhi_done, n - len(banks) + 1)
                k = 0
                for ch in range(C):
                    w = slice(ch * HF + c, (ch + 1) * HF, HC)
                    for a, b in ((self.s_lo, self.xt_hi), (self.s_hi, self.xt_lo), (self.s_hi, self.xt_hi)):
                        last = self.nc.tensor.matmul(banks[n % len(banks)], a[:, s, w], b[:, q % 2, ch], start=(k == 0), stop=(k == 3 * C - 1))
                        k += 1
                last.then_inc(self.h_psum, 1)

    def scalar_hidden(self, act, q, s, banks):
        for c in range(HC):
            n = (q * NSH + s) * HC + c
            act.wait_ge(self.h_psum, n + 1)
            if n >= 2:
                act.wait_ge(self.hlo_done, n - 1)
            if q >= 1 and c == 0:
                act.wait_ge(self.y_psum, NSH * (q - 1) + s + 1)
            self.nc.scalar.activation(self.g[:, n % 2], banks[n % len(banks)], ACT.Gelu, bias=self.sb1T[:, s, c:c + 1]).then_inc(self.g_done, 1)
            self.nc.scalar.activation(self.h_hi[:, s, c], banks[n % len(banks)], ACT.Gelu, bias=self.sb1T[:, s, c:c + 1]).then_inc(self.hhi_done, 1)

    def vector_hidden(self, dve, q, s, c):
        n = (q * NSH + s) * HC + c
        dve.wait_ge(self.g_done, n + 1)
        dve.wait_ge(self.hhi_done, n + 1)
        self.nc.vector.tensor_tensor(out=self.h_lo[:, s, c], in0=self.g[:, n % 2], in1=self.h_hi[:, s, c].bitcast(F32),
                                     op=ALU.subtract).then_inc(self.hlo_done, 1)

    def tensor_output(self, pe, q, banks):
        for s in range(NSH):
            pe.wait_ge(self.hlo_done, (q * NSH + s + 1) * HC)
            if q >= len(banks) and s == 0:
                pe.wait_ge(self.acc_done, 2 * (q - len(banks) + 1))
            for u in range(2):
                for c in range(HC):
                    w = slice(C * HF + c * D, C * HF + (c + 1) * D)
                    for k, (a, b) in enumerate(((self.h_hi, self.s_lo), (self.h_lo, self.s_hi), (self.h_hi, self.s_hi))):
                        last = self.nc.tensor.matmul(banks[q % len(banks)][u], a[:, s, c, u * P:(u + 1) * P], b[:, s, w],
                                                     start=(s == 0 and c == 0 and k == 0), stop=(s == NSH - 1 and c == HC - 1 and k == 2))
            last.then_inc(self.y_psum, 1)

    def vector_output(self, dve, q, banks, x1, out):
        dve.wait_ge(self.y_psum, NSH * (q + 1))
        for u in range(2):
            self.nc.vector.scalar_tensor_tensor(out=out[u], in0=banks[q % len(banks)][u], scalar=1.0 / NSH, in1=x1[u],
                                                op0=ALU.mult, op1=ALU.add).then_inc(self.acc_done, 1)


def x_step(q):
    return NT - 4 + q if q < 2 else NT + 2 * (q - 2) + 1


def attention(nc, ios, keep, scratch, shared):
    (x, ctx, Wv, Wk, Wq, Wo, bo, rw, rb, sb2) = ios
    ident, gap, counts, metas = keep
    x1_d, xt_d, xg_d, acc_d = scratch
    with ExitStack() as es:
        def sb(name, shape, dt=F32):
            return es.enter_context(nc.sbuf_tensor(name, shape, dt))

        def sem(name):
            return es.enter_context(nc.semaphore(name))

        xres = sb("xres", [P, NT, D])
        wraw = sb("wraw", [P, 4, C, D])
        craw = sb("craw", [P, C, D])
        WT = sb("WT", [P, 4, C, D])
        ctxT = sb("ctxT", [P, C, B * L])
        ctxT2 = sb("ctxT2", [P, C, B, 2, L])
        KT = sb("KT", [P, C, B, L])
        Vsb = sb("Vsb", [P, B, D])
        Kbd = sb("Kbd", [P, 2, C, HPC, L])
        Vbd = sb("Vbd", [P, 2, NJ, P])
        maskK = sb("maskK", [P, HPC])
        maskV = sb("maskV", [P, 4, HPC])
        tri = sb("tri", [P, P], BF16)
        ones = sb("ones", [P, P], BF16)
        bo_bc = sb("bo_bc", [P, D])
        rb_bc = sb("rb_bc", [P, NE])
        sb2_bc = sb("sb2_bc", [P, NSH, D])
        sbh = sb("sbh", [P, D])
        rws = sb("rws", [P, C, NE])
        iota8 = sb("iota8", [P, NE])
        ebase = sb("ebase", [P, NE])
        ids = sb("ids", [P, 2, NT], I32)
        half = sb("half", [P, 1])
        warm = sb("warm", [P, 1])
        st1 = sb("st1", [P, NT, 6])
        mv1 = sb("mv1", [P, NT, 2])
        ve1 = sb("ve1", [P, NT])
        rs1 = sb("rs1", [P, NT])
        st2 = sb("st2", [P, NT, 6])
        mv2 = sb("mv2", [P, NT, 2])
        ve2 = sb("ve2", [P, NT])
        rs2 = sb("rs2", [P, NT])
        xn = sb("xn", [P, 2, D])
        xnT = sb("xnT", [P, 2, C, P])
        QT = sb("QT", [P, 2, C, P])
        mx = sb("mx", [P, 2, NH])
        sm = sb("sm", [P, 2, NH])
        inv = sb("inv", [P, 2, NH])
        Pr = sb("Pr", [P, 3, NH, L])
        PT = sb("PT", [P, 2, NJ, P])
        OT = sb("OT", [P, 2, C, P])
        rows = sb("rows", [P, NR, 2, TPB, ROW])
        x2T = sb("x2T", [P, C, TOK])
        gates = sb("gates", [P, 2, TPB, NE])
        top = sb("top", [P, TPB, 8])
        topi = sb("topi", [P, TPB, 8], U32)
        topf = sb("topf", [P, 2, TPB])
        oh = sb("oh", [P, 2, TPB, NE])
        ohs = sb("ohs", [P, NT, NE], BF16)
        ohc = sb("ohc", [P, TPB + 1, NE], BF16)
        rk = sb("rk", [P, TPB, NE])
        pk = sb("pk", [P, 2, TPB, NE])
        slotf = sb("slotf", [P, 2, TPB])
        slots = sb("slots", [P, 2, 2, TPB], I32)
        filler = sb("filler", [P, ROW])
        psS = es.enter_context(nc.psum_tensor("psS", [P, 2, C, 512], F32))
        psP = es.enter_context(nc.psum_tensor("psP", [P, NJ, P], F32))
        psA = es.enter_context(nc.psum_tensor("psA", [P, 512], F32))
        psD = es.enter_context(nc.psum_tensor("psD", [P, 512], F32))
        psW = psS[:, :, :, :].rearrange("p a c n -> p (a c) n")
        h_banks = [psS[:, 0, i, 0:HALF] for i in range(2)]
        more_h_banks = h_banks + [psP[:, 4 * i:4 * i + 2].rearrange("p a n -> p (a n)") for i in range(2)]
        y_banks = [[psS[:, 1, u, 0:D] for u in range(2)]]

        ld_w, ld_c, ld_small = [sem(f"ld_w{m}") for m in range(4)], sem("ld_c"), sem("ld_small")
        ld_x = [sem(f"ld_x{b}") for b in range(B)]
        consts, fillers = sem("consts"), sem("fillers")
        wt_psum, wt_sb = sem("wt_psum"), sem("wt_sb")
        ctxt_psum, ctxt_sb, ctxt2_sb = sem("ctxt_psum"), sem("ctxt_sb"), sem("ctxt2_sb")
        kv_psum, kv_sb = sem("kv_psum"), sem("kv_sb")
        kbd_ready, kbd_next, vbd_ready = sem("kbd_ready"), sem("kbd_next"), sem("vbd_ready")
        st1_done, mv1_done, ve1_done, rs1_done, xn_done = sem("st1_done"), sem("mv1_done"), sem("ve1_done"), sem("rs1_done"), sem("xn_done")
        xnt_psum, xnt_sb, qt_psum, qt_sb = sem("xnt_psum"), sem("xnt_sb"), sem("qt_psum"), sem("qt_sb")
        scores_done, max_done, shift_done, exp_done = sem("scores_done"), sem("max_done"), sem("shift_done"), sem("exp_done")
        sum_done, inv_done, probs_done = sem("sum_done"), sem("inv_done"), sem("probs_done")
        pt_psum, pt_sb, ot_psum, ot_sb = sem("pt_psum"), sem("pt_sb"), sem("ot_psum"), sem("ot_sb")
        att_psum, x1_done, x1s_done, x1_stored = sem("att_psum"), sem("x1_done"), sem("x1s_done"), sem("x1_stored")
        xbo_done, sbh_done, small_done = sem("xbo_done"), sem("sbh_done"), sem("small_done")
        st2_done, mv2_done, ve2_done, rs2_done = sem("st2_done"), sem("mv2_done"), sem("ve2_done"), sem("rs2_done")
        rows_done, rows2_done = sem("rows_done"), sem("rows2_done")
        x2t_psum, x2t_sb, x2t_stored = sem("x2t_psum"), sem("x2t_sb"), sem("x2t_stored")
        gates_psum, gates_sb, gates_done = sem("gates_psum"), sem("gates_sb"), sem("gates_done")
        acc_stored = sem("acc_stored")
        ids_done = sem("ids_done")
        route, ohs_ready, ranks_psum = sem("route"), sem("ohs_ready"), sem("ranks_psum")
        ranks_read, slots_ready, scattered, total_psum = sem("ranks_read"), sem("slots_ready"), [sem(f"scattered{i}") for i in range(NR)], sem("total_psum")
        block = es.enter_context(nc.Block())

        @block.sync
        def _(sp):
            for m, w in ((KEY, Wk), (QUERY, Wq), (VALUE, Wv), (OUT, Wo)):
                sp.dma_start(wraw[:, m], w.rearrange("(c p) e -> p c e", p=P)).then_inc(ld_w[m], 16)
            sp.dma_start(bo_bc[:], bo.partition_broadcast(P)).then_inc(ld_small, 16)
            sp.dma_start(rb_bc[:], rb.partition_broadcast(P)).then_inc(ld_small, 16)
            sp.dma_start(sb2_bc[:], sb2.partition_broadcast(P)).then_inc(ld_small, 16)
            sp.dma_start(rws[:], rw.rearrange("(c p) e -> p c e", p=P)).then_inc(ld_small, 16)
            for b in range(1, B):
                sp.dma_start(xres[:, b * TPB:(b + 1) * TPB], x[b].rearrange("(t p) d -> p t d", p=P)).then_inc(ld_x[b], 16)
            sp.dma_start(shared.sb1T[:], shared.sb1.rearrange("s (p c) -> p s c", p=P)).then_inc(shared.b1_in, 16)
            for n in range(PPE * NSH + RAW):
                shared.load_piece(sp, n)
            for g in range(2 * QA, NT):
                sp.wait_ge(x2t_sb, g + 1)
                sp.dma_start(xt_d[:, :, g * P:(g + 1) * P], x2T[:, :, g * P:(g + 1) * P]).then_inc(x2t_stored, 16)
            sp.wait_ge(x1s_done, NT)
            sp.dma_start(x1_d[2 * QA:NT].rearrange("t p d -> p t d"), xres[:, 2 * QA:NT]).then_inc(x1_stored, 16)
            for q in range(QA):
                sp.wait_ge(shared.acc_done, 2 * q + 2)
                sp.dma_start(acc_d[2 * q:2 * q + 2].rearrange("t p d -> p t d"), xres[:, 2 * q:2 * q + 2]).then_inc(acc_stored, 16)
            sp.wait_ge(x1_stored, 16)
            sp.wait_ge(x2t_stored, 16 * (NT - 2 * QA))
            sp.wait_ge(acc_stored, 16 * QA)

        @block.gpsimd
        def _(pool):
            pool.memset(ident[:], 0.0).then_inc(consts, 1)
            pool.memset(maskK[:], 1.0).then_inc(consts, 1)
            pool.memset(maskV[:], 1.0).then_inc(consts, 1)
            pool.memset(tri[:], 1.0).then_inc(consts, 1)
            pool.memset(ones[:], 1.0).then_inc(consts, 1)
            pool.memset(half[:], -0.5).then_inc(consts, 1)
            pool.memset(filler[:], 0.0).then_inc(consts, 1)
            pool.memset(rows[:, :, :, :, D:ROW], 0.0).then_inc(consts, 1)
            pool.wait_ge(consts, 8)
            pool.affine_select(out=ident[:], in_=ident[:], compare_op=ALU.not_equal, fill=1.0, base=0,
                               pattern=[[-1, P]], channel_multiplier=1).then_inc(consts, 1)
            pool.affine_select(out=tri[:], in_=tri[:], compare_op=ALU.is_ge, fill=0.0, base=-1,
                               pattern=[[1, P]], channel_multiplier=-1).then_inc(consts, 1)
            pool.affine_select(out=maskK[:], in_=maskK[:], compare_op=ALU.is_ge, fill=0.0, base=0,
                               pattern=[[-HD, HPC]], channel_multiplier=1).then_inc(consts, 1)
            pool.affine_select(out=maskV[:], in_=maskV[:], compare_op=ALU.is_ge, fill=0.0, base=0,
                               pattern=[[2 * L, 4], [-L, HPC]], channel_multiplier=1).then_inc(consts, 1)
            pool.iota(iota8[:], pattern=[[1, NE]], base=0, channel_multiplier=0,
                      allow_small_or_imprecise_dtypes=True).then_inc(consts, 1)
            pool.iota(ebase[:], pattern=[[CAP, NE]], base=0, channel_multiplier=0,
                      allow_small_or_imprecise_dtypes=True).then_inc(consts, 1)
            pool.iota(ids[:, 0, :], pattern=[[P, NT]], base=0, channel_multiplier=1).then_inc(consts, 1)
            pool.iota(ids[:, 1, :], pattern=[[P, NT]], base=TOK, channel_multiplier=1).then_inc(consts, 1)
            pool.iota(filler[:, D:D + 1].bitcast(I32), pattern=[[0, 1]], base=SKIP, channel_multiplier=1).then_inc(consts, 1)
            pool.wait_ge(consts, 17)
            pool.affine_select(out=maskK[:], in_=maskK[:], compare_op=ALU.is_ge, fill=0.0, base=HD - 1,
                               pattern=[[HD, HPC]], channel_multiplier=-1).then_inc(consts, 1)
            pool.affine_select(out=maskV[:], in_=maskV[:], compare_op=ALU.is_ge, fill=0.0, base=L - 1,
                               pattern=[[-2 * L, 4], [L, HPC]], channel_multiplier=-1).then_inc(consts, 1)
            pool.dma_start(xg_d[FILL_ROW:FILL_ROW + P, :], filler[:]).then_inc(fillers, 16)
            def rstd1(b):
                pool.wait_ge(ve1_done, TPB * (b + 1))
                pool.tensor_tensor(out=rs1[:, b * TPB:(b + 1) * TPB], in0=ve1[:, b * TPB:(b + 1) * TPB],
                                   in1=half[:].to_broadcast([P, TPB]), op=ALU.pow).then_inc(rs1_done, 1)

            rstd1(0)
            pool.wait_ge(kv_sb, 1)
            pool.wait_ge(consts, 19)
            pool.tensor_tensor(out=Kbd[:, 0, 0], in0=KT[:, 0, 0].unsqueeze(1).to_broadcast([P, HPC, L]),
                               in1=maskK[:].unsqueeze(2).to_broadcast([P, HPC, L]), op=ALU.mult).then_inc(kbd_ready, 1)
            pool.wait_ge(ld_small, 16 * 4)
            pool.tensor_tensor(out=sbh[:], in0=sb2_bc[:, 0], in1=sb2_bc[:, 1], op=ALU.add).then_inc(small_done, 1)
            pool.wait_ge(small_done, 1)
            pool.tensor_scalar(out=sbh[:], in0=sbh[:], scalar1=1.0 / NSH, scalar2=None, op0=ALU.mult).then_inc(small_done, 1)
            pool.wait_ge(small_done, 2)

            def residual(g):
                pool.wait_ge(rows_done, g + 1)
                pool.tensor_tensor(out=xres[:, g], in0=xres[:, g], in1=sbh[:], op=ALU.add).then_inc(x1s_done, 1)

            def scatter(b, t):
                for k in range(2):
                    pool.indirect_dma_start(xg_d, bass.IndirectOffsetOnAxis(ap=slots[:, b % 2, k, t:t + 1], axis=0),
                                            rows[:, b % NR, k, t, :], None).then_inc(scattered[b % NR], 16)

            def v_diagonal(b, c):
                pool.wait_ge(kv_sb, C + 1 + b // 2)
                if b >= 2:
                    pool.wait_ge(ot_psum, TPB * (b - 1))
                pool.tensor_tensor(out=Vbd[:, b % 2, 4 * c:4 * c + 4].rearrange("p j (h d) -> p j h d", d=HD),
                                   in0=Vsb[:, b, c * P:(c + 1) * P].rearrange("p (h d) -> p h d", d=HD).unsqueeze(1).to_broadcast([P, 4, HPC, HD]),
                                   in1=maskV[:].unsqueeze(3).to_broadcast([P, 4, HPC, HD]), op=ALU.mult).then_inc(vbd_ready, 1)
            for s in range(NT + LAST):
                if 5 <= s < NT + 5:
                    g = s - 5
                    pool.wait_ge(ve2_done, g + 1)
                    pool.tensor_tensor(out=rs2[:, g:g + 1], in0=ve2[:, g:g + 1], in1=half[:], op=ALU.pow).then_inc(rs2_done, 1)
                if s % TPB == 1 and s // TPB + 1 < B:
                    rstd1(s // TPB + 1)
                if 1 <= s <= NT:
                    g = s - 1
                    pool.wait_ge(inv_done, g + 1)
                    pool.tensor_tensor(out=Pr[:, g % 3], in0=Pr[:, g % 3], in1=inv[:, g % 2].unsqueeze(2).to_broadcast([P, NH, L]),
                                       op=ALU.mult).then_inc(probs_done, 1)
                if s < NT:
                    pool.wait_ge(xn_done, s + 1)
                    pool.tensor_tensor(out=xres[:, s], in0=xres[:, s], in1=bo_bc[:], op=ALU.add).then_inc(xbo_done, 1)
                if s % TPB == 3 and s // TPB + 1 < B:
                    v_diagonal(s // TPB + 1, 0)
                if s % TPB == 0 and s // TPB < B:
                    if s == 0:
                        v_diagonal(0, 0)
                    v_diagonal(s // TPB, 1)
                if 2 <= s < 2 + PPE * NSH:
                    n = s - 2
                    shared.split_low(pool, n, shared.part(shared.s_hi, n, 0), shared.part(shared.s_lo, n, 0))
                if s >= NT - 3:
                    for g in range(2 * (s - NT + 3), min(2 * (s - NT + 4), NT)):
                        residual(g)
                if s >= 7 + 3:
                    b, t = (s - 10) // TPB, (s - 10) % TPB
                    if t == 0:
                        if b >= NR:
                            pool.wait_ge(scattered[b % NR], 16 * 2 * TPB * (b // NR))
                        pool.tensor_copy(rows[:, b % NR, :, :, D].bitcast(I32), ids[:, :, b * TPB:(b + 1) * TPB]).then_inc(ids_done, 1)
                        pool.wait_ge(ids_done, b + 1)
                        pool.wait_ge(slots_ready, b + 1)
                        pool.wait_ge(rows2_done, TPB * (b + 1))
                    if b < B - 1:
                        scatter(b, t)
                    elif t == 0:
                        for t in range(TPB):
                            scatter(b, t)
            for i in range(NR):
                pool.wait_ge(scattered[i], 16 * 2 * TPB * len(range(i, B, NR)))
            pool.wait_ge(fillers, 16)

        @block.scalar
        def _(act):
            nc.scalar.dma_start(craw[:], ctx.rearrange("(r b) k e -> (b k) r e", b=2)).then_inc(ld_c, 16)
            nc.scalar.dma_start(xres[:, 0:TPB], x[0].rearrange("(t p) d -> p t d", p=P)).then_inc(ld_x[0], 16)
            act.wait_ge(consts, 8)
            nc.scalar.activation(warm[:], half[:], ACT.Copy)
            def weight(n, m):
                act.wait_ge(wt_psum, n + 1)
                nc.scalar.activation(WT[:, m], psW[:, m].rearrange("p (c f) -> p c f", c=C), ACT.Copy).then_inc(wt_sb, 1)

            weight(0, KEY)
            act.wait_ge(ctxt_psum, 1)
            nc.scalar.activation(ctxT[:], psA[:, :].rearrange("p (c n) -> p c n", c=C), ACT.Copy).then_inc(ctxt_sb, 1)
            weight(1, QUERY)
            act.wait_ge(ctxt_sb, 1)
            for c in range(C):
                nc.scalar.activation(ctxT2[:, c], ctxT[:, c].rearrange("p (b k) -> p b k", b=B).unsqueeze(2).to_broadcast([P, B, 2, L]),
                                     ACT.Copy).then_inc(ctxt2_sb, 1)
            act.wait_ge(kv_psum, 1)
            for c in range(C):
                nc.scalar.activation(KT[:, c], psP[:, 4 * c:4 * c + 2].rearrange("p a (b k) -> p (a b) k", k=L), ACT.Copy, scale=float(HD) ** -0.5).then_inc(kv_sb, 1)
            def xnt_evac(g):
                act.wait_ge(xnt_psum, g + 1)
                if g >= 2:
                    act.wait_ge(qt_psum, g - 1)
                nc.scalar.activation(xnT[:, g % 2], psA[:, 0:D].rearrange("p (c n) -> p c n", c=C), ACT.Copy).then_inc(xnt_sb, 1)

            def qt_evac(g):
                act.wait_ge(qt_psum, g + 1)
                if g >= 2:
                    act.wait_ge(scores_done, g - 1)
                nc.scalar.activation(QT[:, g % 2], psA[:, D:2 * D].rearrange("p (c n) -> p c n", c=C), ACT.Copy).then_inc(qt_sb, 1)

            def values_evac(i):
                act.wait_ge(kv_psum, 2 + i)
                nc.scalar.activation(Vsb[:, 2 * i:2 * i + 2], psP[:, 4 * i:4 * i + 4].rearrange("p (b a) n -> p b (a n)", b=2), ACT.Copy).then_inc(kv_sb, 1)

            def keys_diagonal(b, i):
                for n in range(i * NH // TPB, (i + 1) * NH // TPB):
                    c, h = n // HPC, n % HPC
                    nc.scalar.activation(Kbd[:, b % 2, c, h], KT[:, c, b], ACT.Copy, scale=maskK[:, h:h + 1]).then_inc(kbd_next, 1)

            weight(2, VALUE)
            xnt_evac(0)
            qt_evac(0)
            weight(3, OUT)
            act.wait_ge(kv_sb, C)
            for i in range(TPB):
                keys_diagonal(1, i)
            values_evac(0)
            for s in range(NT + LAST):
                if s == 1:
                    values_evac(1)
                if s + 1 < NT:
                    xnt_evac(s + 1)
                if 6 <= s < NT + 6:
                    g = s - 6
                    act.wait_ge(gates_psum, g + 1)
                    if g >= TPB:
                        act.wait_ge(gates_done, g // TPB)
                    nc.scalar.activation(gates[:, 0, g % TPB], psA[:, D:D + NE], ACT.Copy).then_inc(gates_sb, 1)
                if s == NT:
                    nc.scalar.activation(warm[:], half[:], ACT.Gelu)
                if s + 1 < NT:
                    qt_evac(s + 1)
                if 2 <= s // TPB + 1 < B:
                    act.wait_ge(scores_done, TPB * (s // TPB))
                    keys_diagonal(s // TPB + 1, s % TPB)
                if 2 <= s < 2 + PPE * NSH:
                    n = s - 2
                    shared.split_high(act, n, shared.part(shared.s_hi, n, 0))
                if s < NT:
                    act.wait_ge(shift_done, s + 1)
                    nc.scalar.activation(Pr[:, s % 3], Pr[:, s % 3], ACT.Exp).then_inc(exp_done, 1)
                if 3 <= s < NT + 3:
                    g = s - 3
                    act.wait_ge(ot_psum, g + 1)
                    if g >= 2:
                        act.wait_ge(att_psum, g - 1)
                    nc.scalar.activation(OT[:, g % 2], psA[:, D:2 * D].rearrange("p (c n) -> p c n", c=C), ACT.Copy).then_inc(ot_sb, 1)
                if 2 <= s < NT + 2:
                    g = s - 2
                    act.wait_ge(pt_psum, g + 1)
                    if g >= 2:
                        act.wait_ge(ot_psum, g - 1)
                    nc.scalar.activation(PT[:, g % 2], psP[:], ACT.Copy).then_inc(pt_sb, 1)
                if 5 <= s < NT + 5:
                    g = s - 5
                    b, t = g // TPB, g % TPB
                    act.wait_ge(rows_done, g + 1)
                    if b >= NR and t == 0:
                        act.wait_ge(scattered[b % NR], 16 * 2 * TPB * (b // NR))
                    nc.scalar.activation(rows[:, b % NR, 1, t, 0:D], rows[:, b % NR, 0, t, 0:D], ACT.Copy).then_inc(rows2_done, 1)
                    act.wait_ge(x2t_psum, g + 1)
                    nc.scalar.activation(x2T[:, :, g * P:(g + 1) * P], psA[:, 0:D].rearrange("p (c n) -> p c n", c=C), ACT.Copy).then_inc(x2t_sb, 1)
                for q in range(QA + 2):
                    if s == x_step(q):
                        act.wait_ge(x2t_sb, 2 * q + 2)
                        shared.scalar_x(act, q, x2T[:, :, q * HALF:(q + 1) * HALF])
                if s >= NT and (s - NT) % 2 == 0:
                    if s == NT:
                        act.wait_ge(shared.b1_in, 16)
                    for e in range(NSH):
                        shared.scalar_hidden(act, (s - NT) // 2, e, h_banks if s == NT else more_h_banks)

        @block.vector
        def _(dve):
            def stats(g):
                b = g // TPB
                if g % TPB == 0:
                    dve.wait_ge(ld_x[b], 16)
                nc.vector.bn_stats(st1[:, g], xres[:, g]).then_inc(st1_done, 1)

            def norm1(g):
                dve.wait_ge(rs1_done, g // TPB + 1)
                if g >= 2:
                    dve.wait_ge(xnt_psum, g - 1)
                nc.vector.tensor_scalar(out=xn[:, g % 2], in0=xres[:, g], scalar1=mv1[:, g, 0:1], scalar2=rs1[:, g:g + 1],
                                        op0=ALU.subtract, op1=ALU.mult).then_inc(xn_done, 1)

            def aggregate(g):
                dve.wait_ge(st1_done, g + 1)
                nc.vector.bn_aggr(mv1[:, g], st1[:, g]).then_inc(mv1_done, 1)
                dve.wait_ge(mv1_done, g + 1)
                nc.vector.tensor_scalar(out=ve1[:, g:g + 1], in0=mv1[:, g, 1:2], scalar1=EPS, scalar2=None, op0=ALU.add).then_inc(ve1_done, 1)

            for g in range(TPB):
                stats(g)
            for g in range(TPB):
                dve.wait_ge(st1_done, g + 1)
                nc.vector.bn_aggr(mv1[:, g], st1[:, g]).then_inc(mv1_done, 1)
            dve.wait_ge(mv1_done, TPB)
            nc.vector.tensor_scalar(out=ve1[:, 0:TPB], in0=mv1[:, 0:TPB, 1], scalar1=EPS, scalar2=None, op0=ALU.add).then_inc(ve1_done, TPB)
            norm1(0)
            norm1(1)
            dve.wait_ge(kv_sb, 2)
            dve.wait_ge(consts, 19)
            nc.vector.tensor_tensor(out=Kbd[:, 0, 1], in0=KT[:, 1, 0].unsqueeze(1).to_broadcast([P, HPC, L]),
                                    in1=maskK[:].unsqueeze(2).to_broadcast([P, HPC, L]), op=ALU.mult).then_inc(kbd_ready, 1)
            for g in range(TPB, AHEAD + 1):
                stats(g)
            for g in range(TPB, AHEAD):
                aggregate(g)

            routed = [0]

            def chain(ins):
                routed[0] += 1
                ins.then_inc(route, 1)
                dve.wait_ge(route, routed[0])

            chain(nc.vector.memset(ohc[:, 0], 0.0))

            def choose(b):
                dve.wait_ge(gates_sb, TPB * (b + 1))
                if b == 0:
                    dve.wait_ge(ld_small, 16 * 4)
                nc.vector.tensor_tensor(out=gates[:, 1], in0=gates[:, 0], in1=rb_bc[:].unsqueeze(1).to_broadcast([P, TPB, NE]),
                                        op=ALU.add).then_inc(gates_done, 1)
                dve.wait_ge(gates_done, b + 1)
                for t in range(TPB):
                    ins = nc.vector.max(out=top[:, t], in_=gates[:, 1, t])
                chain(ins)
                for t in range(TPB):
                    ins = nc.vector.max_index(out=topi[:, t], in_max=top[:, t], in_values=gates[:, 1, t])
                chain(ins)
                nc.vector.tensor_tensor(out=gap[:, b * TPB:(b + 1) * TPB], in0=top[:, :, 1], in1=top[:, :, 0], op=ALU.subtract).then_inc(metas, 1)
                chain(nc.vector.tensor_copy(topf[:].rearrange("p k t -> p t k"), topi[:, :, 0:2]))
                for k in range(2):
                    ins = nc.vector.tensor_tensor(out=oh[:, k], in0=iota8[:].unsqueeze(1).to_broadcast([P, TPB, NE]),
                                                  in1=topf[:, k].unsqueeze(2).to_broadcast([P, TPB, NE]), op=ALU.is_equal)
                chain(ins)
                chain(nc.vector.tensor_tensor(out=ohs[:, b * TPB:(b + 1) * TPB], in0=oh[:, 0], in1=oh[:, 1], op=ALU.add))
                for t in range(TPB):
                    ins = nc.vector.tensor_tensor(out=ohc[:, t + 1], in0=ohc[:, t], in1=ohs[:, b * TPB + t], op=ALU.add)
                    if t < TPB - 1:
                        chain(ins)
                ins.then_inc(ohs_ready, 1)

            def place(b):
                dve.wait_ge(ranks_psum, b + 1)
                nc.vector.tensor_tensor(out=rk[:], in0=psD[:, 384:384 + TPB * NE].rearrange("p (t e) -> p t e", e=NE),
                                        in1=ebase[:].unsqueeze(1).to_broadcast([P, TPB, NE]), op=ALU.add).then_inc(ranks_read, 1)
                dve.wait_ge(ranks_read, b + 1)
                for k in range(2):
                    ins = nc.vector.tensor_tensor(out=pk[:, k], in0=oh[:, k], in1=rk[:], op=ALU.mult)
                chain(ins)
                chain(nc.vector.reduce_sum(slotf[:], pk[:], axis=AX.X))
                if b >= 2:
                    dve.wait_ge(scattered[(b - 2) % NR], 16 * 2 * TPB * ((b - 2) // NR + 1))
                nc.vector.tensor_copy(slots[:, b % 2], slotf[:]).then_inc(slots_ready, 1)
                if b + 1 < B:
                    chain(nc.vector.tensor_copy(ohc[:, 0], ohc[:, TPB]))

            for s in range(NT + LAST):
                if s < NT:
                    dve.wait_ge(scores_done, s + 1)
                    v = psS[:, s % 2].rearrange("p c (h k) -> p (c h) k", k=L)
                    nc.vector.reduce_max(mx[:, s % 2], v, axis=AX.X).then_inc(max_done, 1)
                if 4 <= s < NT + 4:
                    g = s - 4
                    dve.wait_ge(att_psum, g + 1)
                    dve.wait_ge(xbo_done, g + 1)
                    nc.vector.tensor_tensor(out=xres[:, g], in0=psD[:, 0:D], in1=xres[:, g], op=ALU.add).then_inc(x1_done, 1)
                if s < NT:
                    if s >= 3:
                        dve.wait_ge(pt_psum, s - 2)
                    dve.wait_ge(max_done, s + 1)
                    nc.vector.tensor_tensor(out=Pr[:, s % 3], in0=v, in1=mx[:, s % 2].unsqueeze(2).to_broadcast([P, NH, L]),
                                            op=ALU.subtract).then_inc(shift_done, 1)
                if 5 <= s < NT + 5:
                    g = s - 5
                    b, t = g // TPB, g % TPB
                    dve.wait_ge(rs2_done, g + 1)
                    if b >= NR and t == 0:
                        dve.wait_ge(scattered[b % NR], 16 * 2 * TPB * (b // NR))
                    nc.vector.tensor_scalar(out=rows[:, b % NR, 0, t, 0:D], in0=xres[:, g], scalar1=mv2[:, g, 0:1],
                                            scalar2=rs2[:, g:g + 1], op0=ALU.subtract, op1=ALU.mult).then_inc(rows_done, 1)
                if s + 2 < NT:
                    norm1(s + 2)
                if 4 <= s < NT + 4:
                    g = s - 4
                    dve.wait_ge(x1_done, g + 1)
                    nc.vector.bn_stats(st2[:, g], xres[:, g]).then_inc(st2_done, 1)
                if s + AHEAD < NT:
                    aggregate(s + AHEAD)
                if s < NT:
                    dve.wait_ge(exp_done, s + 1)
                    nc.vector.reduce_sum(sm[:, s % 2], Pr[:, s % 3], axis=AX.X).then_inc(sum_done, 1)
                if 4 <= s < NT + 4:
                    dve.wait_ge(st2_done, g + 1)
                    nc.vector.bn_aggr(mv2[:, g], st2[:, g]).then_inc(mv2_done, 1)
                if s + AHEAD + 1 < NT:
                    stats(s + AHEAD + 1)
                if s < NT:
                    dve.wait_ge(sum_done, s + 1)
                    if s >= 2:
                        dve.wait_ge(probs_done, s - 1)
                    nc.vector.reciprocal(inv[:, s % 2], sm[:, s % 2]).then_inc(inv_done, 1)
                if 4 <= s < NT + 4:
                    dve.wait_ge(mv2_done, g + 1)
                    nc.vector.tensor_scalar(out=ve2[:, g:g + 1], in0=mv2[:, g, 1:2], scalar1=EPS, scalar2=None, op0=ALU.add).then_inc(ve2_done, 1)
                if s >= 7 + 3 and (s - 7) % TPB == 3:
                    place((s - 7) // TPB)
                if 6 <= s < NT + 6 and (s - 6) % TPB == TPB - 1:
                    choose((s - 6) // TPB)
                for q in range(QA + 2):
                    if s == x_step(q):
                        dve.wait_ge(x2t_sb, 2 * q + 2)
                        shared.vector_x(dve, q, x2T[:, :, q * HALF:(q + 1) * HALF])
                if s > NT and (s - NT) % 2 == 0:
                    q = (s - NT) // 2 - 1
                    dve.wait_ge(x1s_done, 2 * q + 2)
                    own = [xres[:, 2 * q + u] for u in range(2)]
                    shared.vector_output(dve, q, y_banks, own, own)
                if s >= NT and (s - NT) % 2 == 0:
                    for e in range(NSH):
                        for c in range(HC):
                            shared.vector_hidden(dve, (s - NT) // 2, e, c)
            dve.wait_ge(total_psum, 1)
            nc.vector.tensor_copy(counts[:], psD[:, 0:NE]).then_inc(metas, 1)

        @block.tensor
        def _(pe):
            pe.wait_ge(consts, 17)
            def weight(m):
                pe.wait_ge(ld_w[m], 16)
                for c in range(C):
                    for f in range(C):
                        last = nc.tensor.transpose(psW[:, m, c * D + f * P:c * D + (f + 1) * P], wraw[:, m, f, c * P:(c + 1) * P], ident[:])
                last.then_inc(wt_psum, 1)

            weight(KEY)
            pe.wait_ge(ld_c, 16)
            for c in range(C):
                for r in range(C):
                    last = nc.tensor.transpose(psA[:, c * 256 + r * P:c * 256 + (r + 1) * P], craw[:, r, c * P:(c + 1) * P], ident[:])
            last.then_inc(ctxt_psum, 1)
            weight(QUERY)
            pe.wait_ge(ctxt_sb, 1)
            pe.wait_ge(wt_sb, 1)
            for f in range(C):
                for c in range(C):
                    last = nc.tensor.matmul(psP[:, 4 * f:4 * f + 2].rearrange("p a n -> p (a n)"), WT[:, KEY, c, f * P:(f + 1) * P], ctxT[:, c],
                                            start=(c == 0), stop=(c == C - 1))
            last.then_inc(kv_psum, 1)
            weight(VALUE)
            weight(OUT)

            def xn_transpose(g):
                pe.wait_ge(xn_done, g + 1)
                for c in range(C):
                    last = nc.tensor.transpose(psA[:, c * P:(c + 1) * P], xn[:, g % 2, c * P:(c + 1) * P], ident[:])
                last.then_inc(xnt_psum, 1)

            def queries(g):
                pe.wait_ge(xnt_sb, g + 1)
                for f in range(C):
                    for c in range(C):
                        last = nc.tensor.matmul(psA[:, D + f * P:D + (f + 1) * P], WT[:, QUERY, c, f * P:(f + 1) * P], xnT[:, g % 2, c],
                                                start=(c == 0), stop=(c == C - 1))
                last.then_inc(qt_psum, 1)

            pe.wait_ge(wt_sb, 2)
            xn_transpose(0)
            queries(0)

            def scores(g, c):
                b = g // TPB
                if g % TPB == 0 and c == 0:
                    if b == 0:
                        pe.wait_ge(kbd_ready, C)
                    else:
                        pe.wait_ge(kbd_next, D // HD * b)
                if c == 0:
                    pe.wait_ge(qt_sb, g + 1)
                    if g >= 2:
                        pe.wait_ge(shift_done, g - 1)
                last = nc.tensor.matmul(psS[:, g % 2, c], QT[:, g % 2, c], Kbd[:, b % 2, c].rearrange("p h k -> p (h k)"),
                                        start=True, stop=True)
                if c == C - 1:
                    last.then_inc(scores_done, 1)

            def values(i):
                for b in range(2 * i, 2 * i + 2):
                    for c in range(C):
                        last = nc.tensor.matmul(psP[:, 2 * b:2 * b + 2].rearrange("p a n -> p (a n)"), ctxT2[:, c, b].rearrange("p a k -> p (a k)"), WT[:, VALUE, c],
                                                start=(c == 0), stop=(c == C - 1))
                last.then_inc(kv_psum, 1)

            for c in range(C):
                scores(0, c)
            pe.wait_ge(ctxt2_sb, C)
            pe.wait_ge(kv_sb, C)
            pe.wait_ge(wt_sb, 4)
            values(0)
            for s in range(NT + LAST):
                if s == 1:
                    values(1)
                if s + 1 < NT or 6 <= s < NT + 6:
                    if s >= 6:
                        pe.wait_ge(x2t_sb, s - 5)
                    elif s >= 4:
                        pe.wait_ge(ot_sb, s - 3)
                if 6 <= s < NT + 6:
                    g = s - 6
                    if g == 0:
                        pe.wait_ge(ld_small, 16 * 4)
                    for c in range(C):
                        last = nc.tensor.matmul(psA[:, D:D + NE], x2T[:, c, g * P:(g + 1) * P], rws[:, c], start=(c == 0), stop=(c == C - 1))
                    last.then_inc(gates_psum, 1)
                if s + 1 < NT:
                    pe.wait_ge(qt_sb, s + 1)
                    xn_transpose(s + 1)
                if 4 <= s < NT + 4:
                    g = s - 4
                    pe.wait_ge(ot_sb, g + 1)
                    if g >= 1:
                        pe.wait_ge(x1_done, g)
                    if s >= 8 + 3 and (s - 8) % TPB == 3:
                        pe.wait_ge(ranks_read, (s - 8) // TPB + 1)
                    for c in range(C):
                        last = nc.tensor.matmul(psD[:, 0:D], OT[:, g % 2, c], WT[:, OUT, c], start=(c == 0), stop=(c == C - 1))
                    last.then_inc(att_psum, 1)
                if s + 1 < NT:
                    if s >= 6:
                        pe.wait_ge(gates_sb, s - 5)
                    queries(s + 1)
                if 2 <= s < NT + 2:
                    g = s - 2
                    pe.wait_ge(probs_done, g + 1)
                    if g == 0:
                        pe.wait_ge(kv_sb, C + 2)
                    else:
                        pe.wait_ge(pt_sb, g)
                    for j in range(NJ):
                        last = nc.tensor.transpose(psP[:, j], Pr[:, g % 3, 2 * j:2 * j + 2].rearrange("p h k -> p (h k)"), ident[:])
                    last.then_inc(pt_psum, 1)
                if 3 <= s < NT + 3:
                    g = s - 3
                    b = g // TPB
                    if g % TPB == 0:
                        pe.wait_ge(vbd_ready, C * (b + 1))
                    pe.wait_ge(pt_sb, g + 1)
                    pe.wait_ge(qt_sb, min(s + 2, NT))
                    if s >= 6:
                        pe.wait_ge(gates_sb, s - 5)
                    for c in range(C):
                        for j in range(4):
                            last = nc.tensor.matmul(psA[:, D + c * P:D + (c + 1) * P], Vbd[:, b % 2, 4 * c + j], PT[:, g % 2, 4 * c + j],
                                                    start=(j == 0), stop=(j == 3))
                    last.then_inc(ot_psum, 1)
                if s >= 7 + 3 and (s - 7) % TPB == 3:
                    b = (s - 7) // TPB
                    pe.wait_ge(ohs_ready, b + 1)
                    pe.wait_ge(x1_done, min(s - 3, NT))
                    for t in range(TPB):
                        o = psD[:, 384 + t * NE:384 + (t + 1) * NE]
                        nc.tensor.matmul(o, tri[:], ohs[:, b * TPB + t], start=True, stop=False)
                        last = nc.tensor.matmul(o, ones[:], ohc[:, t], start=False, stop=True)
                    last.then_inc(ranks_psum, 1)
                if s + 1 < NT:
                    scores(s + 1, 0)
                if 5 <= s < NT + 5:
                    g = s - 5
                    b, t = g // TPB, g % TPB
                    pe.wait_ge(rows_done, g + 1)
                    pe.wait_ge(ot_sb, min(s - 2, NT))
                    if s >= 6:
                        pe.wait_ge(gates_sb, s - 5)
                    for c in range(C):
                        last = nc.tensor.transpose(psA[:, c * P:(c + 1) * P], rows[:, b % NR, 0, t, c * P:(c + 1) * P], ident[:])
                    last.then_inc(x2t_psum, 1)
                if s + 1 < NT:
                    scores(s + 1, 1)
                if s >= NT:
                    if s == NT:
                        pe.wait_ge(shift_done, NT)
                    if (s - NT) % 2 == 0:
                        if s == NT + 2:
                            pe.wait_ge(pt_sb, NT)
                        shared.tensor_hidden(pe, (s - NT) // 2, h_banks if s == NT else more_h_banks, fresh=s == NT + 2)
                    else:
                        shared.tensor_output(pe, (s - NT) // 2, y_banks)
            pe.wait_ge(slots_ready, B)
            nc.tensor.matmul(psD[:, 0:NE], ones[:], ohc[:, TPB], start=True, stop=True).then_inc(total_psum, 1)


def shared_experts(nc, b1, keep, scratch, shared):
    b1T, b1_in, xg, xg_in, acc_out, w_hi, w_lo, counts, row_tab, exp_tab, tabs_ready = keep
    x1_d, xt_d, xg_d, acc_d = scratch
    with ExitStack() as es:
        def sb(name, shape, dt=F32):
            return es.enter_context(nc.sbuf_tensor(name, shape, dt))

        def sem(name):
            return es.enter_context(nc.semaphore(name))

        xt = sb("xt", [P, 2, C, HALF])
        acc = sb("acc", [P, 2, 2, D])
        filler = sb("filler2", [P, ROW])
        tile_f = sb("tile_f", [1, TILES])
        ntf = sb("ntf", [1, NE])
        nti = sb("nti", [1, 2, NE], I32)
        cum = sb("cum", [1, NE])
        onef = sb("onef", [1, NE])
        past = sb("past", [1, 2, NE, TILES])
        exp_f = sb("exp_f", [1, TILES])
        row_f = sb("row_f", [1, 3, TILES])
        fill_f = sb("fill_f", [1, 2, NE])
        fill_i = sb("fill_i", [1, NE], I32)
        psH = es.enter_context(nc.psum_tensor("psH", [P, 4, 512], F32))
        psY = es.enter_context(nc.psum_tensor("psY", [P, 4, 512], F32))
        h_banks = [psH[:, i, 0:HALF] for i in range(4)]
        y_banks = [[psY[:, 2 * i + u, 0:D] for u in range(2)] for i in range(2)]

        xt_in = [sem(f"xt_in{i}") for i in range(2)]
        acc_in = [sem(f"acc_in{i}") for i in range(2)]
        cst, tab, fill_ready, fill_out = sem("cst"), sem("tab"), sem("fill_ready"), sem("fill_out")
        block = es.enter_context(nc.Block())

        FIRST, PIECES = PPE * NSH, PPE * (NSH + NE)
        STEPS = NQ - QA

        def target(w, n):
            return shared.part(w, n, NSH)

        @block.sync
        def _(sp):
            for j in range(2, STEPS):
                sp.dma_start(xt[:, j % 2], xt_d[:, :, (QA + j) * HALF:(QA + j + 1) * HALF]).then_inc(xt_in[j % 2], 16)
            for n in range(FIRST + RAW, PIECES):
                shared.load_piece(sp, n)
                if n % 2 and n >= PIECES - 2 * NE - 4 and n < PIECES - 4:
                    e = (n - PIECES + 2 * NE + 4) // 2
                    sp.wait_ge(fill_ready, 1)
                    sp.wait_ge(cst, 4)
                    r = sp.value_load(fill_i[0:1, e:e + 1], min_val=0, max_val=FILL_ROW - P)
                    sp.dma_start(xg_d[bass.ds(r, P), :], filler[:]).then_inc(fill_out, 16)
            sp.dma_start(b1T[:], b1.rearrange("e (p c) -> p e c", p=P)).then_inc(b1_in, 16)
            sp.wait_ge(fill_out, 16 * NE)
            sp.wait_ge(tabs_ready, 2)
            for t in range(EARLY):
                for i in range(t * ROW // PIECE, ((t + 1) * ROW - 1) // PIECE + 1):
                    sp.wait_ge(shared.lo_done[i], PIECES // RAW)
                r = sp.value_load(row_tab[0:1, t:t + 1], min_val=0, max_val=FILL_ROW)
                sp.dma_start(xg[:, t], xg_d[bass.ds(r, P), :]).then_inc(xg_in[t], 16)

        @block.gpsimd
        def _(pool):
            pool.memset(filler[:], 0.0).then_inc(cst, 1)
            pool.memset(onef[:], 1.0).then_inc(cst, 1)
            pool.iota(tile_f[:], pattern=[[1, TILES]], base=0, channel_multiplier=0,
                      allow_small_or_imprecise_dtypes=True).then_inc(cst, 1)
            pool.wait_ge(cst, 3)
            pool.iota(filler[:, D:D + 1].bitcast(I32), pattern=[[0, 1]], base=SKIP, channel_multiplier=1).then_inc(cst, 1)
            for n in range(FIRST, PIECES):
                if n % RAW < RAW - 1:
                    shared.split_low(pool, n, target(w_hi, n), target(w_lo, n))

        @block.scalar
        def _(act):
            def load_acc(j):
                if j >= 2:
                    act.wait_ge(acc_out[j % 2], 16 * (j // 2))
                t = 2 * (QA + j)
                nc.scalar.dma_start(acc[:, j % 2], x1_d[t:t + 2].rearrange("t p d -> p t d")).then_inc(acc_in[j % 2], 16)

            def store_acc(j):
                act.wait_ge(shared.acc_done, 2 * (QA + j + 1))
                t = 2 * (QA + j)
                nc.scalar.dma_start(acc_d[t:t + 2].rearrange("t p d -> p t d"), acc[:, j % 2]).then_inc(acc_out[j % 2], 16)

            def split_x(j):
                act.wait_ge(xt_in[j % 2], 16)
                shared.scalar_x(act, QA + j, xt[:, j % 2])

            load_acc(0)
            load_acc(1)
            for j in range(1, STEPS):
                for s in range(NSH):
                    shared.scalar_hidden(act, QA + j, s, h_banks)
                    if s == 0 and 2 <= j + 1 < STEPS:
                        split_x(j + 1)
                    if s == 0:
                        store_acc(j - 1)
                    if s == 1 and j + 1 < STEPS:
                        load_acc(j + 1)
            store_acc(STEPS - 1)

        @block.vector
        def _(dve):
            steps = [0]

            def chain(ins):
                steps[0] += 1
                ins.then_inc(tab, 1)
                dve.wait_ge(tab, steps[0])

            V = nc.vector
            pieces = iter(range(FIRST, PIECES))

            def split(count):
                for _ in range(count):
                    n = next(pieces)
                    dve.wait_ge(shared.raw_in[n % RAW], 16 * (n // RAW + 1))
                    V.tensor_copy(target(w_hi, n), shared.raw[:, n % RAW]).then_inc(shared.hi_done[n % RAW], 1)
                    if n % RAW == RAW - 1:
                        shared.split_low(dve, n, target(w_hi, n), target(w_lo, n))

            split(4)
            dve.wait_ge(cst, 4)
            chain(V.tensor_scalar(out=nti[:, 0], in0=counts[0:1, :], scalar1=float(P - 1), scalar2=None, op0=ALU.add))
            chain(V.tensor_scalar(out=nti[:, 1], in0=nti[:, 0], scalar1=P.bit_length() - 1, scalar2=None, op0=ALU.arith_shift_right))
            chain(V.tensor_copy(ntf[:], nti[:, 1]))
            chain(V.tensor_tensor_scan(out=cum[:], data0=onef[:], data1=ntf[:], initial=0.0, op0=ALU.mult, op1=ALU.add))
            V.tensor_scalar(out=fill_f[:, 0], in0=tile_f[:, 0:NE], scalar1=float(CAP), scalar2=None, op0=ALU.mult)
            chain(V.tensor_tensor(out=past[:, 0], in0=tile_f[:].unsqueeze(1).to_broadcast([1, NE, TILES]),
                                  in1=cum[:].unsqueeze(2).to_broadcast([1, NE, TILES]), op=ALU.is_ge))
            V.tensor_tensor(out=fill_f[:, 1], in0=fill_f[:, 0], in1=counts[0:1, :], op=ALU.add)
            V.tensor_tensor(out=past[:, 1], in0=past[:, 0], in1=ntf[:].unsqueeze(2).to_broadcast([1, NE, TILES]), op=ALU.mult)
            chain(V.reduce_sum(exp_f[:], past[:, 0, 0:NE - 1].rearrange("p e t -> p t e"), axis=AX.X))
            V.tensor_copy(fill_i[:], fill_f[:, 1]).then_inc(fill_ready, 1)
            chain(V.reduce_sum(row_f[:, 0], past[:, 1, 0:NE - 1].rearrange("p e t -> p t e"), axis=AX.X))
            chain(V.tensor_tensor(out=row_f[:, 1], in0=tile_f[:], in1=row_f[:, 0], op=ALU.subtract))
            chain(V.tensor_scalar(out=row_f[:, 2], in0=exp_f[:], scalar1=float(CAP), scalar2=None, op0=ALU.mult))
            chain(V.scalar_tensor_tensor(out=row_f[:, 0], in0=row_f[:, 1], scalar=float(P), in1=row_f[:, 2], op0=ALU.mult, op1=ALU.add))
            chain(V.tensor_scalar(out=row_f[:, 1], in0=row_f[:, 0], scalar1=-1.0, scalar2=float(FILL_ROW), op0=ALU.mult, op1=ALU.add))
            chain(V.tensor_tensor(out=row_f[:, 2], in0=row_f[:, 1], in1=past[:, 0, NE - 1], op=ALU.mult))
            chain(V.tensor_tensor(out=row_f[:, 1], in0=row_f[:, 0], in1=row_f[:, 2], op=ALU.add))
            V.tensor_copy(row_tab[:], row_f[:, 1]).then_inc(tabs_ready, 1)
            V.tensor_copy(exp_tab[:], exp_f[:]).then_inc(tabs_ready, 1)
            split(4)
            for j in range(STEPS):
                q = QA + j
                for s in range(NSH if j else 0):
                    for c in range(HC):
                        shared.vector_hidden(dve, q, s, c)
                        if c % 2:
                            split(1)
                    if s == 0 and 2 <= j + 1 < STEPS:
                        shared.vector_x(dve, q + 1, xt[:, (j + 1) % 2])
                if j:
                    split(4 if j < STEPS - 1 else 2)
                dve.wait_ge(acc_in[j % 2], 16 * (j // 2 + 1))
                own = [acc[:, j % 2, u] for u in range(2)]
                shared.vector_output(dve, q, y_banks, own, own)
            split(2)

        @block.tensor
        def _(pe):
            for q in range(QA, NQ):
                if q > QA:
                    shared.tensor_hidden(pe, q, h_banks)
                shared.tensor_output(pe, q, y_banks)


def routed_experts(nc, ios, keep, scratch, out):
    b2 = ios
    ident, b1T, b1_in, xg, xg_in, acc_out, w_hi, w_lo, gap, row_tab, exp_tab, tabs_ready = keep
    xg_d, acc_d, y_d = scratch
    with ExitStack() as es:
        def sb(name, shape, dt=F32):
            return es.enter_context(nc.sbuf_tensor(name, shape, dt))

        def sem(name):
            return es.enter_context(nc.semaphore(name))

        ain = sb("ain", [P, NT, D])
        ge = sb("ge", [P, 2, NT])
        p12 = sb("p12", [P, 2, NT])
        yin = sb("yin", [P, NT - 8, 2, D])
        work = sb("work", [P, 8, 2, D])
        b2_bc = sb("b2_bc", [P, NE, D])
        NYB, NX = 4, 3
        x_hi = sb("x_hi", [P, NX, C, P], F32R)
        x_lo = sb("x_lo", [P, NX, C, P], F32R)
        hpre = work[:, 0:2].rearrange("p t k d -> p t (k d)")
        hb = work[:, 2:4].rearrange("p t k (c n) -> p t (k c) n", n=P)
        g = work[:, 4:6].rearrange("p t k (c n) -> p t (k c) n", n=P)
        y = work[:, 6:8].rearrange("p t k d -> p (t k) d")

        def results(t):
            return work[:, t] if t < 8 else yin[:, t - 8]

        h_hi = sb("hh_hi", [P, 2, HC, P], F32R)
        h_lo = sb("hh_lo", [P, 2, HC, P], F32R)
        ps = es.enter_context(nc.psum_tensor("ps3", [P, 8, 512], F32))

        y_out = [sem(f"y_out{i}") for i in range(NXB)]
        small = sem("b2_in")
        exp2_done, weights = sem("exp2_done"), sem("weights")
        xt_psum, xhi_done, xlo_done = sem("xt_psum"), sem("xhi3"), sem("xlo3")
        hid_psum, hpre_done, ht_psum, hb_done = sem("hid_psum"), sem("hpre_done"), sem("ht_psum"), sem("hb_done")
        g_done, hhi_done, hlo_done, res_psum, y_done = sem("g3_done"), sem("hhi3"), sem("hlo3"), sem("res_psum"), sem("y_done")
        yin_in = [sem(f"yin_in{i}") for i in range(NT)]
        ain_in = sem("ain_in")
        half_done, fin_done = sem("half_done"), sem("fin_done")
        stored = sem("stored")
        block = es.enter_context(nc.Block())

        @block.sync
        def _(sp):
            for t in range(EARLY, TILES):
                if t == EARLY + 2:
                    sp.dma_start(b2_bc[:], b2.partition_broadcast(P)).then_inc(small, 16)
                if t == NXB:
                    for parity in range(2):
                        sp.wait_ge(acc_out[parity], 16 * len(range(parity, NQ - QA, 2)))
                if NXB <= t < NXB + NT:
                    sp.dma_start(ain[:, t - NXB], acc_d[t - NXB]).then_inc(ain_in, 16)
                r = sp.value_load(row_tab[0:1, t:t + 1], min_val=0, max_val=FILL_ROW)
                if t >= NXB:
                    sp.wait_ge(y_out[t % NXB], 16 * (t // NXB))
                sp.dma_start(xg[:, t % NXB], xg_d[bass.ds(r, P), :]).then_inc(xg_in[t % NXB], 16)
            for i in range(NXB):
                sp.wait_ge(y_out[i], 16 * len(range(i, TILES, NXB)))
            for t in range(NT):
                sp.dma_start(results(t), y_d[:, t * P:(t + 1) * P, :].rearrange("k p d -> p k d")).then_inc(yin_in[t], 16)

        @block.gpsimd
        def _(pool):
            for t in range(TILES):
                pool.wait_ge(y_done, t + 1)
                pool.indirect_dma_start(y_d.rearrange("k n d -> (k n) d"),
                                        bass.IndirectOffsetOnAxis(ap=xg[:, t % NXB, D:D + 1].bitcast(U32), axis=0),
                                        y[:, t % NYB], None, bounds_check=2 * TOK - 1, oob_is_err=False).then_inc(y_out[t % NXB], 16)

        @block.scalar
        def _(act):
            for t in range(-2, TILES + 1):
                if t + 2 < TILES:
                    n = t + 2
                    act.wait_ge(xt_psum, n + 1)
                    if n >= NX:
                        act.wait_ge(hid_psum, n - NX + 1)
                    nc.scalar.activation(x_hi[:, n % NX], ps[:, n % 2, 0:D].rearrange("p (c n) -> p c n", c=C), ACT.Copy).then_inc(xhi_done, 1)
                if 0 <= t < TILES:
                    act.wait_ge(hid_psum, t + 1)
                    if t >= 2:
                        act.wait_ge(ht_psum, t - 1)
                    nc.scalar.activation(hpre[:, t % 2], ps[:, 2 + t % 2], ACT.Copy).then_inc(hpre_done, 1)
                if 1 <= t:
                    n = t - 1
                    act.wait_ge(hb_done, n + 1)
                    if n >= 2:
                        act.wait_ge(hlo_done, n - 1)
                    nc.scalar.activation(g[:, n % 2], hb[:, n % 2], ACT.Gelu).then_inc(g_done, 1)
                    if n >= 2:
                        act.wait_ge(res_psum, n - 1)
                    nc.scalar.activation(h_hi[:, n % 2], hb[:, n % 2], ACT.Gelu).then_inc(hhi_done, 1)
            nc.scalar.activation(ge[:, 0], gap[:], ACT.Exp).then_inc(exp2_done, 1)
            for t in range(NT):
                act.wait_ge(fin_done, t + 1)
                nc.scalar.dma_start(out[t], ain[:, t]).then_inc(stored, 16)
            act.wait_ge(stored, 16 * NT)

        @block.vector
        def _(dve):
            V = nc.vector
            dve.wait_ge(b1_in, 16)
            dve.wait_ge(tabs_ready, 2)
            expert = {}
            for t in range(-2, TILES + 2):
                if 1 <= t <= TILES:
                    n = t - 1
                    expert[n] = dve.value_load(exp_tab[0:1, n:n + 1], min_val=0, max_val=NE - 1)
                    dve.wait_ge(ht_psum, n + 1)
                    if n >= 2:
                        dve.wait_ge(hhi_done, n - 1)
                    V.tensor_tensor(out=hb[:, n % 2], in0=ps[:, 4 + n % 2].rearrange("p (c n) -> p c n", c=HC),
                                    in1=b1T[:, bass.ds(expert[n], 1), :].squeeze(1).unsqueeze(2).to_broadcast([P, HC, P]), op=ALU.add).then_inc(hb_done, 1)
                if t + 2 < TILES:
                    n = t + 2
                    dve.wait_ge(xhi_done, n + 1)
                    V.tensor_tensor(out=x_lo[:, n % NX], in0=ps[:, n % 2, 0:D].rearrange("p (c n) -> p c n", c=C),
                                    in1=x_hi[:, n % NX].bitcast(F32), op=ALU.subtract).then_inc(xlo_done, 1)
                if 2 <= t:
                    n = t - 2
                    dve.wait_ge(res_psum, n + 1)
                    if n == 0:
                        dve.wait_ge(small, 16)
                    if n >= NYB:
                        dve.wait_ge(y_out[(n - NYB) % NXB], 16 * ((n - NYB) // NXB + 1))
                    V.tensor_tensor(out=y[:, n % NYB], in0=ps[:, 6 + n % 2, 0:D], in1=b2_bc[:, bass.ds(expert[n], 1), :].squeeze(1),
                                    op=ALU.add).then_inc(y_done, 1)
                if 1 <= t <= TILES:
                    n = t - 1
                    dve.wait_ge(g_done, n + 1)
                    dve.wait_ge(hhi_done, n + 1)
                    V.tensor_tensor(out=h_lo[:, n % 2], in0=g[:, n % 2], in1=h_hi[:, n % 2].bitcast(F32), op=ALU.subtract).then_inc(hlo_done, 1)
            dve.wait_ge(exp2_done, 1)
            V.tensor_scalar(out=ge[:, 1], in0=ge[:, 0], scalar1=1.0, scalar2=None, op0=ALU.add).then_inc(weights, 1)
            dve.wait_ge(weights, 1)
            V.reciprocal(p12[:, 0], ge[:, 1]).then_inc(weights, 1)
            dve.wait_ge(weights, 2)
            V.tensor_tensor(out=p12[:, 1], in0=p12[:, 0], in1=ge[:, 0], op=ALU.mult).then_inc(weights, 1)
            dve.wait_ge(weights, 3)
            dve.wait_ge(ain_in, 16 * NT)
            for t in range(NT + 1):
                if t < NT:
                    dve.wait_ge(yin_in[t], 16)
                    V.scalar_tensor_tensor(out=ain[:, t], in0=results(t)[:, 0], scalar=p12[:, 0, t:t + 1], in1=ain[:, t],
                                           op0=ALU.mult, op1=ALU.add).then_inc(half_done, 1)
                if t >= 1:
                    n = t - 1
                    dve.wait_ge(half_done, n + 1)
                    V.scalar_tensor_tensor(out=ain[:, n], in0=results(n)[:, 1], scalar=p12[:, 1, n:n + 1], in1=ain[:, n],
                                           op0=ALU.mult, op1=ALU.add).then_inc(fin_done, 1)

        @block.tensor
        def _(pe):
            pe.wait_ge(tabs_ready, 2)

            def x_transpose(n):
                pe.wait_ge(xg_in[n % NXB], 16 * (n // NXB + 1))
                if n >= 2:
                    pe.wait_ge(xlo_done, n - 1)
                for c in range(C):
                    last = nc.tensor.transpose(ps[:, n % 2, c * P:(c + 1) * P], xg[:, n % NXB, c * P:(c + 1) * P], ident[:])
                last.then_inc(xt_psum, 1)

            x_transpose(0)
            x_transpose(1)
            for t in range(TILES + 2):
                if t + 2 < TILES:
                    x_transpose(t + 2)
                if t < TILES:
                    e = pe.value_load(exp_tab[0:1, t:t + 1], min_val=0, max_val=NE - 1)
                    pe.wait_ge(xlo_done, t + 1)
                    if t >= 2:
                        pe.wait_ge(hpre_done, t - 1)
                    k = 0
                    for c in range(C):
                        for a, b in ((x_hi, w_lo), (x_lo, w_hi), (x_hi, w_hi)):
                            last = nc.tensor.matmul(ps[:, 2 + t % 2], a[:, t % NX, c], b[:, bass.ds(e, 1), c * HF:(c + 1) * HF].squeeze(1),
                                                    start=(k == 0), stop=(k == 3 * C - 1))
                            k += 1
                    last.then_inc(hid_psum, 1)
                if 1 <= t <= TILES:
                    n = t - 1
                    pe.wait_ge(hpre_done, n + 1)
                    if n >= 2:
                        pe.wait_ge(hb_done, n - 1)
                    for c in range(HC):
                        last = nc.tensor.transpose(ps[:, 4 + n % 2, c * P:(c + 1) * P], hpre[:, n % 2, c:HF:HC], ident[:])
                    last.then_inc(ht_psum, 1)
                if 2 <= t:
                    n = t - 2
                    e = pe.value_load(exp_tab[0:1, n:n + 1], min_val=0, max_val=NE - 1)
                    pe.wait_ge(hlo_done, n + 1)
                    if n >= 2:
                        pe.wait_ge(y_done, n - 1)
                    k = 0
                    for c in range(HC):
                        for a, b in ((h_hi, w_lo), (h_lo, w_hi), (h_hi, w_hi)):
                            last = nc.tensor.matmul(ps[:, 6 + n % 2, 0:D], a[:, n % 2, c],
                                                    b[:, bass.ds(e, 1), C * HF + c * D:C * HF + (c + 1) * D].squeeze(1),
                                                    start=(k == 0), stop=(k == 3 * HC - 1))
                            k += 1
                    last.then_inc(res_psum, 1)


def build(nc, a, out):
    x1_d = nc.dram_tensor("x1_d", [NT, P, D], F32, kind="Internal").ap()
    xt_d = nc.dram_tensor("xt_d", [P, C, TOK], F32, kind="Internal").ap()
    xg_d = nc.dram_tensor("xg_d", [XG_ROWS, ROW], F32, kind="Internal").ap()
    acc_d = nc.dram_tensor("acc_d", [NT, P, D], F32, kind="Internal").ap()
    y_d = nc.dram_tensor("y_d", [2, TOK, D], F32, kind="Internal").ap()
    with ExitStack() as es:
        def sb(name, shape, dt=F32):
            return es.enter_context(nc.sbuf_tensor(name, shape, dt))

        ident = sb("ident", [P, P])
        b1T = sb("b1T", [P, NE, HC])
        gap = sb("gap", [P, NT])
        counts = sb("counts", [P, NE])
        row_tab = sb("row_tab", [1, TILES], I32)
        exp_tab = sb("exp_tab", [1, TILES], I32)
        counts_ready = es.enter_context(nc.semaphore("counts_ready"))
        tabs_ready = es.enter_context(nc.semaphore("tabs_ready"))
        b1_in = es.enter_context(nc.semaphore("routed_b1_in"))
        xg_in = [es.enter_context(nc.semaphore(f"xg_in{i}")) for i in range(NXB)]
        acc_out = [es.enter_context(nc.semaphore(f"acc_out{i}")) for i in range(2)]
        stage = sb("stage", [P, max(RAW * PIECE, NXB * ROW)])
        xg = stage[:, 0:NXB * ROW].rearrange("p (b n) -> p b n", b=NXB)
        X, F = "L0_xattn_", "L0_ffn_"
        with ExitStack() as es_shared:
            shared = SharedExperts(nc, es_shared, stage, (a[F + "w1"], a[F + "w2"], a[F + "sw1"], a[F + "sb1"], a[F + "sw2"]))
            attention(nc, (a["x"], a["ctx_1024"], a[X + "Wv"], a[X + "Wk"], a[X + "Wq"], a[X + "Wo"], a[X + "bo"],
                           a[F + "router_w"], a[F + "router_b"], a[F + "sb2"]), (ident, gap, counts, counts_ready), (x1_d, xt_d, xg_d, acc_d), shared)
            w_hi = sb("w_hi", [P, NE, WPE], F32R)
            w_lo = sb("w_lo", [P, NE, WPE], F32R)
            shared_experts(nc, a[F + "b1"], (b1T, b1_in, xg, xg_in, acc_out, w_hi, w_lo, counts, row_tab, exp_tab, tabs_ready), (x1_d, xt_d, xg_d, acc_d), shared)
        routed_experts(nc, a[F + "b2"], (ident, b1T, b1_in, xg, xg_in, acc_out, w_hi, w_lo, gap, row_tab, exp_tab, tabs_ready), (xg_d, acc_d, y_d),
                       out.rearrange("b (t p) d -> (b t) p d", p=P))


INS = ["x", "ctx_1024", "L0_xattn_Wv", "L0_xattn_Wk", "L0_xattn_Wq", "L0_xattn_Wo", "L0_xattn_bo", "L0_ffn_router_w",
       "L0_ffn_router_b", "L0_ffn_w1", "L0_ffn_b1", "L0_ffn_w2", "L0_ffn_b2", "L0_ffn_sw1", "L0_ffn_sb1", "L0_ffn_sw2", "L0_ffn_sb2"]


def kernel(**inputs):
    import concourse.bacc as bacc
    from concourse.bass_utils import run_bass_kernel_spmd

    nc = bacc.Bacc("TRN2", target_bir_lowering=False, num_devices=1)
    arrays, aps = {}, {}
    for name in INS:
        a = np.ascontiguousarray(inputs[name])
        arrays[f"in_{name}"] = a
        aps[name] = nc.dram_tensor(f"in_{name}", a.shape, mybir.dt.from_np(a.dtype), kind="ExternalInput").ap()
    out = nc.dram_tensor("out", (B, S, D), F32, kind="ExternalOutput").ap()
    build(nc, aps, out)
    r = run_bass_kernel_spmd(nc, [arrays], core_ids=[0])
    return r.results[0]["out"]
```
